# Optimizing a Trainium2 kernel written in Bass

```python
import numpy as np
import jax
import jax.numpy as jnp

def _softmax(x, axis=-1):
    return jax.nn.softmax(x, axis=axis)

def _gelu(x):
    return jax.nn.gelu(x, approximate=True)

def _silu(x):
    return jax.nn.silu(x)

def _sigmoid(x):
    return jax.nn.sigmoid(x)

def _layernorm(x, axis=-1, eps=1e-05):
    m = jnp.mean(x, axis=axis, keepdims=True)
    v = jnp.var(x, axis=axis, keepdims=True)
    return (x - m) / jnp.sqrt(v + eps)

def _scatter_add(tgt, idx, src, axis=0):
    return tgt.at[idx].add(src)

def _segment_sum(src, seg, n):
    return jax.ops.segment_sum(src, seg, n)
kernel_name = 'mk_macaron_d1_jaxref_r8_863183'

def setup_inputs(seed: int=0):
    np.random.seed(seed)
    _w = jnp.asarray

    def _L0_attn_setup():
        import jax, jax.numpy as jnp
        import numpy as np
        D_MODEL = 256
        D_STATE = 128
        D_CONV = 4
        EXPAND = 2
        HEADDIM = 64
        NGROUPS = 1
        CHUNK = 32
        D_INNER = EXPAND * D_MODEL
        NHEADS = D_INNER // HEADDIM
        CONV_DIM = D_INNER + 2 * NGROUPS * D_STATE
        D_IN_PROJ = 2 * D_INNER + 2 * NGROUPS * D_STATE + NHEADS
        EPS = 1e-05

        def _segsum(x):
            T = x.shape[-1]
            cs = jnp.cumsum(x, axis=-1)
            seg = cs[..., :, None] - cs[..., None, :]
            mask = jnp.tril(jnp.ones((T, T), dtype=bool))
            return jnp.where(mask, seg, -jnp.inf)

        def _causal_conv1d_silu(x, w, b):
            K = w.shape[-1]
            Lx = x.shape[-1]
            xp = jnp.pad(x, ((0, 0), (0, 0), (K - 1, 0)))
            y = b[None, :, None]
            for k in range(K):
                y = y + w[None, :, k:k + 1] * xp[:, :, k:k + Lx]
            return jax.nn.silu(y)

        def _mamba2_forward(u, in_proj_kernel, conv1d_weight, conv1d_bias, dt_bias, A_log, D, norm_weight, out_proj_kernel):
            B_, L, _ = u.shape
            zxbcdt = u @ in_proj_kernel
            z = zxbcdt[..., :D_INNER]
            xBC = zxbcdt[..., D_INNER:D_INNER + CONV_DIM]
            dt = zxbcdt[..., D_INNER + CONV_DIM:]
            xBC = _causal_conv1d_silu(jnp.transpose(xBC, (0, 2, 1)), conv1d_weight, conv1d_bias)
            xBC = jnp.transpose(xBC, (0, 2, 1))
            x = xBC[..., :D_INNER].reshape(B_, L, NHEADS, HEADDIM)
            Bm = xBC[..., D_INNER:D_INNER + NGROUPS * D_STATE].reshape(B_, L, NGROUPS, D_STATE)
            Cm = xBC[..., D_INNER + NGROUPS * D_STATE:].reshape(B_, L, NGROUPS, D_STATE)
            dt = jax.nn.softplus(dt + dt_bias)
            A = -jnp.exp(A_log)
            nc = L // CHUNK
            r = NHEADS // NGROUPS
            xc = x.reshape(B_, nc, CHUNK, NGROUPS, r, HEADDIM)
            dtc = dt.reshape(B_, nc, CHUNK, NGROUPS, r)
            Bc = Bm.reshape(B_, nc, CHUNK, NGROUPS, D_STATE)
            Cc = Cm.reshape(B_, nc, CHUNK, NGROUPS, D_STATE)
            xdt = xc * dtc[..., None]
            dA = dtc * A.reshape(NGROUPS, r)
            dA = jnp.transpose(dA, (0, 3, 4, 1, 2))
            A_cs = jnp.cumsum(dA, axis=-1)
            Lmat = jnp.exp(_segsum(dA))
            Y_diag = jnp.einsum('bclgn,bcsgn,bgrcls,bcsgrp->bclgrp', Cc, Bc, Lmat, xdt)
            decay_states = jnp.exp(A_cs[..., -1:] - A_cs)
            states = jnp.einsum('bcsgn,bgrcs,bcsgrp->bcgrpn', Bc, decay_states, xdt)
            chunk_decay = jnp.exp(A_cs[..., -1])
            states_t = jnp.moveaxis(states, 1, 0)
            decay_t = jnp.moveaxis(chunk_decay, -1, 0)

            def step(S, inp):
                d, st = inp
                S_new = S * d[..., None, None] + st
                return (S_new, S)
            S0 = jnp.zeros(states_t.shape[1:], states_t.dtype)
            _, prev_states = jax.lax.scan(step, S0, (decay_t, states_t))
            prev_states = jnp.moveaxis(prev_states, 0, 1)
            state_decay = jnp.exp(A_cs)
            Y_off = jnp.einsum('bclgn,bcgrpn,bgrcl->bclgrp', Cc, prev_states, state_decay)
            Y = (Y_diag + Y_off).reshape(B_, nc, CHUNK, NHEADS, HEADDIM)
            Y = Y + x.reshape(B_, nc, CHUNK, NHEADS, HEADDIM) * D[:, None]
            y = Y.reshape(B_, L, D_INNER)
            y = y * jax.nn.silu(z)
            y = y * jax.lax.rsqrt(jnp.mean(y * y, axis=-1, keepdims=True) + EPS) * norm_weight
            return y @ out_proj_kernel
        key = jax.random.key(seed)
        ks = jax.random.split(key, 8)
        B, L = (2, 512)
        u = jax.random.normal(ks[0], (B, L, D_MODEL), jnp.float32)
        in_proj_kernel = jax.random.normal(ks[1], (D_MODEL, D_IN_PROJ), jnp.float32) * (1.0 / np.sqrt(D_MODEL))
        conv1d_weight = jax.random.normal(ks[2], (CONV_DIM, D_CONV), jnp.float32) * (1.0 / np.sqrt(D_CONV))
        conv1d_bias = jnp.zeros((CONV_DIM,), jnp.float32)
        uu = jax.random.uniform(ks[3], (NHEADS,), jnp.float32)
        dt = jnp.exp(uu * (np.log(0.1) - np.log(0.001)) + np.log(0.001))
        dt = jnp.maximum(dt, 0.0001)
        dt_bias = dt + jnp.log(-jnp.expm1(-dt))
        A_log = jnp.log(jax.random.uniform(ks[4], (NHEADS,), jnp.float32, minval=1.0, maxval=16.0))
        D = jnp.ones((NHEADS,), jnp.float32)
        norm_weight = jnp.ones((D_INNER,), jnp.float32)
        out_proj_kernel = jax.random.normal(ks[5], (D_INNER, D_MODEL), jnp.float32) * (1.0 / np.sqrt(D_INNER))
        return {'u': u, 'in_proj_kernel': in_proj_kernel, 'conv1d_weight': conv1d_weight, 'conv1d_bias': conv1d_bias, 'dt_bias': dt_bias, 'A_log': A_log, 'D': D, 'norm_weight': norm_weight, 'out_proj_kernel': out_proj_kernel}
    _L0_attn_in = _L0_attn_setup()

    def _L0_ffn_setup():
        import jax, jax.numpy as jnp
        import numpy as np
        EPS = 1e-06
        K_STEPS = 4
        USE_GATING = True

        def layer_norm(x, gamma, beta):
            mu = jnp.mean(x, axis=-1, keepdims=True)
            var = jnp.mean(jnp.square(x - mu), axis=-1, keepdims=True)
            return (x - mu) * jax.lax.rsqrt(var + EPS) * gamma + beta
        key = jax.random.key(seed)
        B, L, D, H = (4, 512, 256, 1024)
        ks = jax.random.split(key, 16)
        s = 0.02
        return {'x': jax.random.normal(ks[0], (B, L, D), dtype=jnp.float32), 'in_gamma': jnp.ones((D,), jnp.float32), 'in_beta': jnp.zeros((D,), jnp.float32), 'agg_w': jax.random.normal(ks[1], (D, D), jnp.float32) * s, 'agg_b': jnp.zeros((D,), jnp.float32), 'pn_gamma': jnp.ones((D,), jnp.float32), 'pn_beta': jnp.zeros((D,), jnp.float32), 'd1_w': jax.random.normal(ks[2], (D, H), jnp.float32) * s, 'd1_b': jnp.zeros((H,), jnp.float32), 'd2_w': jax.random.normal(ks[3], (H, D), jnp.float32) * s, 'd2_b': jnp.zeros((D,), jnp.float32), 'bc_w': jax.random.normal(ks[4], (D, D), jnp.float32) * s, 'bc_b': jnp.zeros((D,), jnp.float32), 'gate_w': jax.random.normal(ks[5], (D, D), jnp.float32) * s, 'gate_b': jnp.zeros((D,), jnp.float32), 'out_gamma': jnp.ones((D,), jnp.float32), 'out_beta': jnp.zeros((D,), jnp.float32)}
    _L0_ffn_in = _L0_ffn_setup()
    _d = {'L0_attn_u': _L0_attn_in['u'], 'L0_attn_in_proj_kernel': _L0_attn_in['in_proj_kernel'], 'L0_attn_conv1d_weight': _L0_attn_in['conv1d_weight'], 'L0_attn_conv1d_bias': _L0_attn_in['conv1d_bias'], 'L0_attn_dt_bias': _L0_attn_in['dt_bias'], 'L0_attn_A_log': _L0_attn_in['A_log'], 'L0_attn_D': _L0_attn_in['D'], 'L0_attn_norm_weight': _L0_attn_in['norm_weight'], 'L0_attn_out_proj_kernel': _L0_attn_in['out_proj_kernel'], 'L0_ffn_in_gamma': _L0_ffn_in['in_gamma'], 'L0_ffn_in_beta': _L0_ffn_in['in_beta'], 'L0_ffn_agg_w': _L0_ffn_in['agg_w'], 'L0_ffn_agg_b': _L0_ffn_in['agg_b'], 'L0_ffn_pn_gamma': _L0_ffn_in['pn_gamma'], 'L0_ffn_pn_beta': _L0_ffn_in['pn_beta'], 'L0_ffn_d1_w': _L0_ffn_in['d1_w'], 'L0_ffn_d1_b': _L0_ffn_in['d1_b'], 'L0_ffn_d2_w': _L0_ffn_in['d2_w'], 'L0_ffn_d2_b': _L0_ffn_in['d2_b'], 'L0_ffn_bc_w': _L0_ffn_in['bc_w'], 'L0_ffn_bc_b': _L0_ffn_in['bc_b'], 'L0_ffn_gate_w': _L0_ffn_in['gate_w'], 'L0_ffn_gate_b': _L0_ffn_in['gate_b'], 'L0_ffn_out_gamma': _L0_ffn_in['out_gamma'], 'L0_ffn_out_beta': _L0_ffn_in['out_beta']}
    _x0 = _d['L0_attn_u']
    _d['L0_attn_u'] = jax.random.normal(jax.random.fold_in(jax.random.key(seed), 1), (2, 512, 256), dtype=_x0.dtype)
    del _x0
    return _d

def reference(L0_attn_u, L0_attn_in_proj_kernel, L0_attn_conv1d_weight, L0_attn_conv1d_bias, L0_attn_dt_bias, L0_attn_A_log, L0_attn_D, L0_attn_norm_weight, L0_attn_out_proj_kernel, L0_ffn_in_gamma, L0_ffn_in_beta, L0_ffn_agg_w, L0_ffn_agg_b, L0_ffn_pn_gamma, L0_ffn_pn_beta, L0_ffn_d1_w, L0_ffn_d1_b, L0_ffn_d2_w, L0_ffn_d2_b, L0_ffn_bc_w, L0_ffn_bc_b, L0_ffn_gate_w, L0_ffn_gate_b, L0_ffn_out_gamma, L0_ffn_out_beta):

    def _L0_attn_ref(u, in_proj_kernel, conv1d_weight, conv1d_bias, dt_bias, A_log, D, norm_weight, out_proj_kernel):
        import jax, jax.numpy as jnp
        import numpy as np
        D_MODEL = 256
        D_STATE = 128
        D_CONV = 4
        EXPAND = 2
        HEADDIM = 64
        NGROUPS = 1
        CHUNK = 32
        D_INNER = EXPAND * D_MODEL
        NHEADS = D_INNER // HEADDIM
        CONV_DIM = D_INNER + 2 * NGROUPS * D_STATE
        D_IN_PROJ = 2 * D_INNER + 2 * NGROUPS * D_STATE + NHEADS
        EPS = 1e-05

        def _segsum(x):
            T = x.shape[-1]
            cs = jnp.cumsum(x, axis=-1)
            seg = cs[..., :, None] - cs[..., None, :]
            mask = jnp.tril(jnp.ones((T, T), dtype=bool))
            return jnp.where(mask, seg, -jnp.inf)

        def _causal_conv1d_silu(x, w, b):
            K = w.shape[-1]
            Lx = x.shape[-1]
            xp = jnp.pad(x, ((0, 0), (0, 0), (K - 1, 0)))
            y = b[None, :, None]
            for k in range(K):
                y = y + w[None, :, k:k + 1] * xp[:, :, k:k + Lx]
            return jax.nn.silu(y)

        def _mamba2_forward(u, in_proj_kernel, conv1d_weight, conv1d_bias, dt_bias, A_log, D, norm_weight, out_proj_kernel):
            B_, L, _ = u.shape
            zxbcdt = u @ in_proj_kernel
            z = zxbcdt[..., :D_INNER]
            xBC = zxbcdt[..., D_INNER:D_INNER + CONV_DIM]
            dt = zxbcdt[..., D_INNER + CONV_DIM:]
            xBC = _causal_conv1d_silu(jnp.transpose(xBC, (0, 2, 1)), conv1d_weight, conv1d_bias)
            xBC = jnp.transpose(xBC, (0, 2, 1))
            x = xBC[..., :D_INNER].reshape(B_, L, NHEADS, HEADDIM)
            Bm = xBC[..., D_INNER:D_INNER + NGROUPS * D_STATE].reshape(B_, L, NGROUPS, D_STATE)
            Cm = xBC[..., D_INNER + NGROUPS * D_STATE:].reshape(B_, L, NGROUPS, D_STATE)
            dt = jax.nn.softplus(dt + dt_bias)
            A = -jnp.exp(A_log)
            nc = L // CHUNK
            r = NHEADS // NGROUPS
            xc = x.reshape(B_, nc, CHUNK, NGROUPS, r, HEADDIM)
            dtc = dt.reshape(B_, nc, CHUNK, NGROUPS, r)
            Bc = Bm.reshape(B_, nc, CHUNK, NGROUPS, D_STATE)
            Cc = Cm.reshape(B_, nc, CHUNK, NGROUPS, D_STATE)
            xdt = xc * dtc[..., None]
            dA = dtc * A.reshape(NGROUPS, r)
            dA = jnp.transpose(dA, (0, 3, 4, 1, 2))
            A_cs = jnp.cumsum(dA, axis=-1)
            Lmat = jnp.exp(_segsum(dA))
            Y_diag = jnp.einsum('bclgn,bcsgn,bgrcls,bcsgrp->bclgrp', Cc, Bc, Lmat, xdt)
            decay_states = jnp.exp(A_cs[..., -1:] - A_cs)
            states = jnp.einsum('bcsgn,bgrcs,bcsgrp->bcgrpn', Bc, decay_states, xdt)
            chunk_decay = jnp.exp(A_cs[..., -1])
            states_t = jnp.moveaxis(states, 1, 0)
            decay_t = jnp.moveaxis(chunk_decay, -1, 0)

            def step(S, inp):
                d, st = inp
                S_new = S * d[..., None, None] + st
                return (S_new, S)
            S0 = jnp.zeros(states_t.shape[1:], states_t.dtype)
            _, prev_states = jax.lax.scan(step, S0, (decay_t, states_t))
            prev_states = jnp.moveaxis(prev_states, 0, 1)
            state_decay = jnp.exp(A_cs)
            Y_off = jnp.einsum('bclgn,bcgrpn,bgrcl->bclgrp', Cc, prev_states, state_decay)
            Y = (Y_diag + Y_off).reshape(B_, nc, CHUNK, NHEADS, HEADDIM)
            Y = Y + x.reshape(B_, nc, CHUNK, NHEADS, HEADDIM) * D[:, None]
            y = Y.reshape(B_, L, D_INNER)
            y = y * jax.nn.silu(z)
            y = y * jax.lax.rsqrt(jnp.mean(y * y, axis=-1, keepdims=True) + EPS) * norm_weight
            return y @ out_proj_kernel
        return _mamba2_forward(u, in_proj_kernel, conv1d_weight, conv1d_bias, dt_bias, A_log, D, norm_weight, out_proj_kernel)

    def _L0_ffn_ref(x, in_gamma, in_beta, agg_w, agg_b, pn_gamma, pn_beta, d1_w, d1_b, d2_w, d2_b, bc_w, bc_b, gate_w, gate_b, out_gamma, out_beta):
        import jax, jax.numpy as jnp
        import numpy as np
        EPS = 1e-06
        K_STEPS = 4
        USE_GATING = True

        def layer_norm(x, gamma, beta):
            mu = jnp.mean(x, axis=-1, keepdims=True)
            var = jnp.mean(jnp.square(x - mu), axis=-1, keepdims=True)
            return (x - mu) * jax.lax.rsqrt(var + EPS) * gamma + beta
        x_norm = layer_norm(x, in_gamma, in_beta)
        thought = x_norm[:, -1, :] @ agg_w + agg_b
        for _ in range(K_STEPS):
            t = layer_norm(thought, pn_gamma, pn_beta)
            t = jax.nn.gelu(t @ d1_w + d1_b, approximate=False)
            thought = thought + (t @ d2_w + d2_b)
        broadcast = (thought @ bc_w + bc_b)[:, None, :]
        if USE_GATING:
            gate = jax.nn.sigmoid(x @ gate_w + gate_b)
            out = x + gate * broadcast
        else:
            out = x + broadcast
        return layer_norm(out, out_gamma, out_beta)
    x = L0_attn_u
    x = x + 0.5 * _L0_ffn_ref(_layernorm(x, axis=-1), L0_ffn_in_gamma, L0_ffn_in_beta, L0_ffn_agg_w, L0_ffn_agg_b, L0_ffn_pn_gamma, L0_ffn_pn_beta, L0_ffn_d1_w, L0_ffn_d1_b, L0_ffn_d2_w, L0_ffn_d2_b, L0_ffn_bc_w, L0_ffn_bc_b, L0_ffn_gate_w, L0_ffn_gate_b, L0_ffn_out_gamma, L0_ffn_out_beta)
    x = x + _L0_attn_ref(_layernorm(x, axis=-1), L0_attn_in_proj_kernel, L0_attn_conv1d_weight, L0_attn_conv1d_bias, L0_attn_dt_bias, L0_attn_A_log, L0_attn_D, L0_attn_norm_weight, L0_attn_out_proj_kernel)
    x = x + 0.5 * _L0_ffn_ref(_layernorm(x, axis=-1), L0_ffn_in_gamma, L0_ffn_in_beta, L0_ffn_agg_w, L0_ffn_agg_b, L0_ffn_pn_gamma, L0_ffn_pn_beta, L0_ffn_d1_w, L0_ffn_d1_b, L0_ffn_d2_w, L0_ffn_d2_b, L0_ffn_bc_w, L0_ffn_bc_b, L0_ffn_gate_w, L0_ffn_gate_b, L0_ffn_out_gamma, L0_ffn_out_beta)
    return x

_drawn_inputs = setup_inputs


def setup_inputs(seed=0):
    import zlib

    import numpy as np

    out = dict(_drawn_inputs(seed))
    spreads = {'L0_attn_conv1d_bias': (0.0, 0.1),
     'L0_attn_D': (1.0, 0.2),
     'L0_attn_norm_weight': (1.0, 0.2),
     'L0_ffn_in_gamma': (1.0, 0.6),
     'L0_ffn_in_beta': (0.0, 0.8),
     'L0_ffn_agg_b': (0.0, 0.52),
     'L0_ffn_pn_gamma': (1.0, 0.6),
     'L0_ffn_pn_beta': (0.0, 0.8),
     'L0_ffn_d1_b': (0.0, 0.613),
     'L0_ffn_d2_b': (0.0, 0.1),
     'L0_ffn_bc_b': (0.0, 0.28),
     'L0_ffn_gate_b': (0.0, 0.8),
     'L0_ffn_out_gamma': (1.0, 0.2),
     'L0_ffn_out_beta': (0.0, 0.1)}
    factors = {'L0_ffn_gate_w': 5.541}
    for name, (base, spread) in spreads.items():
        noise = np.random.default_rng([zlib.crc32(name.encode()), seed]).standard_normal(out[name].shape)
        drawn = base * np.exp(spread * noise) if base else spread * noise
        out[name] = jnp.asarray(drawn.astype(out[name].dtype))
    for name, factor in factors.items():
        out[name] = (out[name] * factor).astype(out[name].dtype)
    return out
```

```python
from contextlib import ExitStack

import concourse.bass as bass
from concourse import mybir

F32 = mybir.dt.float32
ALU = mybir.AluOpType
ACT = mybir.ActivationFunctionType

P = 128


def macaron_program(nc: bass.Bass, a, out):
    NB, L, D = a["u"].shape
    KT = D // P
    NT = NB * L // P
    NC = L // P
    DI, CW = a["out_proj"].shape[0], a["conv_w"].shape[1]
    NH = a["D"].shape[0]
    HD = DI // NH
    CD = a["conv_w"].shape[0]
    CT = CD // P
    XT = DI // P
    H = a["d1_w"].shape[1]
    HT = H // P
    STEPS = 4
    PAIRS = NT // 2
    LAST = [NC * (b + 1) - 1 for b in range(NB)]
    EPS_LN, EPS_FFN = 1e-5, 1e-6

    with ExitStack() as ctx:
        def sb(name, shape, dt=F32):
            return ctx.enter_context(nc.sbuf_tensor(name, shape, dt))

        def sem(name):
            return ctx.enter_context(nc.semaphore(name))

        banks = [ctx.enter_context(nc.psum_tensor(f"bank{i}", [P, 512], F32)) for i in (0, 1)]
        seg_ps = ctx.enter_context(nc.psum_tensor("seg_ps", [P, 1024], F32))
        banks += [seg_ps[:, 0:512], seg_ps[:, 512:1024]]
        banks += [ctx.enter_context(nc.psum_tensor(f"bank{i}", [P, 512], F32)) for i in (4, 5, 6, 7)]
        bank = [x[:, :] for x in banks]

        x_sb = [sb(f"x{n}", [P, NT, D]) for n in range(3)]
        x_sb.append(x_sb[0])
        xn = sb("xn", [P, NT, D])
        xnT = sb("xnT", [P, KT, NT * P])
        ident = sb("ident", [P, P])
        ones = sb("ones", [P, P])
        avg = sb("avg", [P, P])
        tri = sb("tri", [P, P])
        after = sb("after", [P, P])
        mhalf = sb("mhalf", [P, 1])
        zero = sb("zero", [P, 1])

        w_in = sb("w_in", [P, KT, a["in_proj"].shape[1]])
        w_out = sb("w_out", [P, XT, D])
        w_gate = sb("w_gate", [P, KT, D])
        w_agg = sb("w_agg", [P, KT, D])
        w_bc = sb("w_bc", [P, KT, D])
        w_d1 = sb("w_d1", [P, KT, H])
        w_d2 = sb("w_d2", [P, HT, D])
        conv_w = sb("conv_w", [P, CT, CW])
        row_gate_b = sb("row_gate_b", [1, D])
        row_bc_b = sb("row_bc_b", [1, D])
        gam = sb("gam", [P, D])
        bet = sb("bet", [P, D])
        head_par = sb("head_par", [P, 3, NH])
        ROWS = [("in_gamma", KT), ("in_beta", KT), ("agg_b", KT), ("pn_gamma", KT), ("pn_beta", KT),
                ("d2_b", KT), ("d1_b", HT), ("norm_w", XT), ("conv_b", CT)]
        row_at, n_rows = {}, 0
        for name, n in ROWS:
            row_at[name] = (n_rows, n)
            n_rows += n
        rows = sb("rows", [n_rows, P])
        cols = sb("cols", [P, n_rows])

        def col(name):
            at, n = row_at[name]
            return cols[:, at:at + n]

        LN_TILES = [list(range(NT)), LAST, list(range(NT)), list(range(NT)),
                    list(range(NT)), LAST, list(range(NT))]
        LN_EPS = [EPS_LN, EPS_FFN, EPS_FFN, EPS_LN, EPS_LN, EPS_FFN, EPS_FFN]
        bn_before = [sum(len(t) for t in LN_TILES[:k]) for k in range(len(LN_TILES) + 1)]
        bn = sb("bn", [P, len(LN_TILES), NT, 6])
        mv = sb("mv", [P, len(LN_TILES), NT, 2])
        ve = sb("ve", [P, len(LN_TILES), NT])
        rstd = sb("rstd", [P, len(LN_TILES), NT])

        xnn = sb("xnn", [P, NB, D])
        sz = sb("sz", [P, NT, DI])
        sg, o = sz[:, :, 0:D], sz[:, :, D:2 * D]
        lastT = sb("lastT", [P, KT, NB])
        lastg = sb("lastg", [P, KT, NB])
        th = sb("th", [P, 2 * (STEPS + 1), KT, NB])
        thb = sb("thb", [P, 2 * STEPS, KT, NB])
        dc = sb("dc", [P, KT, NB])
        sq = sb("sq", [P, KT, NB])
        vs = sb("vs", [P, NB])
        rs = sb("rs", [P, NB])
        hr = sb("hr", [P, HT, NB])
        hb = sb("hb", [P, HT, NB])
        hg = sb("hg", [P, HT, NB])
        c1 = sb("c1", [P, HT])
        thr = sb("thr", [P, NB, KT, P])

        cv = sb("cv", [P, 3, L])
        xc = sb("xc", [P, CT, NB * L])
        N64 = NT * NH
        dtv = sb("dtv", [P, NT, NH])
        dtn = sb("dtn", [P, NT, NH])
        dte = sb("dte", [P, NT, NH])
        dtl = sb("dtl", [P, NT, NH])
        dt = sb("dt", [P, NT, NH])
        ea = sb("ea", [P, NH])
        dA = sb("dA", [P, NT, NH])
        cs = sb("cs", [P, NT, NH])
        ecs = sb("ecs", [P, NT, NH])
        dec = sb("dec", [P, NT, NH])
        rest = sb("rest", [P, NT, NH])
        erest = sb("erest", [P, NT, NH])
        wd = sb("wd", [P, NT, NH])
        R = sb("R", [P, 2, NH, P])
        E = sb("E", [P, 2, NH, P])
        M = sb("M", [P, 2, NH, P])
        GT = sb("GT", [P, 2, P])
        Bt = sb("Bt", [P, 2, P])
        xt = sb("xt", [P, 2, DI])
        xdt = sb("xdt", [P, 2, DI])
        xw = sb("xw", [P, 2, DI])
        xD = sb("xD", [P, 2, DI])
        S = sb("S", [P, 2, DI])
        Sd = sb("Sd", [P, 2, DI])
        yo = sb("yo", [P, 2, DI])
        yd = sb("yd", [P, 2, DI])
        u = sb("u", [P, 2, DI])
        usq = sb("usq", [P, DI])
        ss = sb("ss", [P, NT])
        se = sb("se", [P, NT])
        sr = sb("sr", [P, NT])
        uT = sb("uT", [P, 2, XT, P])

        ld_x, ld_rows, ld_chain, ld_d1, ld_d2, ld_gate, ld_bc, ld_aff, ld_head, ld_in, ld_conv, ld_out = map(
            sem, "ld_x ld_rows ld_chain ld_d1 ld_d2 ld_gate ld_bc ld_aff ld_head ld_in ld_conv ld_out".split())
        consts_zeroed, consts_done, rows_T, cols_ready, d1_scaled, gamma_ready, beta_ready, out_scaled = map(
            sem, "consts_zeroed consts_done rows_T cols_ready d1_scaled gamma_ready beta_ready out_scaled".split())
        bn_done, ag_done, ve_done, rstd_done, xn_done, xnn_done = map(
            sem, "bn_done ag_done ve_done rstd_done xn_done xnn_done".split())
        xnT_ps, xnT_done, gate_ps, sg_done = map(sem, "xnT_ps xnT_done gate_ps sg_done".split())
        last_ps, last_mid, last_done, c1_ps, c1_done, agg_ps, th_done = map(
            sem, "last_ps last_mid last_done c1_ps c1_done agg_ps th_done".split())
        mean_ps, dc_done, sq_done, var_ps, vs_done, rs_done, h_ps, hr_done, hb_done, gelu_done, d2_ps, thb_done = map(
            sem, "mean_ps dc_done sq_done var_ps vs_done rs_done h_ps hr_done hb_done gelu_done d2_ps thb_done".split())
        thr_done, bc_ps, ob_done, o_done, og_done, xb_done, x_done = map(
            sem, "thr_done bc_ps ob_done o_done og_done xb_done x_done".split())
        dt_ps, dt_v, dt_n, dt_e, dt_l, dt_done, ea_done, dA_done, cs_ps, cs_done, rest_done, exps_done, wd_done = map(
            sem, "dt_ps dt_v dt_n dt_e dt_l dt_done ea_done dA_done cs_ps cs_done rest_done exps_done wd_done".split())
        proj_ps, tap0_done, conv_done, xc_done, z_ps, sz_done = map(
            sem, "proj_ps tap0_done conv_done xc_done z_ps sz_done".split())
        R_done, seg_ready, E_done, M_done, G_ps, GB_done = map(
            sem, "R_done seg_ready E_done M_done G_ps GB_done".split())
        xt_ps, xt_done, xdt_done, xw_done, xD_done, st_ps, Sd_done, S_done = map(
            sem, "xt_ps xt_done xdt_done xw_done xD_done st_ps Sd_done S_done".split())
        y_ps, yoff_ps, yo_done, yd_done, yy_done, u_done, ss_done, se_done, sr_done = map(
            sem, "y_ps yoff_ps yo_done yd_done yy_done u_done ss_done se_done sr_done".split())
        uT_ps, uT_done, out_ps, x2_done, stored = map(
            sem, "uT_ps uT_done out_ps x2_done stored".split())

        block = ctx.enter_context(nc.Block())
        x_tiles = a["u"].rearrange("b (c p) d -> p (b c) d", p=P)
        out_tiles = out.rearrange("b (c p) d -> p (b c) d", p=P)

        def as_row(v):
            return v.rearrange("(o n) -> o n", o=1)

        def every_partition(v):
            return as_row(v).to_broadcast([P, v.shape[0]])

        def all_of(n):
            return 16 * n

        XN_OF = {0: 0, 3: 1, 4: 2}
        SSD_STATES = [i for i in range(NT) if i % NC < NC - 1]
        n_states = {i: sum(j <= i for j in SSD_STATES) for i in range(NT)}
        SSD_OFF = [i for i in range(NT) if i % NC > 0]
        n_off = {i: sum(j <= i for j in SSD_OFF) for i in range(NT)}

        @block.sync
        def _(sp):
            sp.dma_start(x_sb[0][:, 0:NT // 2, :], x_tiles[:, 0:NT // 2, :]).then_inc(ld_x, 16)
            sp.dma_start(x_sb[0][:, NT // 2:NT, :], x_tiles[:, NT // 2:NT, :]).then_inc(ld_x, 16)
            sp.dma_start(w_agg[:, :, :], a["agg_w"].rearrange("(t p) n -> p t n", p=P)).then_inc(ld_chain, 16)
            sp.dma_start(w_d1[:, :, :], a["d1_w"].rearrange("(t p) n -> p t n", p=P)).then_inc(ld_d1, 16)
            sp.dma_start(w_d2[:, :, :], a["d2_w"].rearrange("(t p) n -> p t n", p=P)).then_inc(ld_d2, 16)
            sp.dma_start(w_bc[:, :, :], a["bc_w"].rearrange("(t p) n -> p t n", p=P)).then_inc(ld_bc, 16)
            sp.dma_start(w_in[:, :, :], a["in_proj"].rearrange("(t p) n -> p t n", p=P)).then_inc(ld_in, 16)
            sp.dma_start(w_out[:, :, :], a["out_proj"].rearrange("(t p) n -> p t n", p=P)).then_inc(ld_out, 16)
            for g in range(PAIRS):
                sp.wait_ge(x_done, NT + 2 * g + 2)
                sp.dma_start(out_tiles[:, 2 * g:2 * g + 2, :], x_sb[3][:, 2 * g:2 * g + 2, :]).then_inc(stored, 16)
            sp.wait_ge(stored, all_of(PAIRS))

        @block.gpsimd
        def _(pool):
            for t, v in ((ident, 0.0), (ones, 1.0), (avg, 1.0 / D), (tri, 1.0), (after, 1.0), (mhalf, -0.5), (zero, 0.0)):
                pool.memset(t[:, :], v).then_inc(consts_zeroed, 1)
            pool.wait_ge(consts_zeroed, 7)
            pool.affine_select(out=ident[:, :], in_=ident[:, :], compare_op=ALU.not_equal, fill=1.0, base=0,
                               pattern=[[-1, P]], channel_multiplier=1).then_inc(consts_done, 1)
            pool.affine_select(out=tri[:, :], in_=tri[:, :], compare_op=ALU.is_ge, fill=0.0, base=0,
                               pattern=[[1, P]], channel_multiplier=-1).then_inc(consts_done, 1)
            pool.affine_select(out=after[:, :], in_=after[:, :], compare_op=ALU.is_gt, fill=0.0, base=0,
                               pattern=[[-1, P]], channel_multiplier=1).then_inc(consts_done, 1)

            def inv_root(dst, src, n):
                return pool.tensor_tensor(dst, src, mhalf[:, 0:1].to_broadcast([P, n]), ALU.pow)

            def ln_rstd(k):
                pool.wait_ge(ve_done, k + 1)
                n = len(LN_TILES[k])
                inv_root(rstd[:, k, 0:n], ve[:, k, 0:n], n).then_inc(rstd_done, 1)

            def ffn(f):
                ln_rstd(4 * f)
                ln_rstd(4 * f + 1)
                pool.wait_ge(beta_ready, 1)
                for i in range(NT):
                    pool.wait_ge(xn_done, NT * 2 * f + i + 1)
                    pool.tensor_tensor(x_sb[2 * f][:, i, :], x_sb[2 * f][:, i, :], bet[:, :], ALU.add).then_inc(xb_done, 1)
                for s in range(STEPS):
                    pool.wait_ge(vs_done, STEPS * f + s + 1)
                    inv_root(rs[:, :], vs[:, :], NB).then_inc(rs_done, 1)
                ln_rstd(4 * f + 2)

            ffn(0)
            ln_rstd(3)

            def seg_moving(i):
                if i >= 2:
                    pool.wait_ge(seg_ready, i - 1)
                pool.tensor_tensor(R[:, i % 2, :, :], dA[:, i, :].unsqueeze(2).to_broadcast([P, NH, P]),
                                   tri[:, :].unsqueeze(1).to_broadcast([P, NH, P]), ALU.mult).then_inc(R_done, 1)

            def per_head(dst, src, w):
                return pool.tensor_tensor(dst.rearrange("p (h q) -> p h q", h=NH), src.rearrange("p (h q) -> p h q", h=NH),
                                          w.unsqueeze(2).to_broadcast([P, NH, HD]), ALU.mult)

            pool.wait_ge(dA_done, 1)
            seg_moving(0)
            seg_moving(1)
            pool.wait_ge(wd_done, 1)
            for i in range(NT):
                pool.wait_ge(xt_done, i + 1)
                if i >= 2:
                    pool.wait_ge(y_ps, i - 1)
                per_head(xdt[:, i % 2, :], xt[:, i % 2, :], dt[:, i, :]).then_inc(xdt_done, 1)
                if i in SSD_STATES:
                    if i >= 2:
                        pool.wait_ge(st_ps, n_states[i - 2])
                    per_head(xw[:, i % 2, :], xt[:, i % 2, :], wd[:, i, :]).then_inc(xw_done, 1)
                if i >= 2:
                    pool.wait_ge(yd_done, i - 1)
                per_head(xD[:, i % 2, :], xt[:, i % 2, :], head_par[:, 2, :]).then_inc(xD_done, 1)
                if i in SSD_STATES and i % NC > 0:
                    pool.wait_ge(S_done, n_states[i - 1])
                    per_head(Sd[:, i % 2, :], S[:, i % 2, :], dec[:, i, :]).then_inc(Sd_done, 1)
                if i + 2 < NT:
                    seg_moving(i + 2)
                pool.wait_ge(se_done, i + 1)
                inv_root(sr[:, i:i + 1], se[:, i:i + 1], 1).then_inc(sr_done, 1)
            ffn(1)

        @block.scalar
        def _(act):
            for name, n in ROWS:
                at, _ = row_at[name]
                act.dma_start(rows[at:at + n, :], a[name].rearrange("(t p) -> t p", p=P)).then_inc(ld_rows, 16)
            act.dma_start(w_gate[:, :, :], a["gate_w"].rearrange("(t p) n -> p t n", p=P)).then_inc(ld_gate, 16)
            act.dma_start(row_gate_b[:, :], as_row(a["gate_b"])).then_inc(ld_gate, 16)
            act.dma_start(row_bc_b[:, :], as_row(a["bc_b"])).then_inc(ld_bc, 16)
            act.dma_start(gam[:, :], every_partition(a["out_gamma"])).then_inc(ld_aff, 16)
            act.dma_start(bet[:, :], every_partition(a["out_beta"])).then_inc(ld_aff, 16)
            for n, name in enumerate(("dt_bias", "A_log", "D")):
                act.dma_start(head_par[:, n, :], every_partition(a[name])).then_inc(ld_head, 16)
            act.dma_start(conv_w[:, :, :], a["conv_w"].rearrange("(t p) k -> p t k", p=P)).then_inc(ld_conv, 16)

            def turn(r):
                for g in range(PAIRS):
                    n = PAIRS * r + g
                    act.wait_ge(xnT_ps, n + 1)
                    act.activation(xnT[:, :, 2 * P * g:2 * P * (g + 1)], bank[n % 2].rearrange("p (t n) -> p t n", t=KT),
                                   ACT.Copy).then_inc(xnT_done, 1)

            def ffn(f):
                turn(2 * f)
                for s in range(STEPS):
                    act.wait_ge(hb_done, STEPS * f + s + 1)
                    act.activation(hg[:, :, :], hb[:, :, :], ACT.Gelu).then_inc(gelu_done, 1)
                for g in range(PAIRS):
                    act.wait_ge(gate_ps, PAIRS * f + g + 1)
                    act.activation(sg[:, 2 * g:2 * g + 2, :], bank[(2, 3, 6, 7)[g]].rearrange("p (t n) -> p t n", t=2),
                                   ACT.Sigmoid).then_inc(sg_done, 1)

            ffn(0)
            turn(1)
            act.wait_ge(ld_head, all_of(3))
            act.activation(ea[:, :], head_par[:, 1, :], ACT.Exp).then_inc(ea_done, 1)
            act.wait_ge(dt_n, 1)
            act.activation(dte[:, :, :], dtn[:, :, :], ACT.Exp).then_inc(dt_e, 1)
            act.wait_ge(dt_e, 1)
            act.activation(dtl[:, :, :], dte[:, :, :], ACT.Ln, bias=ones[:, 0:1]).then_inc(dt_l, 1)

            act.wait_ge(ld_conv, 16)
            act.wait_ge(cols_ready, 1)

            def tap0(n):
                b, ct = divmod(n, CT)
                act.wait_ge(proj_ps, n + 1)
                if n >= 3:
                    act.wait_ge(xc_done, n - 2)
                act.activation(cv[:, n % 3, :], bank[(2, 3, 4)[n % 3]], ACT.Identity,
                               bias=col("conv_b")[:, ct:ct + 1], scale=conv_w[:, ct, CW - 1:CW]).then_inc(tap0_done, 1)

            def silu(n):
                b, ct = divmod(n, CT)
                act.wait_ge(conv_done, (CW - 1) * (n + 1))
                act.activation(xc[:, ct, b * L:(b + 1) * L], cv[:, n % 3, :], ACT.Silu).then_inc(xc_done, 1)

            for n in range(NB * CT):
                tap0(n)
                if n >= 1:
                    silu(n - 1)
            silu(NB * CT - 1)
            for i in range(NT):
                act.wait_ge(z_ps, i + 1)
                act.activation(sz[:, i, :], bank[6 + i % 2], ACT.Silu).then_inc(sz_done, 1)
            act.wait_ge(rest_done, 2)
            act.activation(ecs[:, :, :], cs[:, :, :], ACT.Exp).then_inc(exps_done, 1)
            act.activation(erest[:, :, :], rest[:, :, :], ACT.Exp).then_inc(exps_done, 1)
            act.activation(dec[:, :, :].rearrange("p t h -> p (t h)"), bank[5][:, N64:2 * N64], ACT.Exp).then_inc(exps_done, 1)

            def exp_seg(i):
                act.wait_ge(seg_ready, i + 1)
                if i >= 2:
                    act.wait_ge(M_done, i - 1)
                act.activation(E[:, i % 2, :, :].rearrange("p h l -> p (h l)"), seg_ps[:, :], ACT.Exp).then_inc(E_done, 1)

            def evac_u(i):
                act.wait_ge(uT_ps, i + 1)
                if i >= 2:
                    act.wait_ge(out_ps, i - 1)
                act.activation(uT[:, i % 2, :, :].rearrange("p t n -> p (t n)"), bank[(3 * (i + 1) + 1) % 2], ACT.Copy).then_inc(uT_done, 1)

            for i in range(NT):
                act.wait_ge(xt_ps, i + 1)
                if i >= 2:
                    act.wait_ge(xD_done, i - 1)
                act.activation(xt[:, i % 2, :], bank[(3 * i) % 2], ACT.Copy).then_inc(xt_done, 1)
                exp_seg(i)
                if i >= 1:
                    evac_u(i - 1)
                act.wait_ge(u_done, i + 1)
                if i >= 1:
                    act.wait_ge(ss_done, i)
                act.activation(usq[:, :], u[:, i % 2, :], ACT.Square, accum_out=ss[:, i:i + 1]).then_inc(ss_done, 1)
            evac_u(NT - 1)
            ffn(1)

        @block.tensor
        def _(pe):
            pe.wait_ge(consts_done, 3)
            pe.wait_ge(ld_rows, all_of(len(ROWS)))
            pe.transpose(bank[5][:, 0:n_rows], rows[:, :], ident[0:n_rows, 0:n_rows]).then_inc(rows_T, 1)

            def turn(r):
                for g in range(PAIRS):
                    n = PAIRS * r + g
                    for i in (2 * g, 2 * g + 1):
                        pe.wait_ge(xn_done, NT * r + i + 1)
                        if n >= 2 and i % 2 == 0:
                            pe.wait_ge(xnT_done, n - 1)
                        for t in range(KT):
                            last = pe.transpose(bank[n % 2][:, t * 2 * P + (i % 2) * P:t * 2 * P + (i % 2 + 1) * P],
                                                xn[:, i, t * P:(t + 1) * P], ident[:, :])
                    last.then_inc(xnT_ps, 1)

            def gates(f, g):
                if g == 0:
                    pe.wait_ge(ld_gate, all_of(2))
                pe.wait_ge(xnT_done, PAIRS * 2 * f + g + 1)
                dst = bank[(2, 3, 6, 7)[g]]
                for i in (2 * g, 2 * g + 1):
                    half = dst[:, (i % 2) * D:(i % 2 + 1) * D]
                    for t in range(KT):
                        pe.matmul(half, xnT[:, t, i * P:(i + 1) * P], w_gate[:, t, :], start=(t == 0), stop=False)
                    last = pe.matmul(half, ones[0:1, :], row_gate_b[:, :], start=False, stop=True)
                last.then_inc(gate_ps, 1)

            def d1_const():
                pe.wait_ge(cols_ready, 1)
                pe.wait_ge(ld_d1, 16)
                for m in range(HT):
                    for t in range(KT):
                        last = pe.matmul(bank[4][:, 64 + m:65 + m], w_d1[:, t, m * P:(m + 1) * P], col("pn_beta")[:, t:t + 1],
                                         start=(t == 0), stop=(t == KT - 1))
                last.then_inc(c1_ps, 1)

            def ffn(f):
                if f == 1:
                    pe.wait_ge(x2_done, NT)
                turn(2 * f)
                pe.wait_ge(xnn_done, NB * (f + 1))
                pe.wait_ge(cols_ready, 1)
                for b in range(NB):
                    for t in range(KT):
                        last = pe.matmul(bank[5][:, t * NB + b:t * NB + b + 1], xnn[:, b, t * P:(t + 1) * P], ident[:, P - 1:P],
                                         start=True, stop=True)
                last.then_inc(last_ps, 1)
                pe.wait_ge(ld_chain, 16)
                pe.wait_ge(last_done, f + 1)
                for m in range(KT):
                    for t in range(KT):
                        last = pe.matmul(bank[5][:, 4 + m * NB:4 + (m + 1) * NB], w_agg[:, t, m * P:(m + 1) * P], lastg[:, t, :],
                                         start=(t == 0), stop=(t == KT - 1))
                last.then_inc(agg_ps, 1)
                if f == 0:
                    d1_const()
                for s in range(STEPS):
                    n = STEPS * f + s
                    at = (STEPS + 1) * f + s
                    pe.wait_ge(th_done, at + 1)
                    for t in range(KT):
                        last = pe.matmul(bank[5][:, 8:8 + NB], avg[:, :], th[:, at, t, :], start=(t == 0), stop=(t == KT - 1))
                    last.then_inc(mean_ps, 1)
                    pe.wait_ge(sq_done, n + 1)
                    for t in range(KT):
                        last = pe.matmul(bank[5][:, 8:8 + NB], avg[:, :], sq[:, t, :], start=(t == 0), stop=(t == KT - 1))
                    last.then_inc(var_ps, 1)
                    if n == 0:
                        pe.wait_ge(d1_scaled, KT)
                        pe.wait_ge(c1_done, 1)
                    for m in range(HT):
                        for t in range(KT):
                            last = pe.matmul(bank[4][:, m * NB:(m + 1) * NB], w_d1[:, t, m * P:(m + 1) * P], dc[:, t, :],
                                             start=(t == 0), stop=(t == KT - 1))
                    last.then_inc(h_ps, 1)
                    gates(f, s)
                    pe.wait_ge(gelu_done, n + 1)
                    pe.wait_ge(ld_d2, 16)
                    for m in range(KT):
                        for t in range(HT):
                            last = pe.matmul(bank[5][:, 12 + m * NB:12 + (m + 1) * NB], w_d2[:, t, m * P:(m + 1) * P], hg[:, t, :],
                                             start=(t == 0), stop=(t == HT - 1))
                    last.then_inc(d2_ps, 1)
                pe.wait_ge(ld_bc, all_of(2))
                pe.wait_ge(thr_done, f + 1)
                for b in range(NB):
                    half = bank[4][:, b * D:(b + 1) * D]
                    for t in range(KT):
                        pe.matmul(half, thr[:, b, t, :], w_bc[:, t, :], start=(t == 0), stop=False)
                    last = pe.matmul(half, ones[0:1, :], row_bc_b[:, :], start=False, stop=True)
                last.then_inc(bc_ps, 1)

            ffn(0)
            turn(1)
            pe.wait_ge(ld_in, 16)
            pe.wait_ge(xnT_done, 2 * PAIRS)
            base = DI + CD
            for i in range(NT):
                for t in range(KT):
                    last = pe.matmul(bank[5][:, i * NH:(i + 1) * NH], xnT[:, t, i * P:(i + 1) * P], w_in[:, t, base:base + NH],
                                     start=(t == 0), stop=(t == KT - 1))
            last.then_inc(dt_ps, 1)

            def project(n):
                b, ct = divmod(n, CT)
                if n < 3:
                    pe.wait_ge(sg_done, PAIRS)
                    pe.wait_ge(ob_done, PAIRS)
                else:
                    pe.wait_ge(conv_done, (CW - 1) * (n - 2))
                for t in range(KT):
                    last = pe.matmul(bank[(2, 3, 4)[n % 3]], w_in[:, t, DI + ct * P:DI + (ct + 1) * P], xnT[:, t, b * L:(b + 1) * L],
                                     start=(t == 0), stop=(t == KT - 1))
                last.then_inc(proj_ps, 1)

            def gate_z(i):
                if i >= 2:
                    pe.wait_ge(sz_done, i - 1)
                for t in range(KT):
                    last = pe.matmul(bank[6 + i % 2], xnT[:, t, i * P:(i + 1) * P], w_in[:, t, 0:DI],
                                     start=(t == 0), stop=(t == KT - 1))
                last.then_inc(z_ps, 1)

            for n in range(NB * CT):
                project(n)
                if n == 2:
                    pe.wait_ge(dA_done, 1)
                    moving = dA[:, :, :].rearrange("p t h -> p (t h)")
                    pe.matmul(bank[5][:, 0:N64], tri[:, :], moving, start=True, stop=True)
                    pe.matmul(bank[5][:, N64:2 * N64], ones[:, :], moving, start=True, stop=True).then_inc(cs_ps, 1)
            for i in range(NT):
                gate_z(i)

            def tail(i):
                pe.wait_ge(u_done, i + 1)
                if i >= 1:
                    pe.wait_ge(x2_done, i)
                for t in range(XT):
                    last = pe.transpose(bank[(3 * (i + 1) + 1) % 2][:, t * P:(t + 1) * P], u[:, i % 2, t * P:(t + 1) * P], ident[:, :])
                last.then_inc(uT_ps, 1)
                pe.wait_ge(uT_done, i + 1)
                pe.wait_ge(out_scaled, XT)
                pe.wait_ge(xt_done, min(i + 2, NT))
                for t in range(XT):
                    last = pe.matmul(bank[(3 * (i + 1) + 2) % 2][:, 0:D], uT[:, i % 2, t, :], w_out[:, t, :],
                                     start=(t == 0), stop=(t == XT - 1))
                last.then_inc(out_ps, 1)

            for i in range(NT):
                tok = slice(i * P, (i + 1) * P)
                b = i // NC
                pe.wait_ge(xc_done, CT * (b + 1))
                if i >= 2:
                    pe.wait_ge(uT_done, i - 1)
                for t in range(XT):
                    last = pe.transpose(bank[(3 * i) % 2][:, t * P:(t + 1) * P], xc[:, t, tok], ident[:, :])
                last.then_inc(xt_ps, 1)
                pe.wait_ge(R_done, i + 1)
                if i >= 1:
                    pe.wait_ge(E_done, i)
                for j in range(2):
                    last = pe.matmul(bank[2 + j], after[:, :], R[:, i % 2, :, :].rearrange("p h l -> p (h l)")[:, j * 512:(j + 1) * 512],
                                     start=True, stop=True)
                last.then_inc(seg_ready, 1)
                if i >= 1:
                    pe.wait_ge(GB_done, 2 * i)
                else:
                    pe.wait_ge(exps_done, 3)
                pe.matmul(bank[5][:, 0:P], xc[:, XT, tok], xc[:, XT + 1, tok], start=True, stop=True)
                pe.transpose(bank[5][:, P:2 * P], xc[:, XT, tok], ident[:, :]).then_inc(G_ps, 1)
                if i in SSD_STATES:
                    pe.wait_ge(xw_done, n_states[i])
                    pe.wait_ge(GB_done, 2 * i + 2)
                    if n_states[i] >= 2:
                        pe.wait_ge(S_done, n_states[i] - 1)
                    pe.matmul(bank[4], Bt[:, i % 2, :], xw[:, i % 2, :], start=True, stop=True).then_inc(st_ps, 1)
                if i in SSD_OFF:
                    pe.wait_ge(S_done, n_states[i - 1])
                    if n_off[i] >= 2:
                        pe.wait_ge(yo_done, n_off[i] - 1)
                    pe.matmul(bank[7], xc[:, XT + 1, tok], S[:, i % 2, :], start=True, stop=True).then_inc(yoff_ps, 1)
                pe.wait_ge(M_done, i + 1)
                pe.wait_ge(xdt_done, i + 1)
                if i >= 1:
                    pe.wait_ge(yd_done, i)
                for h in range(NH):
                    last = pe.matmul(bank[6][:, h * HD:(h + 1) * HD], M[:, i % 2, h, :], xdt[:, i % 2, h * HD:(h + 1) * HD],
                                     start=True, stop=True)
                last.then_inc(y_ps, 1)
                if i >= 1:
                    tail(i - 1)
            tail(NT - 1)
            ffn(1)

        @block.vector
        def _(dve):
            def ln_stats(k, src, wait):
                tiles = LN_TILES[k]
                for n, i in enumerate(tiles):
                    wait(i)
                    dve.bn_stats(bn[:, k, n, :], src(n, i)).then_inc(bn_done, 1)
                for n, i in enumerate(tiles):
                    dve.wait_ge(bn_done, bn_before[k] + n + 1)
                    dve.bn_aggr(mv[:, k, n, :], bn[:, k, n, :]).then_inc(ag_done, 1)
                dve.wait_ge(ag_done, bn_before[k + 1])
                dve.tensor_scalar(ve[:, k, 0:len(tiles)], mv[:, k, 0:len(tiles), 1], LN_EPS[k], None, ALU.add).then_inc(ve_done, 1)

            def normalise(k, n, src, dst):
                return dve.tensor_scalar(dst, src, mv[:, k, n, 0:1], rstd[:, k, n:n + 1], ALU.subtract, ALU.mult)

            def norm_all(k, src, wait):
                r = XN_OF[k]
                ln_stats(k, lambda n, i: src[:, i, :], wait)
                dve.wait_ge(rstd_done, k + 1)
                if r > 0:
                    dve.wait_ge(xnT_ps, PAIRS * r)
                    dve.wait_ge(o_done, PAIRS)
                for i in range(NT):
                    normalise(k, i, src[:, i, :], xn[:, i, :]).then_inc(xn_done, 1)

            def ffn(f, wait):
                x, k = x_sb[2 * f], 4 * f
                norm_all(k, x, wait)
                ln_stats(k + 1, lambda n, i: xn[:, i, :], lambda i: dve.wait_ge(xn_done, NT * 2 * f + i + 1))
                dve.wait_ge(rstd_done, k + 2)
                for b in range(NB):
                    normalise(k + 1, b, xn[:, LAST[b], :], xnn[:, b, :]).then_inc(xnn_done, 1)
                if f == 0:
                    dve.wait_ge(rows_T, 1)
                    dve.tensor_copy(cols[:, :], bank[5][:, 0:n_rows]).then_inc(cols_ready, 1)
                    dve.wait_ge(cols_ready, 1)
                dve.wait_ge(last_ps, f + 1)
                wide = lambda v: v.unsqueeze(2).to_broadcast([P, v.shape[1], NB])
                dve.tensor_tensor(lastT[:, :, :], bank[5][:, 0:KT * NB].rearrange("p (t b) -> p t b", t=KT), wide(col("in_gamma")),
                                  ALU.mult).then_inc(last_mid, 1)
                dve.wait_ge(last_mid, f + 1)
                dve.tensor_tensor(lastg[:, :, :], lastT[:, :, :], wide(col("in_beta")), ALU.add).then_inc(last_done, 1)
                dve.wait_ge(agg_ps, f + 1)
                at = (STEPS + 1) * f
                dve.tensor_tensor(th[:, at, :, :], bank[5][:, 4:4 + KT * NB].rearrange("p (t b) -> p t b", t=KT), wide(col("agg_b")),
                                  ALU.add).then_inc(th_done, 1)
                if f == 0:
                    dve.wait_ge(ld_d1, 16)
                    dve.wait_ge(c1_ps, 1)
                    for t in range(KT):
                        dve.tensor_scalar(w_d1[:, t, :], w_d1[:, t, :], col("pn_gamma")[:, t:t + 1], None, ALU.mult).then_inc(d1_scaled, 1)
                    dve.tensor_tensor(c1[:, :], bank[4][:, 64:64 + HT], col("d1_b"), ALU.add).then_inc(c1_done, 1)
                    dve.wait_ge(ld_aff, all_of(2))
                    dve.tensor_scalar(gam[:, :], gam[:, :], 0.5, None, ALU.mult).then_inc(gamma_ready, 1)
                    dve.tensor_scalar(bet[:, :], bet[:, :], 0.5, None, ALU.mult).then_inc(beta_ready, 1)
                    dve.wait_ge(ld_out, 16)
                    for t in range(XT):
                        dve.tensor_scalar(w_out[:, t, :], w_out[:, t, :], col("norm_w")[:, t:t + 1], None, ALU.mult).then_inc(out_scaled, 1)
                for s in range(STEPS):
                    n, at = STEPS * f + s, (STEPS + 1) * f + s
                    dve.wait_ge(mean_ps, n + 1)
                    if n >= 1:
                        dve.wait_ge(h_ps, n)
                    dve.wait_ge(th_done, at + 1)
                    mean = bank[5][:, 8:8 + NB].unsqueeze(1).to_broadcast([P, KT, NB])
                    dve.tensor_tensor(dc[:, :, :], th[:, at, :, :], mean, ALU.subtract).then_inc(dc_done, 1)
                    dve.tensor_tensor(thb[:, n, :, :], th[:, at, :, :], wide(col("d2_b")), ALU.add).then_inc(thb_done, 1)
                    dve.wait_ge(dc_done, n + 1)
                    dve.tensor_tensor(sq[:, :, :], dc[:, :, :], dc[:, :, :], ALU.mult).then_inc(sq_done, 1)
                    dve.wait_ge(var_ps, n + 1)
                    dve.tensor_scalar(vs[:, :], bank[5][:, 8:8 + NB], EPS_FFN, None, ALU.add).then_inc(vs_done, 1)
                    dve.wait_ge(rs_done, n + 1)
                    dve.wait_ge(h_ps, n + 1)
                    dve.tensor_tensor(hr[:, :, :], bank[4][:, 0:HT * NB].rearrange("p (m b) -> p m b", m=HT),
                                      rs[:, :].unsqueeze(1).to_broadcast([P, HT, NB]), ALU.mult).then_inc(hr_done, 1)
                    dve.wait_ge(hr_done, n + 1)
                    dve.tensor_tensor(hb[:, :, :], hr[:, :, :], wide(c1[:, :]), ALU.add).then_inc(hb_done, 1)
                    dve.wait_ge(d2_ps, n + 1)
                    dve.wait_ge(thb_done, n + 1)
                    dve.tensor_tensor(th[:, at + 1, :, :], bank[5][:, 12:12 + KT * NB].rearrange("p (t b) -> p t b", t=KT),
                                      thb[:, n, :, :], ALU.add).then_inc(th_done, 1)
                at = (STEPS + 1) * f + STEPS
                dve.wait_ge(th_done, at + 1)
                for b in range(NB):
                    ins = dve.tensor_copy(thr[:, b, :, :], th[:, at, :, b].unsqueeze(2).to_broadcast([P, KT, P]))
                ins.then_inc(thr_done, 1)
                dve.wait_ge(bc_ps, f + 1)
                for g in range(PAIRS):
                    b = 2 * g // NC
                    dve.wait_ge(sg_done, PAIRS * f + g + 1)
                    pair = slice(2 * g, 2 * g + 2)
                    dve.tensor_tensor(o[:, pair, :], sg[:, pair, :], bank[4][:, b * D:(b + 1) * D].unsqueeze(1).to_broadcast([P, 2, D]),
                                      ALU.mult).then_inc(ob_done, 1)
                    dve.wait_ge(ob_done, PAIRS * f + g + 1)
                    dve.tensor_tensor(o[:, pair, :], o[:, pair, :], xn[:, pair, :], ALU.add).then_inc(o_done, 1)
                ln_stats(k + 2, lambda n, i: o[:, i, :], lambda i: dve.wait_ge(o_done, PAIRS * f + i // 2 + 1))
                dve.wait_ge(ag_done, bn_before[k + 3])
                dve.wait_ge(gamma_ready, 1)
                for i in range(NT):
                    dve.scalar_tensor_tensor(out=o[:, i, :], in0=o[:, i, :], scalar=mv[:, k + 2, i, 0:1], in1=gam[:, :],
                                             op0=ALU.subtract, op1=ALU.mult).then_inc(og_done, 1)
                dve.wait_ge(rstd_done, k + 3)
                dve.wait_ge(xb_done, NT * (f + 1))
                for i in range(NT):
                    dve.wait_ge(og_done, NT * f + i + 1)
                    dve.scalar_tensor_tensor(out=x_sb[2 * f + 1][:, i, :], in0=o[:, i, :], scalar=rstd[:, k + 2, i:i + 1],
                                             in1=x[:, i, :], op0=ALU.mult, op1=ALU.add).then_inc(x_done, 1)

            ffn(0, lambda i: dve.wait_ge(ld_x, all_of(2)))
            norm_all(3, x_sb[1], lambda i: dve.wait_ge(x_done, i + 1))

            by_tile = lambda v: v.unsqueeze(1).to_broadcast([P, NT, NH])
            dve.wait_ge(ld_head, all_of(3))
            dve.wait_ge(dt_ps, 1)
            dve.tensor_tensor(dtv[:, :, :], bank[5][:, 0:N64].rearrange("p (t h) -> p t h", t=NT), by_tile(head_par[:, 0, :]),
                              ALU.add).then_inc(dt_v, 1)
            dve.wait_ge(dt_v, 1)
            flat = lambda v: v[:, :, :].rearrange("p t h -> p (t h)")
            dve.scalar_tensor_tensor(out=flat(dtn), in0=flat(dtv), scalar=-1.0, in1=flat(dtv), op0=ALU.mult, op1=ALU.min).then_inc(dt_n, 1)
            dve.wait_ge(dt_l, 1)
            dve.scalar_tensor_tensor(out=flat(dt), in0=flat(dtv), scalar=0.0, in1=flat(dtl), op0=ALU.max, op1=ALU.add).then_inc(dt_done, 1)
            dve.wait_ge(dt_done, 1)
            dve.wait_ge(ea_done, 1)
            dve.scalar_tensor_tensor(out=dA[:, :, :], in0=dt[:, :, :], scalar=-1.0, in1=by_tile(ea[:, :]), op0=ALU.mult,
                                     op1=ALU.mult).then_inc(dA_done, 1)

            for n in range(NB * CT):
                b, ct = divmod(n, CT)
                dve.wait_ge(tap0_done, n + 1)
                for k in range(1, CW):
                    dst = cv[:, n % 3, k:L]
                    if k > 1:
                        dve.wait_ge(conv_done, (CW - 1) * n + k - 1)
                    dve.scalar_tensor_tensor(out=dst, in0=bank[(2, 3, 4)[n % 3]][:, 0:L - k], scalar=conv_w[:, ct, CW - 1 - k:CW - k],
                                             in1=dst, op0=ALU.mult, op1=ALU.add).then_inc(conv_done, 1)
                if n == 3:
                    dve.wait_ge(cs_ps, 1)
                    dve.tensor_copy(flat(cs), bank[5][:, 0:N64]).then_inc(cs_done, 1)
                    dve.wait_ge(cs_done, 1)
                    dve.tensor_tensor(flat(rest), bank[5][:, N64:2 * N64], flat(cs), ALU.subtract).then_inc(rest_done, 2)

            dve.wait_ge(exps_done, 2)
            dve.tensor_tensor(flat(wd), flat(erest), flat(dt), ALU.mult).then_inc(wd_done, 1)
            dve.wait_ge(exps_done, 3)
            heads = lambda v: v.rearrange("p (h q) -> p h q", h=NH)
            for i in range(NT):
                j = i % 2
                dve.wait_ge(G_ps, i + 1)
                if i >= 2:
                    dve.wait_ge(st_ps, n_states[i - 2])
                    dve.wait_ge(M_done, i - 1)
                dve.tensor_tensor(GT[:, j, :], bank[5][:, 0:P], tri[:, :], ALU.mult).then_inc(GB_done, 1)
                dve.tensor_copy(Bt[:, j, :], bank[5][:, P:2 * P]).then_inc(GB_done, 1)
                dve.wait_ge(E_done, i + 1)
                dve.wait_ge(GB_done, 2 * i + 1)
                if i >= 2:
                    dve.wait_ge(y_ps, i - 1)
                dve.tensor_tensor(M[:, j, :, :], E[:, j, :, :], GT[:, j, :].unsqueeze(1).to_broadcast([P, NH, P]), ALU.mult)\
                   .then_inc(M_done, 1)
                if i in SSD_STATES:
                    dve.wait_ge(st_ps, n_states[i])
                    if i >= 2:
                        dve.wait_ge(yoff_ps, n_off[i - 1])
                    if i % NC == 0:
                        dve.tensor_copy(S[:, (i + 1) % 2, :], bank[4]).then_inc(S_done, 1)
                    else:
                        dve.wait_ge(Sd_done, i // NC * (NC - 2) + i % NC)
                        dve.tensor_tensor(S[:, (i + 1) % 2, :], Sd[:, j, :], bank[4], ALU.add).then_inc(S_done, 1)
                if i in SSD_OFF:
                    dve.wait_ge(yoff_ps, n_off[i])
                    dve.tensor_tensor(heads(yo[:, j, :]), heads(bank[7]), ecs[:, i, :].unsqueeze(2).to_broadcast([P, NH, HD]), ALU.mult)\
                       .then_inc(yo_done, 1)
                dve.wait_ge(y_ps, i + 1)
                dve.wait_ge(xD_done, i + 1)
                dve.tensor_tensor(yd[:, j, :], bank[6], xD[:, j, :], ALU.add).then_inc(yd_done, 1)
                dve.wait_ge(yd_done, i + 1)
                if i in SSD_OFF:
                    dve.wait_ge(yo_done, n_off[i])
                    dve.tensor_tensor(yd[:, j, :], yd[:, j, :], yo[:, j, :], ALU.add).then_inc(yy_done, 1)
                    dve.wait_ge(yy_done, n_off[i])
                dve.wait_ge(sz_done, i + 1)
                if i >= 2:
                    dve.wait_ge(uT_ps, i - 1)
                    dve.wait_ge(ss_done, i - 1)
                dve.tensor_tensor(u[:, j, :], yd[:, j, :], sz[:, i, :], ALU.mult).then_inc(u_done, 1)

                def finish(i):
                    dve.wait_ge(ss_done, i + 1)
                    dve.tensor_scalar(se[:, i:i + 1], ss[:, i:i + 1], 1.0 / DI, EPS_LN, ALU.mult, ALU.add).then_inc(se_done, 1)

                def residual(i):
                    dve.wait_ge(out_ps, i + 1)
                    dve.wait_ge(sr_done, i + 1)
                    dve.scalar_tensor_tensor(out=x_sb[2][:, i, :], in0=bank[(3 * (i + 1) + 2) % 2][:, 0:D], scalar=sr[:, i:i + 1],
                                             in1=x_sb[1][:, i, :], op0=ALU.mult, op1=ALU.add).then_inc(x2_done, 1)
                finish(i)
                if i >= 1:
                    residual(i - 1)
            residual(NT - 1)
            ffn(1, lambda i: dve.wait_ge(x2_done, i + 1))


_SHORT = {
    "u": "L0_attn_u", "in_proj": "L0_attn_in_proj_kernel", "conv_w": "L0_attn_conv1d_weight", "conv_b": "L0_attn_conv1d_bias",
    "dt_bias": "L0_attn_dt_bias", "A_log": "L0_attn_A_log", "D": "L0_attn_D", "norm_w": "L0_attn_norm_weight",
    "out_proj": "L0_attn_out_proj_kernel", "in_gamma": "L0_ffn_in_gamma", "in_beta": "L0_ffn_in_beta", "agg_w": "L0_ffn_agg_w",
    "agg_b": "L0_ffn_agg_b", "pn_gamma": "L0_ffn_pn_gamma", "pn_beta": "L0_ffn_pn_beta", "d1_w": "L0_ffn_d1_w",
    "d1_b": "L0_ffn_d1_b", "d2_w": "L0_ffn_d2_w", "d2_b": "L0_ffn_d2_b", "bc_w": "L0_ffn_bc_w", "bc_b": "L0_ffn_bc_b",
    "gate_w": "L0_ffn_gate_w", "gate_b": "L0_ffn_gate_b", "out_gamma": "L0_ffn_out_gamma", "out_beta": "L0_ffn_out_beta",
}


def kernel(**inputs):
    import numpy as _np
    import concourse.bacc as _bacc
    from concourse import mybir as _mybir
    from concourse.bass_utils import run_bass_kernel_spmd as _run

    nc = _bacc.Bacc("TRN2", target_bir_lowering=False, num_devices=1)
    arrays, args = {}, {}
    for short, name in _SHORT.items():
        v = _np.ascontiguousarray(inputs[name])
        arrays[f"in_{name}"] = v
        args[short] = nc.dram_tensor(f"in_{name}", v.shape, _mybir.dt.from_np(v.dtype), kind="ExternalInput").ap()
    shape = arrays["in_L0_attn_u"].shape
    result = nc.dram_tensor("result", shape, _mybir.dt.float32, kind="ExternalOutput").ap()
    macaron_program(nc, args, result)
    r = _run(nc, [arrays], core_ids=[0])
    return r.results[0]["result"]
```

```python
from contextlib import ExitStack

import concourse.bass as bass
from concourse import mybir

F32 = mybir.dt.float32
BF16 = mybir.dt.bfloat16
AX = mybir.AxisListType
ALU = mybir.AluOpType
ACT = mybir.ActivationFunctionType

P = 128


def macaron_program(nc: bass.Bass, a, out):
    NB, L, D = a["u"].shape
    KT = D // P
    NT = NB * L // P
    NC = L // P
    DI, CW = a["out_proj"].shape[0], a["conv_w"].shape[1]
    NH = a["D"].shape[0]
    HD = DI // NH
    CD = a["conv_w"].shape[0]
    CT = CD // P
    XT = DI // P
    H = a["d1_w"].shape[1]
    HT = H // P
    STEPS = 4
    PAIRS = NT // 2
    LAST = [NC * (b + 1) - 1 for b in range(NB)]
    ORDER = LAST + [i for i in range(NT) if i not in LAST]
    EPS_LN, EPS_FFN = 1e-5, 1e-6

    with ExitStack() as ctx:
        def sb(name, shape, dt=F32):
            return ctx.enter_context(nc.sbuf_tensor(name, shape, dt))

        def sem(name):
            return ctx.enter_context(nc.semaphore(name))

        banks = [ctx.enter_context(nc.psum_tensor(f"bank{i}", [P, 512], F32)) for i in (0, 1)]
        seg_ps = ctx.enter_context(nc.psum_tensor("seg_ps", [P, 1024], F32))
        banks += [seg_ps[:, 0:512], seg_ps[:, 512:1024]]
        banks += [ctx.enter_context(nc.psum_tensor(f"bank{i}", [P, 512], F32)) for i in (4, 5, 6, 7)]
        bank = [x[:, :] for x in banks]

        x_sb = [sb(f"x{n}", [P, NT, D]) for n in range(3)]
        x_sb.append(x_sb[0])
        xn = sb("xn", [P, NT, D])
        xnT = sb("xnT", [P, KT, NT * P])
        ident = sb("ident", [P, P])
        ones = sb("ones", [P, P])
        avg = sb("avg", [P, P])
        tri = sb("tri", [P, P])
        after = sb("after", [P, P])
        mhalf = sb("mhalf", [P, 1])
        zero = sb("zero", [P, 1])

        w_in = sb("w_in", [P, KT, a["in_proj"].shape[1]])
        w_out = sb("w_out", [P, XT, D])
        w_gate = sb("w_gate", [P, KT, D])
        w_agg = sb("w_agg", [P, KT, D])
        w_bc = sb("w_bc", [P, KT, D])
        w_d1 = sb("w_d1", [P, 3, KT, H], BF16)
        w_d2 = sb("w_d2", [P, 3, HT, D], BF16)
        conv_w = sb("conv_w", [P, CT, CW])
        row_gate_b = sb("row_gate_b", [1, D])
        gam = sb("gam", [P, D])
        bet = sb("bet", [P, D])
        head_par = sb("head_par", [P, 3, NH])
        ROWS = [("in_gamma", KT), ("in_beta", KT), ("agg_b", KT), ("pn_gamma", KT), ("pn_beta", KT),
                ("d2_b", KT), ("d1_b", HT), ("norm_w", XT), ("conv_b", CT), ("bc_b", KT)]
        row_at, n_rows = {}, 0
        for name, n in ROWS:
            row_at[name] = (n_rows, n)
            n_rows += n
        rows = sb("rows", [n_rows, P])
        cols = sb("cols", [P, n_rows])

        def col(name):
            at, n = row_at[name]
            return cols[:, at:at + n]

        OTHERS = [i for i in range(NT) if i not in LAST]
        HALF = [list(range(NT // 2)), list(range(NT // 2, NT))]
        LN = [("in", 0, LAST, EPS_LN), ("last", 0, LAST, EPS_FFN), ("in", 1, OTHERS, EPS_LN),
              ("out", 0, HALF[0], EPS_FFN), ("out", 0, HALF[1], EPS_FFN),
              ("mamba", 0, HALF[0], EPS_LN),
              ("mamba", 1, HALF[1], EPS_LN)]
        IN2, LAST2 = {}, {}
        for p, i in enumerate(ORDER):
            IN2[p] = len(LN)
            LN.append(("in", 1, [i], EPS_LN))
            if i in LAST:
                LAST2[p] = len(LN)
                LN.append(("last", 1, [i], EPS_FFN))
        OUT2 = len(LN)
        LN += [("out", 1, ORDER[:NT // 2], EPS_FFN), ("out", 1, ORDER[NT // 2:], EPS_FFN)]
        LN_TILES = [g[2] for g in LN]
        LN_EPS = [g[3] for g in LN]
        MAMBA_LN = 5
        bn_before = [sum(len(t) for t in LN_TILES[:k]) for k in range(len(LN_TILES) + 1)]
        bn = sb("bn", [P, bn_before[-1], 6])
        mv = sb("mv", [P, bn_before[-1], 2])
        ve = sb("ve", [P, bn_before[-1]])
        rstd = sb("rstd", [P, bn_before[-1]])

        xnn = sb("xnn", [P, NB, D])
        sz = sb("sz", [P, NT, DI])
        sg, o = sz[:, :, 0:D], sz[:, :, D:2 * D]
        lastT = sb("lastT", [P, KT, NB])
        lastg = sb("lastg", [P, KT, NB])
        th = sb("th", [P, 2 * (STEPS + 1), KT, NB])
        thb = sb("thb", [P, 2 * STEPS, KT, NB])
        tg = sb("tg", [P, KT, NB])
        tr = sb("tr", [P, KT, NB])
        TC = NB + 2
        tp = sb("tp", [P, KT, 3, TC], BF16)
        gb_rest = sb("gb_rest", [P, KT, 2])
        gb_mid = sb("gb_mid", [P, KT, 2])
        hp = sb("hp", [P, HT, 3, NB], BF16)
        hrest = sb("hrest", [P, HT, NB])
        mu = sb("mu", [P, NB])
        gW = sb("gW", [P, HT])
        mgW = sb("mgW", [P, HT, NB])
        hs = sb("hs", [P, HT, NB])
        hc = sb("hc", [P, HT, NB])
        dsum = sb("dsum", [P, KT, NB])
        bcol = sb("bcol", [P, KT, NB])
        brest = sb("brest", [P, KT, NB])
        bp = sb("bp", [P, 3, KT, NB], BF16)
        identb = sb("identb", [P, P], BF16)
        onesb = sb("onesb", [P, P], BF16)
        dc = sb("dc", [P, KT, NB])
        sq = sb("sq", [P, KT, NB])
        vs = sb("vs", [P, NB])
        rs = sb("rs", [P, NB])
        hr = sb("hr", [P, HT, NB])
        hb = sb("hb", [P, HT, NB])
        hg = sb("hg", [P, HT, NB])
        c1 = sb("c1", [P, HT])

        cv = sb("cv", [P, 3, L])
        flat_cv = cv[:, :, :].rearrange("p t n -> p (t n)")
        uT = flat_cv[:, 0:2 * DI].rearrange("p (s t n) -> p s t n", s=2, n=P)
        usq = flat_cv[:, 2 * DI:3 * DI]
        bdiag = sb("bdiag", [P, 3, KT * NB, P], BF16)
        xc = sb("xc", [P, CT, NB * L])
        flat_xc = xc[:, :, :].rearrange("p t n -> p (t n)")
        raw = [flat_xc[:, 0:KT * H], flat_xc[:, KT * H:2 * KT * H]]
        left = flat_xc[:, 2 * KT * H:3 * KT * H]
        N64 = NT * NH
        dtv = sb("dtv", [P, NT, NH])
        dtn = sb("dtn", [P, NT, NH])
        dte = sb("dte", [P, NT, NH])
        dtl = sb("dtl", [P, NT, NH])
        dt = sb("dt", [P, NT, NH])
        ea = sb("ea", [P, NH])
        dA = sb("dA", [P, NT, NH])
        cs = sb("cs", [P, NT, NH])
        ecs = sb("ecs", [P, NT, NH])
        dec = sb("dec", [P, NT, NH])
        rest = sb("rest", [P, NT, NH])
        erest = sb("erest", [P, NT, NH])
        wd = sb("wd", [P, NT, NH])
        R = sb("R", [P, 2, NH, P])
        E = sb("E", [P, 2, NH, P])
        M = E
        GT = sb("GT", [P, 2, P])
        Bt = sb("Bt", [P, 2, P])
        xt = sb("xt", [P, NT, DI])
        xw = sb("xw", [P, 2, DI])
        xdt = xw
        xD = sb("xD", [P, 2, DI])
        S_more = sb("S_more", [P, 2, DI])
        S_first = x_sb[0][:, :, :].rearrange("p t n -> p (t n)").rearrange("p (s n) -> p s n", n=DI)
        yo = sb("yo", [P, 2, DI])
        Sd = yo
        yd = sb("yd", [P, 2, DI])
        ss = sb("ss", [P, NT])
        se = sb("se", [P, NT])
        sr = sb("sr", [P, NT])

        ld_x, ld_x2, ld_rows, ld_chain, ld_d1, ld_d2, ld_gate, ld_bc, ld_aff, ld_head, ld_in, ld_conv, ld_out = map(
            sem, "ld_x ld_x2 ld_rows ld_chain ld_d1 ld_d2 ld_gate ld_bc ld_aff ld_head ld_in ld_conv ld_out".split())
        consts_zeroed, consts_done, rows_T, cols_ready, gamma_ready, beta_ready, out_scaled = map(
            sem, "consts_zeroed consts_done rows_T cols_ready gamma_ready beta_ready out_scaled".split())
        bn_done, ag_done, ve_done, rstd_done, xn_done, xnn_done = map(
            sem, "bn_done ag_done ve_done rstd_done xn_done xnn_done".split())
        xnT_ps, xnT_done, gate_ps, sg_done = map(sem, "xnT_ps xnT_done gate_ps sg_done".split())
        xnT2_ps, xnT2_done, gate2_ps, sg2_done = map(sem, "xnT2_ps xnT2_done gate2_ps sg2_done".split())
        w_hi, w_left, w_mid, w_lo, gb_parts, gb_left = map(sem, "w_hi w_left w_mid w_lo gb_parts gb_left".split())
        last_ps, last_mid, last_done, agg_ps, th_done, consts16 = map(
            sem, "last_ps last_mid last_done agg_ps th_done consts16".split())
        tg_done, t_hi, t_left, t_mid, t_lo, mean_ps, mu_done, dc_done, sq_done, var_ps, vs_done, rs_done = map(
            sem, "tg_done t_hi t_left t_mid t_lo mean_ps mu_done dc_done sq_done var_ps vs_done rs_done".split())
        gW_done, c1_done, mgW_done, h_ps, hs_done, hc_done, hr_done, hb_done, gelu_done, h_hi, h_left, h_mid, h_lo = map(
            sem, "gW_done c1_done mgW_done h_ps hs_done hc_done hr_done hb_done gelu_done h_hi h_left h_mid h_lo".split())
        d2_ps, thb_done, dsum_done, bcol_ps, bcol_done, b_hi, b_left, b_mid, b_lo, bdiag_done, bc_ps = map(
            sem, "d2_ps thb_done dsum_done bcol_ps bcol_done b_hi b_left b_mid b_lo bdiag_done bc_ps".split())
        ob_done, o_done, og_done, xb_done, x_done = map(sem, "ob_done o_done og_done xb_done x_done".split())
        dt_ps, dt_v, dt_n, dt_e, dt_l, dt_done, ea_done, dA_done, cs_ps, cs_done, rest_done, exps_done, wd_done = map(
            sem, "dt_ps dt_v dt_n dt_e dt_l dt_done ea_done dA_done cs_ps cs_done rest_done exps_done wd_done".split())
        proj_ps, tap0_done, conv_done, xc_done, z_ps, sz_done = map(
            sem, "proj_ps tap0_done conv_done xc_done z_ps sz_done".split())
        R_done, seg_ready, E_done, M_done, G_ps, GT_done, Bt_ps, Bt_done = map(
            sem, "R_done seg_ready E_done M_done G_ps GT_done Bt_ps Bt_done".split())
        xt_ps, xt_done, xdt_done, xw_done, xD_done, st_ps, Sd_done, S_done = map(
            sem, "xt_ps xt_done xdt_done xw_done xD_done st_ps Sd_done S_done".split())
        y_ps, yoff_ps, yo_done, yd_done, xo_done, u_done, ss_done, se_done, sr_done = map(
            sem, "y_ps yoff_ps yo_done yd_done xo_done u_done ss_done se_done sr_done".split())
        uT_ps, uT_done, out_ps, x2_done, stored = map(
            sem, "uT_ps uT_done out_ps x2_done stored".split())

        block = ctx.enter_context(nc.Block())
        x_tiles = a["u"].rearrange("b (c p) d -> p (b c) d", p=P)
        out_tiles = out.rearrange("b (c p) d -> p (b c) d", p=P)

        def as_row(v):
            return v.rearrange("(o n) -> o n", o=1)

        def every_partition(v):
            return as_row(v).to_broadcast([P, v.shape[0]])

        def all_of(n):
            return 16 * n

        XN_ORDER = LAST + OTHERS, list(range(NT)), ORDER

        def xn_ready(r, i):
            return NT * r + XN_ORDER[r].index(i) + 1
        STATES = [i for i in range(NT) if i % NC < NC - 1]
        Z_WITH = {1 + n: n for n in range(NT - 2)}
        TURN_WITH = {CT + 1 + i: i for i in range(NC)}
        STATE_WITH = {CT + 2 + n: n for n in range(NC - 1)}
        Z_ORDER = ORDER

        def state(i):
            n = STATES.index(i)
            return S_first[:, n, :] if n < NT // 2 else S_more[:, n - NT // 2, :]

        def offs(p):
            return sum(i % NC > 0 for i in ORDER[:p])

        THOUGHT_AT = NB + 1
        STEP_AT = {THOUGHT_AT + 1 + s: s for s in range(STEPS)}

        @block.sync
        def _(sp):
            for i in LAST:
                sp.dma_start(x_sb[0][:, i, :], x_tiles[:, i, :]).then_inc(ld_x, 16)
            sp.dma_start(raw[0].rearrange("p (t n) -> p t n", t=KT), a["d1_w"].rearrange("(t p) n -> p t n", p=P)).then_inc(ld_d1, 16)
            sp.dma_start(w_agg[:, :, :], a["agg_w"].rearrange("(t p) n -> p t n", p=P)).then_inc(ld_chain, 16)
            sp.dma_start(raw[1].rearrange("p (t n) -> p t n", t=HT), a["d2_w"].rearrange("(t p) n -> p t n", p=P)).then_inc(ld_d2, 16)
            for b in range(NB):
                sp.dma_start(x_sb[0][:, NC * b:LAST[b], :], x_tiles[:, NC * b:LAST[b], :]).then_inc(ld_x2, 16)
            sp.dma_start(w_gate[:, :, :], a["gate_w"].rearrange("(t p) n -> p t n", p=P)).then_inc(ld_gate, 16)
            sp.dma_start(w_bc[:, :, :], a["bc_w"].rearrange("(t p) n -> p t n", p=P)).then_inc(ld_bc, 16)
            sp.dma_start(w_in[:, :, :], a["in_proj"].rearrange("(t p) n -> p t n", p=P)).then_inc(ld_in, 16)
            sp.dma_start(w_out[:, :, :], a["out_proj"].rearrange("(t p) n -> p t n", p=P)).then_inc(ld_out, 16)
            for p, i in enumerate(ORDER):
                sp.wait_ge(x_done, NT + p + 1)
                sp.dma_start(out_tiles[:, i, :], x_sb[3][:, i, :]).then_inc(stored, 16)
            sp.wait_ge(stored, all_of(NT))

        @block.gpsimd
        def _(pool):
            for t, v in ((ident, 0.0), (ones, 1.0), (avg, 1.0 / D), (tri, 1.0), (after, 1.0), (mhalf, -0.5), (zero, 0.0)):
                pool.memset(t[:, :], v).then_inc(consts_zeroed, 1)
            pool.wait_ge(consts_zeroed, 7)
            pool.affine_select(out=ident[:, :], in_=ident[:, :], compare_op=ALU.not_equal, fill=1.0, base=0,
                               pattern=[[-1, P]], channel_multiplier=1).then_inc(consts_done, 1)
            pool.affine_select(out=tri[:, :], in_=tri[:, :], compare_op=ALU.is_ge, fill=0.0, base=0,
                               pattern=[[1, P]], channel_multiplier=-1).then_inc(consts_done, 1)
            pool.affine_select(out=after[:, :], in_=after[:, :], compare_op=ALU.is_gt, fill=0.0, base=0,
                               pattern=[[-1, P]], channel_multiplier=1).then_inc(consts_done, 1)

            def inv_root(dst, src, n):
                return pool.tensor_tensor(dst, src, mhalf[:, 0:1].to_broadcast([P, n]), ALU.pow)

            def ln_rstd(k):
                pool.wait_ge(ve_done, k + 1)
                n = slice(bn_before[k], bn_before[k + 1])
                inv_root(rstd[:, n], ve[:, n], len(LN_TILES[k])).then_inc(rstd_done, 1)

            def thought_rstd(n):
                pool.wait_ge(vs_done, n + 1)
                inv_root(rs[:, :], vs[:, :], NB).then_inc(rs_done, 1)

            def add_beta(x, part):
                pool.wait_ge(beta_ready, 1)
                pool.tensor_tensor(x[:, part, :], x[:, part, :],
                                   bet[:, :].unsqueeze(1).to_broadcast([P, part.stop - part.start, D]), ALU.add).then_inc(xb_done, 1)

            pool.wait_ge(consts_done, 3)
            pool.tensor_copy(identb[:, :], ident[:, :]).then_inc(consts16, 1)
            pool.tensor_copy(onesb[:, :], ones[:, :]).then_inc(consts16, 1)
            ln_rstd(0)
            ln_rstd(1)
            for s in range(STEPS):
                if s == 1:
                    ln_rstd(2)
                thought_rstd(s)
                if s == 2:
                    pool.wait_ge(xn_done, NT)
                    for h in HALF:
                        add_beta(x_sb[0], slice(h[0], h[-1] + 1))
            for k in range(3, MAMBA_LN + 2):
                ln_rstd(k)

            def seg_moving(p):
                if p >= 2:
                    pool.wait_ge(seg_ready, p - 1)
                pool.tensor_tensor(R[:, p % 2, :, :], dA[:, ORDER[p], :].unsqueeze(2).to_broadcast([P, NH, P]),
                                   tri[:, :].unsqueeze(1).to_broadcast([P, NH, P]), ALU.mult).then_inc(R_done, 1)

            def per_head(dst, src, w):
                return pool.tensor_tensor(dst.rearrange("p (h q) -> p h q", h=NH), src.rearrange("p (h q) -> p h q", h=NH),
                                          w.unsqueeze(2).to_broadcast([P, NH, HD]), ALU.mult)

            def x_dt(p):
                i = ORDER[p]
                pool.wait_ge(xt_done, i + 1)
                if p >= 2:
                    pool.wait_ge(y_ps, p - 1)
                else:
                    pool.wait_ge(st_ps, len(STATES))
                per_head(xdt[:, p % 2, :], xt[:, i, :], dt[:, i, :]).then_inc(xdt_done, 1)

            def x_D(p):
                if p >= 2:
                    pool.wait_ge(yd_done, p - 1)
                per_head(xD[:, p % 2, :], xt[:, ORDER[p], :], head_par[:, 2, :]).then_inc(xD_done, 1)

            pool.wait_ge(ld_out, 16)
            pool.wait_ge(cols_ready, 1)
            for t in range(XT):
                pool.tensor_scalar(w_out[:, t, :], w_out[:, t, :], col("norm_w")[:, t:t + 1], None, ALU.mult).then_inc(out_scaled, 1)
            pool.wait_ge(dA_done, 1)
            seg_moving(0)
            seg_moving(1)
            pool.wait_ge(wd_done, 1)
            for n, i in enumerate(STATES):
                pool.wait_ge(xt_done, i + 1)
                if n >= 2:
                    pool.wait_ge(st_ps, n - 1)
                per_head(xw[:, n % 2, :], xt[:, i, :], wd[:, i, :]).then_inc(xw_done, 1)
            x_dt(0)
            x_D(0)
            for p in range(NT):
                if p + 1 < NT:
                    x_dt(p + 1)
                if p + 2 < NT:
                    seg_moving(p + 2)
                if p in STEP_AT:
                    thought_rstd(STEPS + STEP_AT[p])
                if ORDER[p] % NC > 0:
                    pool.wait_ge(yo_done, offs(p) + 1)
                    pool.wait_ge(xD_done, p + 1)
                    pool.tensor_tensor(xD[:, p % 2, :], xD[:, p % 2, :], yo[:, p % 2, :], ALU.add).then_inc(xo_done, 1)
                if p + 1 < NT:
                    x_D(p + 1)
                if p >= 1:
                    ln_rstd(IN2[p - 1])
                    if p - 1 in LAST2:
                        ln_rstd(LAST2[p - 1])
                pool.wait_ge(se_done, p + 1)
                inv_root(sr[:, ORDER[p]:ORDER[p] + 1], se[:, ORDER[p]:ORDER[p] + 1], 1).then_inc(sr_done, 1)
                if p >= 4:
                    pool.wait_ge(xn_done, 2 * NT + p - 3)
                    add_beta(x_sb[2], slice(ORDER[p - 4], ORDER[p - 4] + 1))
            ln_rstd(IN2[NT - 1])
            for p in range(NT - 4, NT):
                pool.wait_ge(xn_done, 2 * NT + p + 1)
                add_beta(x_sb[2], slice(ORDER[p], ORDER[p] + 1))
            ln_rstd(OUT2)
            ln_rstd(OUT2 + 1)

        @block.scalar
        def _(act):
            for name, n in ROWS:
                at, _ = row_at[name]
                act.dma_start(rows[at:at + n, :], a[name].rearrange("(t p) -> t p", p=P)).then_inc(ld_rows, 16)
            act.dma_start(row_gate_b[:, :], as_row(a["gate_b"])).then_inc(ld_gate, 16)
            act.dma_start(gam[:, :], every_partition(a["out_gamma"])).then_inc(ld_aff, 16)
            act.dma_start(bet[:, :], every_partition(a["out_beta"])).then_inc(ld_aff, 16)
            for n, name in enumerate(("dt_bias", "A_log", "D")):
                act.dma_start(head_par[:, n, :], every_partition(a[name])).then_inc(ld_head, 16)
            act.dma_start(conv_w[:, :, :], a["conv_w"].rearrange("(t p) k -> p t k", p=P)).then_inc(ld_conv, 16)

            def turn(r, pairs):
                for g in pairs:
                    n = PAIRS * r + g
                    act.wait_ge(xnT_ps, n + 1)
                    act.activation(xnT[:, :, 2 * P * g:2 * P * (g + 1)], bank[n % 2].rearrange("p (t n) -> p t n", t=KT),
                                   ACT.Copy).then_inc(xnT_done, 1)

            def gate(f, g):
                act.wait_ge(gate_ps, PAIRS * f + g + 1)
                act.activation(sg[:, 2 * g:2 * g + 2, :], bank[(2, 3, 6, 7)[g]].rearrange("p (t n) -> p t n", t=2),
                               ACT.Tanh, scale=0.5).then_inc(sg_done, 1)

            def split(n, ld, parts):
                act.wait_ge(ld, 16)
                act.activation(parts(0), raw[n], ACT.Copy).then_inc(w_hi, 1)
                act.wait_ge(w_left, n + 1)
                act.activation(parts(1), left, ACT.Copy).then_inc(w_mid, 1)

            def gelu(n):
                act.wait_ge(hb_done, n + 1)
                act.activation(hg[:, :, :], hb[:, :, :], ACT.Gelu).then_inc(gelu_done, 1)

            split(0, ld_d1, lambda c: w_d1[:, c, :, :].rearrange("p t n -> p (t n)"))
            split(1, ld_d2, lambda c: w_d2[:, c, :, :].rearrange("p t n -> p (t n)"))
            for s in range(STEPS):
                gelu(s)
                if s == 1:
                    turn(0, range(PAIRS))
                if s == 2:
                    gate(0, 0)
                if s == 3:
                    gate(0, 1)
                    gate(0, 2)
            gate(0, 3)
            turn(1, range(PAIRS))
            act.wait_ge(ld_head, all_of(3))
            act.activation(ea[:, :], head_par[:, 1, :], ACT.Exp).then_inc(ea_done, 1)
            act.wait_ge(dt_n, 1)
            act.activation(dte[:, :, :], dtn[:, :, :], ACT.Exp).then_inc(dt_e, 1)
            act.wait_ge(dt_e, 1)
            act.activation(dtl[:, :, :], dte[:, :, :], ACT.Ln, bias=ones[:, 0:1]).then_inc(dt_l, 1)

            act.wait_ge(ld_conv, 16)
            act.wait_ge(cols_ready, 1)

            def tap0(n):
                b, ct = divmod(n, CT)
                act.wait_ge(proj_ps, n + 1)
                if n >= 3:
                    act.wait_ge(xc_done, n - 2)
                act.activation(cv[:, n % 3, :], bank[(2, 3, 4)[n % 3]], ACT.Identity,
                               bias=col("conv_b")[:, ct:ct + 1], scale=conv_w[:, ct, CW - 1:CW]).then_inc(tap0_done, 1)

            def silu(n):
                b, ct = divmod(n, CT)
                act.wait_ge(conv_done, (CW - 1) * (n + 1))
                act.activation(xc[:, ct, b * L:(b + 1) * L], cv[:, n % 3, :], ACT.Silu).then_inc(xc_done, 1)

            def decays():
                act.wait_ge(rest_done, 2)
                act.activation(ecs[:, :, :], cs[:, :, :], ACT.Exp).then_inc(exps_done, 1)
                act.activation(erest[:, :, :], rest[:, :, :], ACT.Exp).then_inc(exps_done, 1)
                act.activation(dec[:, :, :].rearrange("p t h -> p (t h)"), bank[5][:, N64:2 * N64], ACT.Exp).then_inc(exps_done, 1)

            def silu_z(n):
                act.wait_ge(z_ps, n + 1)
                act.activation(sz[:, Z_ORDER[n], :], bank[6], ACT.Silu).then_inc(sz_done, 1)

            def evac_x(i):
                act.wait_ge(xt_ps, i + 1)
                act.activation(xt[:, i, :], bank[i % 2], ACT.Copy).then_inc(xt_done, 1)

            for n in range(NB * CT):
                tap0(n)
                if n >= 1:
                    silu(n - 1)
                if n in Z_WITH:
                    silu_z(Z_WITH[n])
                if n == CT:
                    decays()
                if n in TURN_WITH:
                    evac_x(TURN_WITH[n])
            silu_z(NT - 2)
            silu(NB * CT - 1)
            evac_x(NC)
            silu_z(NT - 1)
            for i in range(NC + 1, NT):
                evac_x(i)

            def exp_seg(p):
                act.wait_ge(seg_ready, p + 1)
                if p >= 2:
                    act.wait_ge(y_ps, p - 1)
                act.activation(E[:, p % 2, :, :].rearrange("p h l -> p (h l)"), seg_ps[:, :], ACT.Exp).then_inc(E_done, 1)

            def evac_u(p):
                act.wait_ge(uT_ps, p + 1)
                if p >= 2:
                    act.wait_ge(out_ps, p - 1)
                act.activation(uT[:, p % 2, :, :].rearrange("p t n -> p (t n)"), bank[0], ACT.Copy).then_inc(uT_done, 1)

            def evac_xnT2(p):
                i = ORDER[p]
                act.wait_ge(xnT2_ps, p + 1)
                act.activation(xnT[:, :, i * P:(i + 1) * P], bank[0][:, 0:D].rearrange("p (t n) -> p t n", t=KT), ACT.Copy)\
                   .then_inc(xnT2_done, 1)

            def gate2(p):
                act.wait_ge(gate2_ps, p + 1)
                act.activation(sg[:, ORDER[p], :], bank[1][:, 0:D], ACT.Tanh, scale=0.5).then_inc(sg2_done, 1)

            exp_seg(0)
            for p in range(NT):
                i = ORDER[p]
                if p + 1 < NT:
                    exp_seg(p + 1)
                if p >= 1:
                    evac_u(p - 1)
                if p in STEP_AT:
                    gelu(STEPS + STEP_AT[p])
                if p >= 2:
                    evac_xnT2(p - 2)
                act.wait_ge(u_done, p + 1)
                if p >= 1:
                    act.wait_ge(ss_done, p)
                act.activation(usq, yd[:, p % 2, :], ACT.Square, accum_out=ss[:, i:i + 1]).then_inc(ss_done, 1)
                if p >= 2:
                    gate2(p - 2)
            evac_u(NT - 1)
            for p in range(NT - 2, NT):
                evac_xnT2(p)
                gate2(p)

        @block.tensor
        def _(pe):
            pe.wait_ge(consts_done, 3)
            pe.wait_ge(ld_rows, all_of(len(ROWS)))
            pe.transpose(bank[5][:, 0:n_rows], rows[:, :], ident[0:n_rows, 0:n_rows]).then_inc(rows_T, 1)

            def turn(r, pairs):
                for g in pairs:
                    n = PAIRS * r + g
                    if n >= 2:
                        pe.wait_ge(xnT_done, n - 1)
                    for i in (2 * g, 2 * g + 1):
                        pe.wait_ge(xn_done, xn_ready(r, i))
                        for t in range(KT):
                            last = pe.transpose(bank[n % 2][:, t * 2 * P + (i % 2) * P:t * 2 * P + (i % 2 + 1) * P],
                                                xn[:, i, t * P:(t + 1) * P], ident[:, :])
                    last.then_inc(xnT_ps, 1)

            def gates(f, g):
                if g == 0:
                    pe.wait_ge(ld_gate, all_of(2))
                pe.wait_ge(xnT_done, PAIRS * 2 * f + g + 1)
                dst = bank[(2, 3, 6, 7)[g]]
                for i in (2 * g, 2 * g + 1):
                    half = dst[:, (i % 2) * D:(i % 2 + 1) * D]
                    for t in range(KT):
                        pe.matmul(half, xnT[:, t, i * P:(i + 1) * P], w_gate[:, t, :], start=(t == 0), stop=False)
                    last = pe.matmul(half, ones[0:1, :], row_gate_b[:, :], start=False, stop=True)
                last.then_inc(gate_ps, 1)

            def thought_in(f):
                pe.wait_ge(xnn_done, NB * (f + 1))
                pe.wait_ge(cols_ready, 1)
                for b in range(NB):
                    for t in range(KT):
                        last = pe.matmul(bank[5][:, t * NB + b:t * NB + b + 1], xnn[:, b, t * P:(t + 1) * P], ident[:, P - 1:P],
                                         start=True, stop=True)
                last.then_inc(last_ps, 1)

            def thought_agg(f):
                pe.wait_ge(ld_chain, 16)
                pe.wait_ge(last_done, f + 1)
                for m in range(KT):
                    for t in range(KT):
                        last = pe.matmul(bank[5][:, 4 + m * NB:4 + (m + 1) * NB], w_agg[:, t, m * P:(m + 1) * P], lastg[:, t, :],
                                         start=(t == 0), stop=(t == KT - 1))
                last.then_inc(agg_ps, 1)

            def variance(n):
                pe.wait_ge(sq_done, n + 1)
                for t in range(KT):
                    last = pe.matmul(bank[5][:, 8:8 + NB], avg[:, :], sq[:, t, :], start=(t == 0), stop=(t == KT - 1))
                last.then_inc(var_ps, 1)

            def up(f, s):
                n, at = STEPS * f + s, (STEPS + 1) * f + s
                pe.wait_ge(th_done, at + 1)
                for t in range(KT):
                    last = pe.matmul(bank[5][:, 8:8 + NB], avg[:, :], th[:, at, t, :], start=(t == 0), stop=(t == KT - 1))
                last.then_inc(mean_ps, 1)
                pe.wait_ge(t_lo, n + 1)
                if n == 0:
                    pe.wait_ge(w_lo, 1)
                    pe.wait_ge(gb_parts, 5)
                width = 3 * TC if n == 0 else 3 * NB
                for m in range(HT):
                    if f == 0 and m == HT // 2:
                        variance(n)
                    for c in range(3):
                        for t in range(KT):
                            moving = tp[:, t, :, 0:(TC if n == 0 else NB)]
                            last = pe.matmul(bank[4][:, m * 3 * TC:m * 3 * TC + width], w_d1[:, c, t, m * P:(m + 1) * P], moving,
                                             start=(c == 0 and t == 0), stop=(c == 2 and t == KT - 1))
                last.then_inc(h_ps, 1)

            def down(f, s):
                n = STEPS * f + s
                pe.wait_ge(h_lo, n + 1)
                if n == 0:
                    pe.wait_ge(w_lo, 2)
                for m in range(KT):
                    for c in range(3):
                        for t in range(HT):
                            last = pe.matmul(bank[5][:, 16 + m * 3 * NB:16 + (m + 1) * 3 * NB], w_d2[:, c, t, m * P:(m + 1) * P],
                                             hp[:, t, :, :].rearrange("p c b -> p (c b)"),
                                             start=(c == 0 and t == 0), stop=(c == 2 and t == HT - 1))
                last.then_inc(d2_ps, 1)

            def spread_columns(f):
                pe.wait_ge(ld_bc, 16)
                at = (STEPS + 1) * f + STEPS
                pe.wait_ge(th_done, at + 1)
                for m in range(KT):
                    for t in range(KT):
                        last = pe.matmul(bank[5][:, 4 + m * NB:4 + (m + 1) * NB], w_bc[:, t, m * P:(m + 1) * P], th[:, at, t, :],
                                         start=(t == 0), stop=(t == KT - 1))
                last.then_inc(bcol_ps, 1)

            def spread_rows(f):
                pe.wait_ge(bdiag_done, 3 * (f + 1))
                for b in range(NB):
                    for t in range(KT):
                        for c in range(3):
                            last = pe.matmul(bank[4][:, b * D + t * P:b * D + (t + 1) * P], onesb[:, :], bdiag[:, c, t * NB + b, :],
                                             start=(c == 0), stop=(c == 2))
                last.then_inc(bc_ps, 1)

            thought_in(0)
            thought_agg(0)
            for s in range(STEPS):
                up(0, s)
                if s == 1:
                    turn(0, range(0, 2))
                elif s >= 2:
                    gates(0, 2 * s - 4)
                down(0, s)
                if s == 1:
                    turn(0, range(2, PAIRS))
                elif s >= 2:
                    gates(0, 2 * s - 3)
            spread_columns(0)
            spread_rows(0)
            turn(1, range(PAIRS))
            pe.wait_ge(ld_in, 16)
            pe.wait_ge(xnT_done, 2 * PAIRS)
            base = DI + CD
            for i in range(NT):
                for t in range(KT):
                    last = pe.matmul(bank[5][:, i * NH:(i + 1) * NH], xnT[:, t, i * P:(i + 1) * P], w_in[:, t, base:base + NH],
                                     start=(t == 0), stop=(t == KT - 1))
            last.then_inc(dt_ps, 1)

            def project(n):
                b, ct = divmod(n, CT)
                if n < 3:
                    pe.wait_ge(sg_done, PAIRS)
                    pe.wait_ge(ob_done, NT)
                else:
                    pe.wait_ge(conv_done, (CW - 1) * (n - 2))
                for t in range(KT):
                    last = pe.matmul(bank[(2, 3, 4)[n % 3]], w_in[:, t, DI + ct * P:DI + (ct + 1) * P], xnT[:, t, b * L:(b + 1) * L],
                                     start=(t == 0), stop=(t == KT - 1))
                last.then_inc(proj_ps, 1)

            def gate_z(n):
                if n >= 1:
                    pe.wait_ge(sz_done, n)
                i = Z_ORDER[n]
                for t in range(KT):
                    last = pe.matmul(bank[6], xnT[:, t, i * P:(i + 1) * P], w_in[:, t, 0:DI],
                                     start=(t == 0), stop=(t == KT - 1))
                last.then_inc(z_ps, 1)

            def sums():
                pe.wait_ge(dA_done, 1)
                moving = dA[:, :, :].rearrange("p t h -> p (t h)")
                pe.matmul(bank[5][:, 0:N64], tri[:, :], moving, start=True, stop=True)
                pe.matmul(bank[5][:, N64:2 * N64], ones[:, :], moving, start=True, stop=True).then_inc(cs_ps, 1)

            def turn_x(i):
                pe.wait_ge(xc_done, CT * (i // NC + 1) - 1)
                if i >= 2:
                    pe.wait_ge(xt_done, i - 1)
                for t in range(XT):
                    last = pe.transpose(bank[i % 2][:, t * P:(t + 1) * P], xc[:, t, i * P:(i + 1) * P], ident[:, :])
                last.then_inc(xt_ps, 1)
                if i in STATES:
                    n = STATES.index(i)
                    if n == 0:
                        pe.wait_ge(exps_done, 3)
                    else:
                        pe.wait_ge(Bt_done, n)
                    pe.transpose(bank[5][:, 0:P], xc[:, XT, i * P:(i + 1) * P], ident[:, :]).then_inc(Bt_ps, 1)

            def new_state(n):
                pe.wait_ge(xw_done, n + 1)
                pe.wait_ge(Bt_done, n + 1)
                if n >= 1:
                    pe.wait_ge(S_done, n)
                pe.matmul(bank[7], Bt[:, n % 2, :], xw[:, n % 2, :], start=True, stop=True).then_inc(st_ps, 1)

            for n in range(NB * CT):
                project(n)
                if n == 2:
                    sums()
                if n in Z_WITH:
                    gate_z(Z_WITH[n])
                if n in TURN_WITH:
                    turn_x(TURN_WITH[n])
                if n in STATE_WITH:
                    new_state(STATE_WITH[n])
            gate_z(NT - 2)
            turn_x(NC)
            gate_z(NT - 1)
            for i in range(NC + 1, NT):
                turn_x(i)
                new_state(STATES.index(i - 1))

            def segments(p):
                pe.wait_ge(R_done, p + 1)
                if p >= 1:
                    pe.wait_ge(E_done, p)
                for j in range(2):
                    last = pe.matmul(bank[2 + j], after[:, :], R[:, p % 2, :, :].rearrange("p h l -> p (h l)")[:, j * 512:(j + 1) * 512],
                                     start=True, stop=True)
                last.then_inc(seg_ready, 1)

            def b_by_c(p):
                tok = slice(ORDER[p] * P, (ORDER[p] + 1) * P)
                if p == 0:
                    pe.wait_ge(xt_done, NT)
                elif p >= 4:
                    pe.wait_ge(sg2_done, p - 3)
                elif p == 3:
                    pe.wait_ge(x2_done, 1)
                else:
                    pe.wait_ge(GT_done, p)
                pe.matmul(bank[1][:, 0:P], xc[:, XT, tok], xc[:, XT + 1, tok], start=True, stop=True).then_inc(G_ps, 1)

            def from_state(p):
                i = ORDER[p]
                if i % NC > 0:
                    pe.wait_ge(S_done, STATES.index(i - 1) + 1)
                    if offs(p) >= 1:
                        pe.wait_ge(yo_done, offs(p))
                    else:
                        pe.wait_ge(S_done, len(STATES))
                    pe.matmul(bank[7], xc[:, XT + 1, i * P:(i + 1) * P], state(i - 1), start=True, stop=True).then_inc(yoff_ps, 1)

            def within_chunk(p):
                pe.wait_ge(M_done, p + 1)
                pe.wait_ge(xdt_done, p + 1)
                if p >= 1:
                    pe.wait_ge(yd_done, p)
                else:
                    pe.wait_ge(sz_done, NT)
                for h in range(NH):
                    last = pe.matmul(bank[6][:, h * HD:(h + 1) * HD], M[:, p % 2, h, :], xdt[:, p % 2, h * HD:(h + 1) * HD],
                                     start=True, stop=True)
                last.then_inc(y_ps, 1)

            def turn_u(p):
                pe.wait_ge(u_done, p + 1)
                if p >= 2:
                    pe.wait_ge(xnT2_done, p - 1)
                elif p == 1:
                    pe.wait_ge(uT_done, 1)
                for t in range(XT):
                    last = pe.transpose(bank[0][:, t * P:(t + 1) * P], yd[:, p % 2, t * P:(t + 1) * P], ident[:, :])
                last.then_inc(uT_ps, 1)

            def project_out(p):
                pe.wait_ge(uT_done, p + 1)
                pe.wait_ge(out_scaled, XT)
                if p + 2 < NT:
                    pe.wait_ge(GT_done, p + 3)
                else:
                    pe.wait_ge(sg2_done, p - 1)
                for t in range(XT):
                    last = pe.matmul(bank[1][:, 0:D], uT[:, p % 2, t, :], w_out[:, t, :],
                                     start=(t == 0), stop=(t == XT - 1))
                last.then_inc(out_ps, 1)

            def turn_xn2(p):
                i = ORDER[p]
                pe.wait_ge(xn_done, 2 * NT + p + 1)
                pe.wait_ge(uT_done, min(p + 2, NT))
                for t in range(KT):
                    last = pe.transpose(bank[0][:, t * P:(t + 1) * P], xn[:, i, t * P:(t + 1) * P], ident[:, :])
                last.then_inc(xnT2_ps, 1)

            def gate2(p):
                tok = slice(ORDER[p] * P, (ORDER[p] + 1) * P)
                pe.wait_ge(xnT2_done, p + 1)
                if p + 1 < NT:
                    pe.wait_ge(x2_done, p + 2)
                else:
                    pe.wait_ge(sg2_done, p)
                for t in range(KT):
                    pe.matmul(bank[1][:, 0:D], xnT[:, t, tok], w_gate[:, t, :], start=(t == 0), stop=False)
                pe.matmul(bank[1][:, 0:D], ones[0:1, :], row_gate_b[:, :], start=False, stop=True).then_inc(gate2_ps, 1)

            segments(0)
            b_by_c(0)
            for p in range(NT):
                if p + 1 < NT:
                    segments(p + 1)
                    b_by_c(p + 1)
                if p == THOUGHT_AT:
                    thought_in(1)
                if p in STEP_AT:
                    up(1, STEP_AT[p])
                from_state(p)
                if p >= 1:
                    turn_u(p - 1)
                if p == THOUGHT_AT:
                    thought_agg(1)
                if p in STEP_AT:
                    variance(STEPS + STEP_AT[p])
                within_chunk(p)
                if p >= 2:
                    turn_xn2(p - 2)
                if p >= 1:
                    project_out(p - 1)
                if p >= 2:
                    gate2(p - 2)
                if p in STEP_AT:
                    down(1, STEP_AT[p])
            spread_columns(1)
            turn_u(NT - 1)
            project_out(NT - 1)
            turn_xn2(NT - 2)
            gate2(NT - 2)
            spread_rows(1)
            turn_xn2(NT - 1)
            gate2(NT - 1)

        @block.vector
        def _(dve):
            def ln_stats(k, src, wait):
                tiles = LN_TILES[k]
                at = bn_before[k]
                for n, i in enumerate(tiles):
                    wait(i)
                    dve.bn_stats(bn[:, at + n, :], src(n, i)).then_inc(bn_done, 1)
                for n, i in enumerate(tiles):
                    dve.wait_ge(bn_done, at + n + 1)
                    dve.bn_aggr(mv[:, at + n, :], bn[:, at + n, :]).then_inc(ag_done, 1)
                dve.wait_ge(ag_done, bn_before[k + 1])
                dve.tensor_scalar(ve[:, at:bn_before[k + 1]], mv[:, at:bn_before[k + 1], 1], LN_EPS[k], None, ALU.add).then_inc(ve_done, 1)

            def normalise(k, n, src, dst):
                at = bn_before[k] + n
                return dve.tensor_scalar(dst, src, mv[:, at, 0:1], rstd[:, at:at + 1], ALU.subtract, ALU.mult)

            def normalise_group(k, src, dst):
                dve.wait_ge(rstd_done, k + 1)
                for n, i in enumerate(LN_TILES[k]):
                    normalise(k, n, src[:, i, :], dst[:, i, :]).then_inc(xn_done, 1)

            wide = lambda v: v.unsqueeze(2).to_broadcast([P, v.shape[1], NB])

            def left_over(n, parts):
                dve.wait_ge(w_hi, n + 1)
                if n > 0:
                    dve.wait_ge(w_lo, n)
                dve.tensor_tensor(left, raw[n], parts(0), ALU.subtract).then_inc(w_left, 1)
                dve.wait_ge(w_mid, n + 1)
                dve.tensor_tensor(parts(2), left, parts(1), ALU.subtract).then_inc(w_lo, 1)


            def columns():
                dve.wait_ge(rows_T, 1)
                dve.tensor_copy(cols[:, :], bank[5][:, 0:n_rows]).then_inc(cols_ready, 1)
                dve.wait_ge(cols_ready, 1)
                at, _ = row_at["pn_gamma"]
                both = cols[:, at:at + 2 * KT].rearrange("p (c t) -> p t c", c=2)
                dve.tensor_copy(tp[:, :, 0, NB:TC], both).then_inc(gb_parts, 1)
                dve.wait_ge(gb_parts, 1)
                dve.tensor_tensor(gb_rest[:, :, :], both, tp[:, :, 0, NB:TC], ALU.subtract).then_inc(gb_parts, 1)
                dve.wait_ge(gb_parts, 2)
                dve.tensor_copy(tp[:, :, 1, NB:TC], gb_rest[:, :, :]).then_inc(gb_parts, 1)
                dve.wait_ge(gb_parts, 3)
                dve.tensor_tensor(tp[:, :, 2, NB:TC], gb_rest[:, :, :], tp[:, :, 1, NB:TC], ALU.subtract).then_inc(gb_parts, 2)

            def thought_start(f):
                dve.wait_ge(last_ps, f + 1)
                dve.tensor_tensor(lastT[:, :, :], bank[5][:, 0:KT * NB].rearrange("p (t b) -> p t b", t=KT), wide(col("in_gamma")),
                                  ALU.mult).then_inc(last_mid, 1)
                dve.wait_ge(last_mid, f + 1)
                dve.tensor_tensor(lastg[:, :, :], lastT[:, :, :], wide(col("in_beta")), ALU.add).then_inc(last_done, 1)

            def thought_first(f):
                dve.wait_ge(agg_ps, f + 1)
                at = (STEPS + 1) * f
                dve.tensor_tensor(th[:, at, :, :], bank[5][:, 4:4 + KT * NB].rearrange("p (t b) -> p t b", t=KT), wide(col("agg_b")),
                                  ALU.add).then_inc(th_done, 1)


            def step_parts(f, s):
                n, at = STEPS * f + s, (STEPS + 1) * f + s
                now = th[:, at, :, :]
                dve.wait_ge(th_done, at + 1)
                dve.tensor_tensor(tg[:, :, :], now, wide(col("pn_gamma")), ALU.mult).then_inc(tg_done, 1)
                if n >= 1:
                    dve.wait_ge(h_ps, n)
                dve.wait_ge(tg_done, n + 1)
                dve.tensor_copy(tp[:, :, 0, 0:NB], tg[:, :, :]).then_inc(t_hi, 1)
                dve.wait_ge(t_hi, n + 1)
                dve.tensor_tensor(tr[:, :, :], tg[:, :, :], tp[:, :, 0, 0:NB], ALU.subtract).then_inc(t_left, 1)
                dve.wait_ge(t_left, n + 1)
                dve.tensor_copy(tp[:, :, 1, 0:NB], tr[:, :, :]).then_inc(t_mid, 1)
                dve.wait_ge(t_mid, n + 1)
                dve.tensor_tensor(tp[:, :, 2, 0:NB], tr[:, :, :], tp[:, :, 1, 0:NB], ALU.subtract).then_inc(t_lo, 1)

            def step_mean(f, s):
                n, at = STEPS * f + s, (STEPS + 1) * f + s
                now = th[:, at, :, :]
                dve.wait_ge(mean_ps, n + 1)
                dve.tensor_copy(mu[:, :], bank[5][:, 8:8 + NB]).then_inc(mu_done, 1)
                dve.wait_ge(mu_done, n + 1)
                dve.tensor_tensor(dc[:, :, :], now, mu[:, :].unsqueeze(1).to_broadcast([P, KT, NB]), ALU.subtract).then_inc(dc_done, 1)
                dve.wait_ge(dc_done, n + 1)
                dve.tensor_tensor(sq[:, :, :], dc[:, :, :], dc[:, :, :], ALU.mult).then_inc(sq_done, 1)
                dve.tensor_tensor(thb[:, n, :, :], now, wide(col("d2_b")), ALU.add).then_inc(thb_done, 1)
                by_mean = mu[:, :].unsqueeze(1).to_broadcast([P, HT, NB])
                if n > 0:
                    dve.tensor_tensor(mgW[:, :, :], wide(gW[:, :]), by_mean, ALU.mult).then_inc(mgW_done, 1)

            def step_variance(n):
                dve.wait_ge(var_ps, n + 1)
                dve.tensor_scalar(vs[:, :], bank[5][:, 8:8 + NB], EPS_FFN, None, ALU.add).then_inc(vs_done, 1)

            def step_hidden(n):
                by_mean = mu[:, :].unsqueeze(1).to_broadcast([P, HT, NB])
                dve.wait_ge(h_ps, n + 1)
                hidden = bank[4][:, 0:HT * 3 * TC].rearrange("p (m r) -> p m r", m=HT)
                if n == 0:
                    both = hidden[:, :, :].rearrange("p m (c j) -> p m j c", c=3)
                    dve.tensor_reduce(gW[:, :], both[:, :, NB, :], AX.X, ALU.add).then_inc(gW_done, 1)
                    dve.tensor_reduce(c1[:, :], both[:, :, NB + 1, :], AX.X, ALU.add).then_inc(c1_done, 1)
                    dve.wait_ge(gW_done, 1)
                    dve.tensor_tensor(mgW[:, :, :], wide(gW[:, :]), by_mean, ALU.mult).then_inc(mgW_done, 1)
                    dve.wait_ge(c1_done, 1)
                    dve.tensor_tensor(c1[:, :], c1[:, :], col("d1_b"), ALU.add).then_inc(c1_done, 1)
                    here = both[:, :, 0:NB, :]
                else:
                    here = hidden[:, :, 0:3 * NB].rearrange("p m (c j) -> p m j c", c=3)
                dve.tensor_reduce(hs[:, :, :], here, AX.X, ALU.add).then_inc(hs_done, 1)
                dve.wait_ge(hs_done, n + 1)
                dve.wait_ge(mgW_done, n + 1)
                dve.tensor_tensor(hc[:, :, :], hs[:, :, :], mgW[:, :, :], ALU.subtract).then_inc(hc_done, 1)
                dve.wait_ge(hc_done, n + 1)
                dve.wait_ge(rs_done, n + 1)
                dve.tensor_tensor(hr[:, :, :], hc[:, :, :], rs[:, :].unsqueeze(1).to_broadcast([P, HT, NB]), ALU.mult).then_inc(hr_done, 1)
                dve.wait_ge(hr_done, n + 1)
                dve.wait_ge(c1_done, 2)
                dve.tensor_tensor(hb[:, :, :], hr[:, :, :], wide(c1[:, :]), ALU.add).then_inc(hb_done, 1)

            def step_gelu(n):
                dve.wait_ge(gelu_done, n + 1)
                if n >= 1:
                    dve.wait_ge(d2_ps, n)
                dve.tensor_copy(hp[:, :, 0, :], hg[:, :, :]).then_inc(h_hi, 1)
                dve.wait_ge(h_hi, n + 1)
                dve.tensor_tensor(hrest[:, :, :], hg[:, :, :], hp[:, :, 0, :], ALU.subtract).then_inc(h_left, 1)
                dve.wait_ge(h_left, n + 1)
                dve.tensor_copy(hp[:, :, 1, :], hrest[:, :, :]).then_inc(h_mid, 1)
                dve.wait_ge(h_mid, n + 1)
                dve.tensor_tensor(hp[:, :, 2, :], hrest[:, :, :], hp[:, :, 1, :], ALU.subtract).then_inc(h_lo, 1)

            def step_end(f, s):
                n, at = STEPS * f + s, (STEPS + 1) * f + s
                dve.wait_ge(d2_ps, n + 1)
                dve.tensor_reduce(dsum[:, :, :], bank[5][:, 16:16 + KT * 3 * NB].rearrange("p (t c b) -> p t b c", t=KT, c=3),
                                  AX.X, ALU.add).then_inc(dsum_done, 1)
                dve.wait_ge(dsum_done, n + 1)
                dve.wait_ge(thb_done, n + 1)
                dve.tensor_tensor(th[:, at + 1, :, :], dsum[:, :, :], thb[:, n, :, :], ALU.add).then_inc(th_done, 1)


            def vector_parts(f):
                dve.wait_ge(bcol_ps, f + 1)
                dve.tensor_tensor(bcol[:, :, :], bank[5][:, 4:4 + KT * NB].rearrange("p (t b) -> p t b", t=KT), wide(col("bc_b")),
                                  ALU.add).then_inc(bcol_done, 1)
                dve.wait_ge(bcol_done, 2 * f + 1)
                dve.tensor_scalar(bcol[:, :, :], bcol[:, :, :], 0.5, None, ALU.mult).then_inc(bcol_done, 1)
                dve.wait_ge(bcol_done, 2 * f + 2)
                dve.tensor_copy(bp[:, 0, :, :], bcol[:, :, :]).then_inc(b_hi, 1)
                dve.wait_ge(b_hi, f + 1)
                dve.tensor_tensor(brest[:, :, :], bcol[:, :, :], bp[:, 0, :, :], ALU.subtract).then_inc(b_left, 1)
                dve.wait_ge(b_left, f + 1)
                dve.tensor_copy(bp[:, 1, :, :], brest[:, :, :]).then_inc(b_mid, 1)
                dve.wait_ge(b_mid, f + 1)
                dve.tensor_tensor(bp[:, 2, :, :], brest[:, :, :], bp[:, 1, :, :], ALU.subtract).then_inc(b_lo, 1)

            def vector_diagonals(f):
                dve.wait_ge(b_lo, f + 1)
                dve.wait_ge(consts16, 2)
                for c in range(3):
                    dve.tensor_tensor(bdiag[:, c, :, :], identb[:, :].unsqueeze(1).to_broadcast([P, KT * NB, P]),
                                      bp[:, c, :, :].rearrange("p t b -> p (t b)").unsqueeze(2).to_broadcast([P, KT * NB, P]),
                                      ALU.mult).then_inc(bdiag_done, 1)

            def gated(f, i, read):
                read()
                b = i // NC
                dve.scalar_tensor_tensor(out=o[:, i, :], in0=sg[:, i, :], scalar=1.0, in1=bank[4][:, b * D:(b + 1) * D],
                                         op0=ALU.add, op1=ALU.mult).then_inc(ob_done, 1)

            def out_centred(k):
                for n, i in enumerate(LN_TILES[k]):
                    dve.scalar_tensor_tensor(out=o[:, i, :], in0=o[:, i, :], scalar=mv[:, bn_before[k] + n, 0:1], in1=gam[:, :],
                                             op0=ALU.subtract, op1=ALU.mult).then_inc(og_done, 1)

            def out_added(f, h, k):
                dve.wait_ge(rstd_done, k + 1)
                for n, i in enumerate(LN_TILES[k]):
                    dve.wait_ge(og_done, NT * f + h * NT // 2 + n + 1)
                    dve.wait_ge(xb_done, h + 1 if f == 0 else 2 + h * NT // 2 + n + 1)
                    at = bn_before[k] + n
                    dve.scalar_tensor_tensor(out=x_sb[2 * f + 1][:, i, :], in0=o[:, i, :], scalar=rstd[:, at:at + 1],
                                             in1=x_sb[2 * f][:, i, :], op0=ALU.mult, op1=ALU.add).then_inc(x_done, 1)

            tiles_of = lambda t: lambda n, i: t[:, i, :]
            parts_1 = lambda c: w_d1[:, c, :, :].rearrange("p t n -> p (t n)")
            parts_2 = lambda c: w_d2[:, c, :, :].rearrange("p t n -> p (t n)")
            x = x_sb[0]
            ln_stats(0, tiles_of(x), lambda i: dve.wait_ge(ld_x, all_of(NB)))
            normalise_group(0, x, xn)
            ln_stats(1, tiles_of(xn), lambda i: dve.wait_ge(xn_done, xn_ready(0, i)))
            dve.wait_ge(rstd_done, 2)
            for b in range(NB):
                normalise(1, b, xn[:, LAST[b], :], xnn[:, b, :]).then_inc(xnn_done, 1)
            columns()
            left_over(0, parts_1)
            thought_start(0)
            thought_first(0)
            for s in range(STEPS):
                step_parts(0, s)
                step_mean(0, s)
                step_variance(s)
                if s == 0:
                    left_over(1, parts_2)
                    ln_stats(2, tiles_of(x), lambda i: dve.wait_ge(ld_x2, all_of(NB)))
                if s == 1:
                    normalise_group(2, x, xn)
                if s == 2:
                    dve.wait_ge(ld_aff, all_of(2))
                    dve.tensor_scalar(bet[:, :], bet[:, :], 0.5, None, ALU.mult).then_inc(beta_ready, 1)
                    dve.tensor_scalar(gam[:, :], gam[:, :], 0.5, None, ALU.mult).then_inc(gamma_ready, 1)
                step_hidden(s)
                step_gelu(s)
                step_end(0, s)
            vector_parts(0)
            vector_diagonals(0)
            dve.wait_ge(bc_ps, 1)
            for i in range(NT):
                gated(0, i, lambda: dve.wait_ge(sg_done, i // 2 + 1))
            for g in range(PAIRS):
                pair = slice(2 * g, 2 * g + 2)
                dve.wait_ge(ob_done, 2 * g + 2)
                dve.tensor_tensor(o[:, pair, :], o[:, pair, :], xn[:, pair, :], ALU.add).then_inc(o_done, 1)
            for h in range(2):
                ln_stats(3 + h, tiles_of(o), lambda i: dve.wait_ge(o_done, i // 2 + 1))
            dve.wait_ge(gamma_ready, 1)
            for h in range(2):
                out_centred(3 + h)
            for h in range(2):
                out_added(0, h, 3 + h)
            for h in range(2):
                ln_stats(MAMBA_LN + h, tiles_of(x_sb[1]), lambda i: dve.wait_ge(x_done, i + 1))
                if h == 0:
                    dve.wait_ge(xnT_ps, PAIRS)
            for h in range(2):
                normalise_group(MAMBA_LN + h, x_sb[1], xn)
            by_tile = lambda v: v.unsqueeze(1).to_broadcast([P, NT, NH])
            dve.wait_ge(ld_head, all_of(3))
            dve.wait_ge(dt_ps, 1)
            dve.tensor_tensor(dtv[:, :, :], bank[5][:, 0:N64].rearrange("p (t h) -> p t h", t=NT), by_tile(head_par[:, 0, :]),
                              ALU.add).then_inc(dt_v, 1)
            dve.wait_ge(dt_v, 1)
            flat = lambda v: v[:, :, :].rearrange("p t h -> p (t h)")
            dve.scalar_tensor_tensor(out=flat(dtn), in0=flat(dtv), scalar=-1.0, in1=flat(dtv), op0=ALU.mult, op1=ALU.min).then_inc(dt_n, 1)
            dve.wait_ge(dt_l, 1)
            dve.scalar_tensor_tensor(out=flat(dt), in0=flat(dtv), scalar=0.0, in1=flat(dtl), op0=ALU.max, op1=ALU.add).then_inc(dt_done, 1)
            dve.wait_ge(dt_done, 1)
            dve.wait_ge(ea_done, 1)
            dve.scalar_tensor_tensor(out=dA[:, :, :], in0=dt[:, :, :], scalar=-1.0, in1=by_tile(ea[:, :]), op0=ALU.mult,
                                     op1=ALU.mult).then_inc(dA_done, 1)

            heads = lambda v: v.rearrange("p (h q) -> p h q", h=NH)

            def convolve(n):
                b, ct = divmod(n, CT)
                dve.wait_ge(tap0_done, n + 1)
                for k in range(1, CW):
                    dst = cv[:, n % 3, k:L]
                    if k > 1:
                        dve.wait_ge(conv_done, (CW - 1) * n + k - 1)
                    dve.scalar_tensor_tensor(out=dst, in0=bank[(2, 3, 4)[n % 3]][:, 0:L - k], scalar=conv_w[:, ct, CW - 1 - k:CW - k],
                                             in1=dst, op0=ALU.mult, op1=ALU.add).then_inc(conv_done, 1)

            def sums():
                dve.wait_ge(cs_ps, 1)
                dve.tensor_copy(flat(cs), bank[5][:, 0:N64]).then_inc(cs_done, 1)
                dve.wait_ge(cs_done, 1)
                dve.tensor_tensor(flat(rest), bank[5][:, N64:2 * N64], flat(cs), ALU.subtract).then_inc(rest_done, 2)

            def evac_B(n):
                if n == 0:
                    dve.wait_ge(exps_done, 3)
                dve.wait_ge(Bt_ps, n + 1)
                if n >= 2:
                    dve.wait_ge(st_ps, n - 1)
                dve.tensor_copy(Bt[:, n % 2, :], bank[5][:, 0:P]).then_inc(Bt_done, 1)

            def advance(n):
                i = STATES[n]
                if i % NC > 0:
                    dve.wait_ge(S_done, n)
                    dve.tensor_tensor(heads(Sd[:, n % 2, :]), heads(state(i - 1)), dec[:, i, :].unsqueeze(2).to_broadcast([P, NH, HD]),
                                      ALU.mult).then_inc(Sd_done, 1)
                dve.wait_ge(st_ps, n + 1)
                if i % NC == 0:
                    dve.tensor_copy(state(i), bank[7]).then_inc(S_done, 1)
                else:
                    dve.wait_ge(Sd_done, n - i // NC)
                    dve.tensor_tensor(state(i), Sd[:, n % 2, :], bank[7], ALU.add).then_inc(S_done, 1)

            for n in range(NB * CT):
                convolve(n)
                if n == 3:
                    sums()
                if n == CT:
                    dve.wait_ge(exps_done, 2)
                    dve.tensor_tensor(flat(wd), flat(erest), flat(dt), ALU.mult).then_inc(wd_done, 1)
                if n in TURN_WITH and TURN_WITH[n] in STATES:
                    evac_B(TURN_WITH[n])
                if n in STATE_WITH:
                    advance(STATE_WITH[n])
            evac_B(NC - 1)
            for n in range(NC, len(STATES)):
                evac_B(n)
                advance(n - 1)
            advance(len(STATES) - 1)

            def masked(p):
                dve.wait_ge(G_ps, p + 1)
                if p >= 2:
                    dve.wait_ge(M_done, p - 1)
                dve.tensor_tensor(GT[:, p % 2, :], bank[1][:, 0:P], tri[:, :], ALU.mult).then_inc(GT_done, 1)

            def weights(p):
                dve.wait_ge(E_done, p + 1)
                dve.wait_ge(GT_done, p + 1)
                dve.tensor_tensor(M[:, p % 2, :, :], E[:, p % 2, :, :], GT[:, p % 2, :].unsqueeze(1).to_broadcast([P, NH, P]), ALU.mult)\
                   .then_inc(M_done, 1)

            def residual(p):
                i = ORDER[p]
                dve.wait_ge(out_ps, p + 1)
                dve.wait_ge(sr_done, p + 1)
                dve.scalar_tensor_tensor(out=x_sb[2][:, i, :], in0=bank[1][:, 0:D], scalar=sr[:, i:i + 1],
                                         in1=x_sb[1][:, i, :], op0=ALU.mult, op1=ALU.add).then_inc(x2_done, 1)
                ln_stats(IN2[p], tiles_of(x_sb[2]), lambda i: dve.wait_ge(x2_done, p + 1))

            def next_xn(p):
                i = ORDER[p]
                normalise_group(IN2[p], x_sb[2], xn)
                if p in LAST2:
                    ln_stats(LAST2[p], tiles_of(xn), lambda i: dve.wait_ge(xn_done, 2 * NT + p + 1))
                    dve.wait_ge(rstd_done, LAST2[p] + 1)
                    normalise(LAST2[p], 0, xn[:, i, :], xnn[:, p, :]).then_inc(xnn_done, 1)

            def gated_2(ps):
                for p in ps:
                    gated(1, ORDER[p], lambda: dve.wait_ge(sg2_done, p + 1))
                for p in ps:
                    i = ORDER[p]
                    dve.wait_ge(ob_done, NT + p + 1)
                    dve.tensor_tensor(o[:, i, :], o[:, i, :], xn[:, i, :], ALU.add).then_inc(o_done, 1)

            masked(0)
            weights(0)
            for p in range(NT):
                i, j = ORDER[p], p % 2
                step = STEP_AT.get(p)
                if step is not None:
                    step_parts(1, step)
                if p == THOUGHT_AT:
                    thought_start(1)
                if p + 1 < NT:
                    masked(p + 1)
                if step is not None:
                    step_mean(1, step)
                if p >= 2 and p - 1 != NB:
                    next_xn(p - 2)
                if i % NC > 0:
                    dve.wait_ge(yoff_ps, offs(p) + 1)
                    if offs(p) == 0:
                        dve.wait_ge(S_done, len(STATES))
                    elif offs(p) >= 2:
                        dve.wait_ge(xo_done, offs(p) - 1)
                    dve.tensor_tensor(heads(yo[:, j, :]), heads(bank[7]), ecs[:, i, :].unsqueeze(2).to_broadcast([P, NH, HD]), ALU.mult)\
                       .then_inc(yo_done, 1)
                if step is not None:
                    step_variance(STEPS + step)
                if p + 1 < NT:
                    weights(p + 1)
                if p == THOUGHT_AT:
                    thought_first(1)
                if step is not None:
                    step_hidden(STEPS + step)
                dve.wait_ge(y_ps, p + 1)
                if i % NC > 0:
                    dve.wait_ge(xo_done, offs(p) + 1)
                else:
                    dve.wait_ge(xD_done, p + 1)
                if p >= 2:
                    dve.wait_ge(uT_ps, p - 1)
                    dve.wait_ge(ss_done, p - 1)
                dve.tensor_tensor(yd[:, j, :], bank[6], xD[:, j, :], ALU.add).then_inc(yd_done, 1)
                if step is not None:
                    step_gelu(STEPS + step)
                dve.wait_ge(yd_done, p + 1)
                dve.wait_ge(sz_done, Z_ORDER.index(i) + 1)
                dve.tensor_tensor(yd[:, j, :], yd[:, j, :], sz[:, i, :], ALU.mult).then_inc(u_done, 1)
                if p >= 1:
                    residual(p - 1)
                if p == NB:
                    next_xn(p - 1)
                dve.wait_ge(ss_done, p + 1)
                dve.tensor_scalar(se[:, i:i + 1], ss[:, i:i + 1], 1.0 / DI, EPS_LN, ALU.mult, ALU.add).then_inc(se_done, 1)
                if step is not None:
                    step_end(1, step)
            next_xn(NT - 2)
            vector_parts(1)
            vector_diagonals(1)
            residual(NT - 1)
            next_xn(NT - 1)
            dve.wait_ge(bc_ps, 2)
            gated_2(range(NT // 2))
            ln_stats(OUT2, tiles_of(o), lambda i: dve.wait_ge(o_done, PAIRS + ORDER.index(i) + 1))
            out_centred(OUT2)
            gated_2(range(NT // 2, NT))
            out_added(1, 0, OUT2)
            ln_stats(OUT2 + 1, tiles_of(o), lambda i: dve.wait_ge(o_done, PAIRS + ORDER.index(i) + 1))
            out_centred(OUT2 + 1)
            out_added(1, 1, OUT2 + 1)


_SHORT = {
    "u": "L0_attn_u", "in_proj": "L0_attn_in_proj_kernel", "conv_w": "L0_attn_conv1d_weight", "conv_b": "L0_attn_conv1d_bias",
    "dt_bias": "L0_attn_dt_bias", "A_log": "L0_attn_A_log", "D": "L0_attn_D", "norm_w": "L0_attn_norm_weight",
    "out_proj": "L0_attn_out_proj_kernel", "in_gamma": "L0_ffn_in_gamma", "in_beta": "L0_ffn_in_beta", "agg_w": "L0_ffn_agg_w",
    "agg_b": "L0_ffn_agg_b", "pn_gamma": "L0_ffn_pn_gamma", "pn_beta": "L0_ffn_pn_beta", "d1_w": "L0_ffn_d1_w",
    "d1_b": "L0_ffn_d1_b", "d2_w": "L0_ffn_d2_w", "d2_b": "L0_ffn_d2_b", "bc_w": "L0_ffn_bc_w", "bc_b": "L0_ffn_bc_b",
    "gate_w": "L0_ffn_gate_w", "gate_b": "L0_ffn_gate_b", "out_gamma": "L0_ffn_out_gamma", "out_beta": "L0_ffn_out_beta",
}


def kernel(**inputs):
    import numpy as _np
    import concourse.bacc as _bacc
    from concourse import mybir as _mybir
    from concourse.bass_utils import run_bass_kernel_spmd as _run

    nc = _bacc.Bacc("TRN2", target_bir_lowering=False, num_devices=1)
    arrays, args = {}, {}
    for short, name in _SHORT.items():
        v = _np.ascontiguousarray(inputs[name])
        arrays[f"in_{name}"] = v
        args[short] = nc.dram_tensor(f"in_{name}", v.shape, _mybir.dt.from_np(v.dtype), kind="ExternalInput").ap()
    shape = arrays["in_L0_attn_u"].shape
    result = nc.dram_tensor("result", shape, _mybir.dt.float32, kind="ExternalOutput").ap()
    macaron_program(nc, args, result)
    r = _run(nc, [arrays], core_ids=[0])
    return r.results[0]["result"]
```

```python
from contextlib import ExitStack

import concourse.bass as bass
from concourse import mybir

F32 = mybir.dt.float32
BF16 = mybir.dt.bfloat16
F32R = mybir.dt.float32r
AX = mybir.AxisListType
ALU = mybir.AluOpType
ACT = mybir.ActivationFunctionType

P = 128


def macaron_program(nc: bass.Bass, a, out):
    NB, L, D = a["u"].shape
    KT = D // P
    NT = NB * L // P
    NC = L // P
    DI, CW = a["out_proj"].shape[0], a["conv_w"].shape[1]
    NH = a["D"].shape[0]
    HD = DI // NH
    CD = a["conv_w"].shape[0]
    CT = CD // P
    XT = DI // P
    H = a["d1_w"].shape[1]
    HT = H // P
    STEPS = 4
    PAIRS = NT // 2
    LAST = [NC * (b + 1) - 1 for b in range(NB)]
    ORDER = LAST + [i for i in range(NT) if i not in LAST]
    EPS_LN, EPS_FFN = 1e-5, 1e-6

    with ExitStack() as ctx:
        def sb(name, shape, dt=F32):
            return ctx.enter_context(nc.sbuf_tensor(name, shape, dt))

        def sem(name):
            return ctx.enter_context(nc.semaphore(name))

        banks = [ctx.enter_context(nc.psum_tensor(f"bank{i}", [P, 512], F32)) for i in (0, 1)]
        seg_ps = ctx.enter_context(nc.psum_tensor("seg_ps", [P, 1024], F32))
        banks += [seg_ps[:, 0:512], seg_ps[:, 512:1024]]
        banks += [ctx.enter_context(nc.psum_tensor(f"bank{i}", [P, 512], F32)) for i in (4, 5, 6, 7)]
        bank = [x[:, :] for x in banks]

        x_sb = [sb(f"x{n}", [P, NT, D]) for n in range(3)]
        x_sb.append(x_sb[0])
        xn = sb("xn", [P, NT, D])
        with ExitStack() as in_proj_only:
            xnT = in_proj_only.enter_context(nc.sbuf_tensor("xnT", [P, 2, KT, NT * P], F32R))
        xnT2 = sb("xnT2", [P, 2, KT, P])
        th_rep = sb("th_rep", [P, KT, NB, P])
        xD = sb("xD", [P, 2, DI])
        S_more = sb("S_more", [P, 2, DI])
        yd = sb("yd", [P, 2, DI])
        ident = sb("ident", [P, P])
        ones = sb("ones", [P, P])
        avg = sb("avg", [P, P])
        tri = sb("tri", [P, P])
        after_r = sb("after_r", [P, P], F32R)
        ones_r = sb("ones_r", [2, P], F32R)
        mhalf = sb("mhalf", [P, 1])
        half_row = sb("half_row", [1, P])

        NI = a["in_proj"].shape[1]
        w_in = sb("w_in", [P, 2, KT, NI], F32R)
        w_out = sb("w_out", [P, XT, D])
        w_gate = sb("w_gate", [P, KT, D])
        w_agg = sb("w_agg", [P, KT, D])
        w_bc = sb("w_bc", [P, KT, D])
        w_d1 = sb("w_d1", [P, 3, KT, H], BF16)
        w_d2 = sb("w_d2", [P, 3, HT, D], BF16)
        conv_w = sb("conv_w", [P, CT, CW])
        gate_b_parts = sb("gate_b_parts", [2, D], F32R)
        gam = sb("gam", [P, D])
        bet = sb("bet", [P, D])
        head_par = sb("head_par", [P, 3, NH])
        ROWS = [("in_gamma", KT), ("in_beta", KT), ("agg_b", KT), ("pn_gamma", KT), ("pn_beta", KT),
                ("d2_b", KT), ("d1_b", HT), ("norm_w", XT), ("conv_b", CT)]
        row_at, n_rows = {}, 0
        for name, n in ROWS:
            row_at[name] = (n_rows, n)
            n_rows += n
        rows = sb("rows", [n_rows, P])
        cols = sb("cols", [P, n_rows])

        def col(name):
            at, n = row_at[name]
            return cols[:, at:at + n]

        OTHERS = [i for i in range(NT) if i not in LAST]
        PAIR = [[2 * g, 2 * g + 1] for g in range(PAIRS)]
        LN = [("in", LAST, EPS_LN), ("last", LAST, EPS_FFN), ("in", OTHERS, EPS_LN)]
        OUT1, MAMBA = {}, {}
        for kind, g in (("out", 0), ("out", 1), ("mamba", 0), ("out", 2), ("mamba", 1), ("out", 3), ("mamba", 2), ("mamba", 3)):
            (OUT1 if kind == "out" else MAMBA)[g] = len(LN)
            LN.append((kind, PAIR[g], EPS_FFN if kind == "out" else EPS_LN))
        IN2, LAST2 = {}, {}
        for p, i in enumerate(ORDER):
            IN2[p] = len(LN)
            LN.append(("in", [i], EPS_LN))
            if i in LAST:
                LAST2[p] = len(LN)
                LN.append(("last", [i], EPS_FFN))
        OUT2 = len(LN)
        LN += [("out", ORDER[2 * g:2 * g + 2], EPS_FFN) for g in range(PAIRS)]
        LN_TILES = [g[1] for g in LN]
        LN_EPS = [g[2] for g in LN]
        bn_before = [sum(len(t) for t in LN_TILES[:k]) for k in range(len(LN_TILES) + 1)]
        bn = sb("bn", [P, bn_before[-1], 6])
        mv = sb("mv", [P, bn_before[-1], 2])
        ve = sb("ve", [P, bn_before[-1]])
        rstd = sb("rstd", [P, bn_before[-1]])
        nb = sb("nb", [P, NT])

        xnn = sb("xnn", [P, NB, D])
        sz = sb("sz", [P, NT, DI])
        sg, o = sz[:, :, 0:D], sz[:, :, D:2 * D]
        lastT = sb("lastT", [P, KT, NB])
        lastg = sb("lastg", [P, KT, NB])
        th = sb("th", [P, 2 * (STEPS + 1), KT, NB])
        thb = sb("thb", [P, 2 * STEPS, KT, NB])
        tg = sb("tg", [P, KT, NB])
        tr = sb("tr", [P, KT, NB])
        TC = NB + 2
        tp = sb("tp", [P, KT, 3, TC], BF16)
        gb_rest = sb("gb_rest", [P, KT, 2])
        hp = sb("hp", [P, HT, 3, NB], BF16)
        hrest = sb("hrest", [P, HT, NB])
        mu = sb("mu", [P, 2, NB])
        gW = sb("gW", [P, HT])
        mgW = sb("mgW", [P, HT, NB])
        hs = sb("hs", [P, HT, NB])
        hc = sb("hc", [P, HT, NB])
        dsum = sb("dsum", [P, KT, NB])
        row_bc_b = sb("row_bc_b", [1, NB, D])
        dcsq = sb("dcsq", [P, KT, 2, NB])
        dc, sq = dcsq[:, :, 0, :], dcsq[:, :, 1, :]
        dmean = sb("dmean", [P, NB])
        m2 = sb("m2", [P, NB])
        vs = sb("vs", [P, NB])
        rs = sb("rs", [P, NB])
        hb = sb("hb", [P, HT, NB])
        hg = sb("hg", [P, HT, NB])
        c1 = sb("c1", [P, HT])

        cv = sb("cv", [P, 3, L])
        flat_cv = cv[:, :, :].rearrange("p t n -> p (t n)")
        uT = flat_cv[:, 0:2 * DI].rearrange("p (s t n) -> p s t n", s=2, n=P)
        usq = flat_cv[:, 2 * DI:3 * DI]
        xc = sb("xc", [P, CT, NB * L])
        flat_xc = xc[:, :, :].rearrange("p t n -> p (t n)")
        raw = [flat_xc[:, q * KT * H // 2:(q + 1) * KT * H // 2] for q in range(4)]

        xnT1 = flat_xc[:, 2 * KT * H:2 * KT * H + KT * NT * P].rearrange("p (t n) -> p t n", t=KT)

        def part(q, c):
            w = (w_d1, w_d2)[q // 2][:, c, :, :].rearrange("p t n -> p (t n)")
            n = KT * H // 2
            return w[:, q % 2 * n:(q % 2 + 1) * n]

        N64 = NT * NH
        dtv = sb("dtv", [P, NT, NH])
        dtn = sb("dtn", [P, NT, NH])
        dte = sb("dte", [P, NT, NH])
        dtl = sb("dtl", [P, NT, NH])
        dt = sb("dt", [P, NT, NH])
        ea = sb("ea", [P, NH])
        dA = sb("dA", [P, NT, NH])
        dA_parts = sb("dA_parts", [P, 2, NT, NH], F32R)
        cs = sb("cs", [P, NT, NH])
        tot = dte
        ecs = sb("ecs", [P, NT, NH])
        dec = sb("dec", [P, NT, NH])
        rest, erest = dtn, dtl
        wd = sb("wd", [P, NT, NH])
        R = sb("R", [P, 2, NH, P], F32R)
        R_lo = w_in[:, :, :, :].rearrange("p c t n -> p (c t n)")[:, 0:2 * NH * P].rearrange("p (j h l) -> p j h l", j=2, h=NH)
        E_yo = sb("E_yo", [P, 2 * NH * P + 2 * DI])
        E = E_yo[:, 0:2 * NH * P].rearrange("p (j h l) -> p j h l", j=2, h=NH)
        yo = E_yo[:, 2 * NH * P:].rearrange("p (j n) -> p j n", j=2)
        raw_in = E_yo[:, 0:KT * NI].rearrange("p (t n) -> p t n", t=KT)
        M = E
        GT = sb("GT", [P, 2, P])
        Bt = sb("Bt", [P, 2, P])
        after = GT[:, 0, :]
        rows_gate_b = Bt[0:2, :, :].rearrange("o a p -> o (a p)")
        xt = sb("xt", [P, NT, DI])
        xw = sb("xw", [P, 2, DI])
        xdt = xw
        S_first = x_sb[0][:, :, :].rearrange("p t n -> p (t n)").rearrange("p (s n) -> p s n", n=DI)
        Sd = yo
        ss = sb("ss", [P, NT])
        se = sb("se", [P, NT])
        sr = sb("sr", [P, NT])

        ld_x, ld_x2, ld_rows, ld_agg, ld_gate, ld_bc, ld_aff, ld_head, ld_in, ld_conv, ld_out = map(
            sem, "ld_x ld_x2 ld_rows ld_agg ld_gate ld_bc ld_aff ld_head ld_in ld_conv ld_out".split())
        ld_d = [sem(n) for n in ("ld_d1_first", "ld_d1_second", "ld_d2_first", "ld_d2_second")]
        consts_zeroed, consts_done, rows_T, cols_ready, gamma_ready, beta_ready, out_scaled = map(
            sem, "consts_zeroed consts_done rows_T cols_ready gamma_ready beta_ready out_scaled".split())
        bn_done, ag_done, ve_done, rstd_done, nb_done, xn_last, xn_others, xn_mamba, xn2_done, xnn_done = map(
            sem, "bn_done ag_done ve_done rstd_done nb_done xn_last xn_others xn_mamba xn2_done xnn_done".split())
        xnT_ps, xnT_done, gate_ps, sg_done = map(sem, "xnT_ps xnT_done gate_ps sg_done".split())
        w_in_hi, w_in_lo, xnT_hi, xnT_lo = map(sem, "w_in_hi w_in_lo xnT_hi xnT_lo".split())
        xnT2_ps, xnT2_done, gate2_ps, sg2_done = map(sem, "xnT2_ps xnT2_done gate2_ps sg2_done".split())
        w_hi, w_left, w_mid, w_lo, gb_parts = map(sem, "w_hi w_left w_mid w_lo gb_parts".split())
        last_ps, last_mid, last_done, agg_ps, th_done = map(
            sem, "last_ps last_mid last_done agg_ps th_done".split())
        tg_done, t_hi, t_left, t_mid, t_lo, mean_ps, mu_done, dmean_done, m2_done, dc_done, sq_done, var_ps, vs_done, rs_done = map(
            sem, "tg_done t_hi t_left t_mid t_lo mean_ps mu_done dmean_done m2_done dc_done sq_done var_ps vs_done rs_done".split())
        gW_done, c1_done, mgW_done, h_ps, hs_done, hc_done, hb_done, gelu_done, h_hi, h_left, h_mid, h_lo = map(
            sem, "gW_done c1_done mgW_done h_ps hs_done hc_done hb_done gelu_done h_hi h_left h_mid h_lo".split())
        d2_ps, thb_done, dsum_done, rep_done, bc_ps = map(
            sem, "d2_ps thb_done dsum_done rep_done bc_ps".split())
        ob_done, o_done, og_done, xb_done, x_done = map(sem, "ob_done o_done og_done xb_done x_done".split())
        dt_ps, dt_v, dt_n, dt_e, dt_l, dt_done, ea_done, dA_done, cs_ps, cs_done, rest_done, exps_done, wd_done = map(
            sem, "dt_ps dt_v dt_n dt_e dt_l dt_done ea_done dA_done cs_ps cs_done rest_done exps_done wd_done".split())
        proj_ps, tap0_done, conv_done, xc_done, z_ps, sz_done = map(
            sem, "proj_ps tap0_done conv_done xc_done z_ps sz_done".split())
        ones_r_done, gate_b_done = map(sem, "ones_r_done gate_b_done".split())
        after_done, dA_hi, dA_lo, R_lo_first, R_lo_done = map(sem, "after_done dA_hi dA_lo R_lo_first R_lo_done".split())
        R_done, seg_ready, E_done, M_done, G_ps, GT_done, Bt_ps, Bt_done = map(
            sem, "R_done seg_ready E_done M_done G_ps GT_done Bt_ps Bt_done".split())
        xt_ps, xt_done, xdt_done, xw_done, xD_done, st_ps, Sd_done, S_done = map(
            sem, "xt_ps xt_done xdt_done xw_done xD_done st_ps Sd_done S_done".split())
        y_ps, yoff_ps, yo_done, yd_done, xo_done, u_done, ss_done, se_done, sr_done = map(
            sem, "y_ps yoff_ps yo_done yd_done xo_done u_done ss_done se_done sr_done".split())
        uT_ps, uT_done, out_ps, x2_done, stored = map(
            sem, "uT_ps uT_done out_ps x2_done stored".split())

        block = ctx.enter_context(nc.Block())
        x_tiles = a["u"].rearrange("b (c p) d -> p (b c) d", p=P)
        out_tiles = out.rearrange("b (c p) d -> p (b c) d", p=P)

        def as_row(v):
            return v.rearrange("(o n) -> o n", o=1)

        def every_partition(v):
            return as_row(v).to_broadcast([P, v.shape[0]])

        def all_of(n):
            return 16 * n

        STATES = [i for i in range(NT) if i % NC < NC - 1]
        Z_WITH = {2: 0, 3: 1, 5: 2, 6: 3, 8: 4, 9: 5, 10: 6, 11: 7}
        DT_WITH = {1 + n: (2 * n, 2 * n + 1) for n in range(NT // 2)}
        TURN_WITH = {CT + 2 + i: i for i in range(NC)}
        z_bank = lambda n: 6 + n % 2
        Z_ORDER = ORDER

        def state(i):
            n = STATES.index(i)
            return S_first[:, n, :] if n < NT // 2 else S_more[:, n - NT // 2, :]

        def offs(p):
            return sum(i % NC > 0 for i in ORDER[:p])

        THOUGHT_AT = NB + 1
        STEP_AT = {THOUGHT_AT + 1 + s: s for s in range(STEPS)}

        @block.sync
        def _(sp):
            for i in LAST:
                sp.dma_start(x_sb[0][:, i, :], x_tiles[:, i, :]).then_inc(ld_x, 16)
            for t in range(KT):
                sp.dma_start(raw[t], a["d1_w"][t * P:(t + 1) * P, :]).then_inc(ld_d[t], 16)
            for name, n in ROWS[0::2]:
                at, _ = row_at[name]
                sp.dma_start(rows[at:at + n, :], a[name].rearrange("(t p) -> t p", p=P)).then_inc(ld_rows, 16)
            sp.dma_start(w_agg[:, :, :], a["agg_w"].rearrange("(t p) n -> p t n", p=P)).then_inc(ld_agg, 16)
            for b in range(NB):
                sp.dma_start(x_sb[0][:, NC * b:LAST[b], :], x_tiles[:, NC * b:LAST[b], :]).then_inc(ld_x2, 16)
            for h in range(2):
                rows_of = a["d2_w"][h * H // 2:(h + 1) * H // 2, :]
                sp.dma_start(raw[2 + h].rearrange("p (t n) -> p t n", n=D), rows_of.rearrange("(t p) n -> p t n", p=P)).then_inc(ld_d[2 + h], 16)
            sp.dma_start(rows_gate_b, as_row(a["gate_b"]).to_broadcast([2, D])).then_inc(ld_gate, 16)
            sp.dma_start(gam[:, :], every_partition(a["out_gamma"])).then_inc(ld_aff, 16)
            sp.dma_start(bet[:, :], every_partition(a["out_beta"])).then_inc(ld_aff, 16)
            for n, name in enumerate(("dt_bias", "A_log", "D")):
                sp.dma_start(head_par[:, n, :], every_partition(a[name])).then_inc(ld_head, 16)
            sp.dma_start(conv_w[:, :, :], a["conv_w"].rearrange("(t p) k -> p t k", p=P)).then_inc(ld_conv, 16)
            sp.dma_start(w_gate[:, :, :], a["gate_w"].rearrange("(t p) n -> p t n", p=P)).then_inc(ld_gate, 16)
            for b in range(NB):
                sp.dma_start(row_bc_b[:, b, :], as_row(a["bc_b"])).then_inc(ld_bc, 16)
            sp.dma_start(w_bc[:, :, :], a["bc_w"].rearrange("(t p) n -> p t n", p=P)).then_inc(ld_bc, 16)
            sp.dma_start(raw_in, a["in_proj"].rearrange("(t p) n -> p t n", p=P)).then_inc(ld_in, 16)
            sp.dma_start(w_out[:, :, :], a["out_proj"].rearrange("(t p) n -> p t n", p=P)).then_inc(ld_out, 16)
            for p, i in enumerate(ORDER):
                sp.wait_ge(x_done, NT + p + 1)
                sp.dma_start(out_tiles[:, i, :], x_sb[3][:, i, :]).then_inc(stored, 16)
            sp.wait_ge(stored, all_of(NT))

        @block.gpsimd
        def _(pool):
            for t, v in ((ident, 0.0), (ones, 1.0), (avg, 1.0 / D), (tri, 1.0), (after, 1.0), (mhalf, -0.5), (half_row, 0.5)):
                pool.memset(t[:, :], v).then_inc(consts_zeroed, 1)
            pool.wait_ge(consts_zeroed, 7)
            pool.affine_select(out=ident[:, :], in_=ident[:, :], compare_op=ALU.not_equal, fill=1.0, base=0,
                               pattern=[[-1, P]], channel_multiplier=1).then_inc(consts_done, 1)
            pool.affine_select(out=tri[:, :], in_=tri[:, :], compare_op=ALU.is_ge, fill=0.0, base=0,
                               pattern=[[1, P]], channel_multiplier=-1).then_inc(consts_done, 1)
            pool.affine_select(out=after[:, :], in_=after[:, :], compare_op=ALU.is_gt, fill=0.0, base=0,
                               pattern=[[-1, P]], channel_multiplier=1).then_inc(consts_done, 1)

            def inv_root(dst, src, n):
                return pool.tensor_tensor(dst, src, mhalf[:, 0:1].to_broadcast([P, n]), ALU.pow)

            def ln_rstd(k):
                pool.wait_ge(ve_done, k + 1)
                n = slice(bn_before[k], bn_before[k + 1])
                inv_root(rstd[:, n], ve[:, n], len(LN_TILES[k])).then_inc(rstd_done, 1)

            def thought_rstd(n):
                pool.wait_ge(vs_done, n + 1)
                inv_root(rs[:, :], vs[:, :], NB).then_inc(rs_done, 1)

            def add_beta(x, part):
                pool.wait_ge(beta_ready, 1)
                pool.tensor_tensor(x[:, part, :], x[:, part, :],
                                   bet[:, :].unsqueeze(1).to_broadcast([P, part.stop - part.start, D]), ALU.add).then_inc(xb_done, 1)

            pool.wait_ge(consts_done, 3)
            ln_rstd(0)
            ln_rstd(1)
            def low_in(t):
                pool.wait_ge(w_in_hi, t + 1)
                pool.tensor_tensor(w_in[:, 1, t, :], raw_in[:, t, :], w_in[:, 0, t, :].bitcast(F32), ALU.subtract).then_inc(w_in_lo, 1)

            for s in range(STEPS):
                thought_rstd(s)
                if s == 1:
                    low_in(0)
                if s == 3:
                    low_in(1)
                if s == 0:
                    ln_rstd(2)
                if s == 2:
                    pool.wait_ge(xn_others, len(OTHERS))
                    for g in range(PAIRS):
                        add_beta(x_sb[0], slice(2 * g, 2 * g + 2))

            def add_xn(g):
                pair = slice(2 * g, 2 * g + 2)
                pool.wait_ge(ob_done, 2 * g + 2)
                pool.tensor_tensor(o[:, pair, :], o[:, pair, :], xn[:, pair, :], ALU.add).then_inc(o_done, 1)

            add_xn(0)
            add_xn(1)
            ln_rstd(OUT1[0])
            add_xn(2)
            ln_rstd(OUT1[1])
            ln_rstd(MAMBA[0])
            add_xn(3)
            ln_rstd(OUT1[2])
            ln_rstd(MAMBA[1])
            ln_rstd(OUT1[3])
            ln_rstd(MAMBA[2])
            ln_rstd(MAMBA[3])

            def seg_moving(p):
                if p >= 2:
                    pool.wait_ge(seg_ready, p - 1)
                else:
                    pool.wait_ge(w_in_lo, KT)
                pool.tensor_tensor(R[:, p % 2, :, :], dA_parts[:, 0, ORDER[p], :].bitcast(F32).unsqueeze(2).to_broadcast([P, NH, P]),
                                   tri[:, :].unsqueeze(1).to_broadcast([P, NH, P]), ALU.mult).then_inc(R_done, 1)

            def seg_moving_lo(p):
                pool.wait_ge(z_ps, NT)
                pool.wait_ge(dA_lo, 1)
                pool.tensor_tensor(R_lo[:, p, :, :], dA_parts[:, 1, ORDER[p], :].bitcast(F32).unsqueeze(2).to_broadcast([P, NH, P]),
                                   tri[:, :].unsqueeze(1).to_broadcast([P, NH, P]), ALU.mult).then_inc(R_lo_first, 1)

            def per_head(dst, src, w):
                return pool.tensor_tensor(dst.rearrange("p (h q) -> p h q", h=NH), src.rearrange("p (h q) -> p h q", h=NH),
                                          w.unsqueeze(2).to_broadcast([P, NH, HD]), ALU.mult)

            def x_dt(p):
                i = ORDER[p]
                pool.wait_ge(xt_done, i + 1)
                if p >= 2:
                    pool.wait_ge(y_ps, p - 1)
                else:
                    pool.wait_ge(st_ps, len(STATES))
                per_head(xdt[:, p % 2, :], xt[:, i, :], dt[:, i, :]).then_inc(xdt_done, 1)

            def x_D(p):
                if p >= 2:
                    pool.wait_ge(yd_done, p - 1)
                per_head(xD[:, p % 2, :], xt[:, ORDER[p], :], head_par[:, 2, :]).then_inc(xD_done, 1)

            pool.wait_ge(ld_out, 16)
            pool.wait_ge(cols_ready, 1)
            for t in range(XT):
                pool.tensor_scalar(w_out[:, t, :], w_out[:, t, :], col("norm_w")[:, t:t + 1], None, ALU.mult).then_inc(out_scaled, 1)
            pool.wait_ge(dA_hi, 1)
            seg_moving(0)
            seg_moving(1)
            pool.wait_ge(wd_done, 1)
            for n, i in enumerate(STATES):
                pool.wait_ge(xt_done, i + 1)
                if n >= 2:
                    pool.wait_ge(st_ps, n - 1)
                per_head(xw[:, n % 2, :], xt[:, i, :], wd[:, i, :]).then_inc(xw_done, 1)
                if n == 1:
                    seg_moving_lo(0)
            seg_moving_lo(1)
            x_dt(0)
            x_D(0)
            seg_moving(2)
            for p in range(NT):
                if p in STEP_AT:
                    thought_rstd(STEPS + STEP_AT[p])
                if ORDER[p] % NC > 0:
                    pool.wait_ge(yo_done, offs(p) + 1)
                    pool.wait_ge(xD_done, p + 1)
                    pool.tensor_tensor(xD[:, p % 2, :], xD[:, p % 2, :], yo[:, p % 2, :], ALU.add).then_inc(xo_done, 1)
                if p + 1 < NT:
                    x_dt(p + 1)
                    x_D(p + 1)
                if p >= 3:
                    pool.wait_ge(xn2_done, p - 2)
                    add_beta(x_sb[2], slice(ORDER[p - 3], ORDER[p - 3] + 1))
                if p + 3 < NT:
                    seg_moving(p + 3)
                if p >= 1:
                    ln_rstd(IN2[p - 1])
                    if p - 1 in LAST2:
                        ln_rstd(LAST2[p - 1])
                pool.wait_ge(se_done, p + 1)
                inv_root(sr[:, ORDER[p]:ORDER[p] + 1], se[:, ORDER[p]:ORDER[p] + 1], 1).then_inc(sr_done, 1)

            def last_beta(p):
                pool.wait_ge(xn2_done, p + 1)
                add_beta(x_sb[2], slice(ORDER[p], ORDER[p] + 1))

            def add_xn2(g):
                for p in (2 * g, 2 * g + 1):
                    i = ORDER[p]
                    pool.wait_ge(ob_done, NT + p + 1)
                    pool.tensor_tensor(o[:, i, :], o[:, i, :], xn[:, i, :], ALU.add).then_inc(o_done, 1)

            last_beta(NT - 3)
            add_xn2(0)
            add_xn2(1)
            ln_rstd(IN2[NT - 1])
            last_beta(NT - 2)
            ln_rstd(OUT2)
            add_xn2(2)
            ln_rstd(OUT2 + 1)
            last_beta(NT - 1)
            add_xn2(3)
            ln_rstd(OUT2 + 2)
            ln_rstd(OUT2 + 3)

        @block.scalar
        def _(act):
            for name, n in ROWS[1::2]:
                at, _ = row_at[name]
                act.dma_start(rows[at:at + n, :], a[name].rearrange("(t p) -> t p", p=P)).then_inc(ld_rows, 16)
            def turn(r, g):
                n = PAIRS * r + g
                act.wait_ge(xnT_ps, n + 1)
                dst, done = (xnT1, xnT_done) if r == 0 else (xnT[:, 0, :, :], xnT_hi)
                act.activation(dst[:, :, 2 * P * g:2 * P * (g + 1)], bank[n % 2].rearrange("p (t n) -> p t n", t=KT),
                               ACT.Copy).then_inc(done, 1)

            def gate(i):
                act.wait_ge(gate_ps, i + 1)
                act.activation(sg[:, i, :], bank[(2, 3, 6, 7)[i % 4]][:, 0:D], ACT.Tanh, scale=0.5).then_inc(sg_done, 1)

            def gelu(n):
                act.wait_ge(hb_done, NB * (n + 1))
                if n >= 1:
                    act.wait_ge(d2_ps, n)
                act.activation(hg[:, :, :], hb[:, :, :], ACT.Gelu).then_inc(gelu_done, 1)
                act.activation(hp[:, :, 0, :], hb[:, :, :], ACT.Gelu).then_inc(h_hi, 1)

            for n in range(2):
                for q in (2 * n, 2 * n + 1):
                    act.wait_ge(ld_d[q], 16)
                    act.activation(part(q, 0), raw[q], ACT.Copy).then_inc(w_hi, 1)
                for q in (2 * n, 2 * n + 1):
                    act.wait_ge(w_left, q + 1)
                    act.activation(part(q, 1), raw[q], ACT.Copy).then_inc(w_mid, 1)
            for s in range(STEPS):
                gelu(s)
                if s < KT:
                    if s == 0:
                        act.wait_ge(ld_in, 16)
                    act.activation(w_in[:, 0, s, :], raw_in[:, s, :], ACT.Copy).then_inc(w_in_hi, 1)
                if s == 1:
                    act.wait_ge(consts_done, 3)
                    act.activation(after_r[:, :], after[:, :], ACT.Copy).then_inc(after_done, 1)
                    act.activation(ones_r[:, :], ones[0:2, :], ACT.Copy).then_inc(ones_r_done, 1)
                if s == 2:
                    turn(0, 0)
                    turn(0, 1)
            for i in range(NC):
                gate(i)
            turn(0, 2)
            turn(0, 3)
            for i in range(NC, NT):
                gate(i)

            def normalise_pair(g):
                at = bn_before[MAMBA[g]]
                act.wait_ge(o_done, g + 1)
                for n, i in enumerate(PAIR[g]):
                    act.wait_ge(nb_done, g + 1)
                    act.activation(xn[:, i, :], x_sb[1][:, i, :], ACT.Identity, bias=nb[:, i:i + 1], scale=rstd[:, at + n:at + n + 1])\
                       .then_inc(xn_mamba, 1)

            act.wait_ge(ld_conv, 16)
            act.wait_ge(cols_ready, 1)

            def tap0(n):
                b, ct = divmod(n, CT)
                act.wait_ge(proj_ps, n + 1)
                if n >= 3:
                    act.wait_ge(xc_done, n - 2)
                act.activation(cv[:, n % 3, :], bank[(2, 3, 4)[n % 3]], ACT.Identity,
                               bias=col("conv_b")[:, ct:ct + 1], scale=conv_w[:, ct, CW - 1:CW]).then_inc(tap0_done, 1)

            def softplus():
                act.wait_ge(ld_head, all_of(3))
                act.activation(ea[:, :], head_par[:, 1, :], ACT.Exp).then_inc(ea_done, 1)
                act.wait_ge(dt_n, 1)
                act.activation(dte[:, :, :], dtn[:, :, :], ACT.Exp).then_inc(dt_e, 1)
                tap0(6)
                act.wait_ge(dt_e, 1)
                act.activation(dtl[:, :, :], dte[:, :, :], ACT.Ln, bias=ones[:, 0:1]).then_inc(dt_l, 1)

            def silu(n):
                b, ct = divmod(n, CT)
                act.wait_ge(conv_done, (CW - 1) * (n + 1))
                act.activation(xc[:, ct, b * L:(b + 1) * L], cv[:, n % 3, :], ACT.Silu).then_inc(xc_done, 1)

            def decays():
                act.wait_ge(rest_done, 2)
                act.activation(ecs[:, :, :], cs[:, :, :], ACT.Exp).then_inc(exps_done, 1)
                act.activation(erest[:, :, :], rest[:, :, :], ACT.Exp).then_inc(exps_done, 1)
                act.activation(dec[:, :, :].rearrange("p t h -> p (t h)"), tot[:, :, :].rearrange("p t h -> p (t h)"), ACT.Exp).then_inc(exps_done, 1)

            def silu_z(n):
                act.wait_ge(z_ps, n + 1)
                act.activation(sz[:, Z_ORDER[n], :], bank[z_bank(n)], ACT.Silu).then_inc(sz_done, 1)

            def evac_x(i):
                act.wait_ge(xt_ps, i + 1)
                act.activation(xt[:, i, :], bank[i % 2], ACT.Copy).then_inc(xt_done, 1)

            normalise_pair(0)
            normalise_pair(1)
            turn(1, 0)
            turn(1, 1)
            normalise_pair(2)
            normalise_pair(3)
            def exp_seg(p):
                act.wait_ge(seg_ready, p + 1)
                if p >= 2:
                    act.wait_ge(y_ps, p - 1)
                act.activation(E[:, p % 2, :, :].rearrange("p h l -> p (h l)"), seg_ps[:, :], ACT.Exp).then_inc(E_done, 1)

            def seg_moving_lo(p):
                act.wait_ge(seg_ready, p - 1)
                for h in range(NH):
                    last = act.activation(R_lo[:, p % 2, h, :], tri[:, :], ACT.Identity,
                                          scale=dA_parts[:, 1, ORDER[p], h:h + 1].bitcast(F32))
                last.then_inc(R_lo_done, 1)

            tap0(0)
            turn(1, 2)
            tap0(1)
            turn(1, 3)
            for n in range(1, NB * CT):
                silu(n - 1)
                if n + 1 < NB * CT and n not in (5, 8):
                    tap0(n + 1)
                if n == 4:
                    softplus()
                if n == 7:
                    decays()
                    tap0(9)
                if n in Z_WITH:
                    silu_z(Z_WITH[n])
                if n in TURN_WITH:
                    evac_x(TURN_WITH[n])
            for i in range(NC, NT):
                evac_x(i)
                if i == NC + 1:
                    silu(NB * CT - 1)
            exp_seg(0)
            seg_moving_lo(2)

            def evac_u(p):
                act.wait_ge(uT_ps, p + 1)
                if p >= 2:
                    act.wait_ge(out_ps, p - 1)
                act.activation(uT[:, p % 2, :, :].rearrange("p t n -> p (t n)"), bank[0], ACT.Copy).then_inc(uT_done, 1)

            def evac_xnT2(p):
                i = ORDER[p]
                act.wait_ge(xnT2_ps, p + 1)
                if p >= 2:
                    act.wait_ge(gate2_ps, p - 1)
                act.activation(xnT2[:, p % 2, :, :], bank[0][:, 0:D].rearrange("p (t n) -> p t n", t=KT), ACT.Copy)\
                   .then_inc(xnT2_done, 1)

            def gate2(p):
                act.wait_ge(gate2_ps, p + 1)
                act.activation(sg[:, ORDER[p], :], bank[1][:, 0:D], ACT.Tanh, scale=0.5).then_inc(sg2_done, 1)

            for p in range(NT):
                i = ORDER[p]
                if p + 1 < NT:
                    exp_seg(p + 1)
                if p >= 1:
                    evac_u(p - 1)
                if p in STEP_AT:
                    gelu(STEPS + STEP_AT[p])
                if p >= 2:
                    evac_xnT2(p - 2)
                if p + 3 < NT:
                    seg_moving_lo(p + 3)
                act.wait_ge(u_done, p + 1)
                if p >= 1:
                    act.wait_ge(ss_done, p)
                act.activation(usq, yd[:, p % 2, :], ACT.Square, accum_out=ss[:, i:i + 1]).then_inc(ss_done, 1)
                if p >= 2:
                    gate2(p - 2)
            evac_u(NT - 1)
            for p in range(NT - 2, NT):
                evac_xnT2(p)
                gate2(p)

        @block.tensor
        def _(pe):
            pe.wait_ge(consts_done, 3)
            pe.wait_ge(ld_rows, all_of(len(ROWS)))
            pe.transpose(bank[5][:, 0:n_rows], rows[:, :], ident[0:n_rows, 0:n_rows]).then_inc(rows_T, 1)

            def turn(r, g):
                n = PAIRS * r + g
                if n >= PAIRS + 2:
                    pe.wait_ge(xnT_lo, n - PAIRS - 1)
                elif n >= 2:
                    pe.wait_ge(xnT_done, n - 1)
                if r == 1:
                    pe.wait_ge(xn_mamba, 2 * g + 2)
                else:
                    pe.wait_ge(xn_last, NB)
                    pe.wait_ge(xn_others, len(OTHERS))
                for i in PAIR[g]:
                    for t in range(KT):
                        last = pe.transpose(bank[n % 2][:, t * 2 * P + (i % 2) * P:t * 2 * P + (i % 2 + 1) * P],
                                            xn[:, i, t * P:(t + 1) * P], ident[:, :])
                last.then_inc(xnT_ps, 1)

            def gate(i):
                if i == 0:
                    pe.wait_ge(ld_gate, all_of(2))
                if i >= 4:
                    pe.wait_ge(sg_done, i - 3)
                pe.wait_ge(xnT_done, i // 2 + 1)
                dst = bank[(2, 3, 6, 7)[i % 4]][:, 0:D]
                for t in range(KT):
                    pe.matmul(dst, xnT1[:, t, i * P:(i + 1) * P], w_gate[:, t, :], start=(t == 0), stop=False)
                if i == 0:
                    pe.wait_ge(ones_r_done, 1)
                    pe.wait_ge(gate_b_done, 2)
                pe.matmul(dst, ones_r[:, :], gate_b_parts[:, :], start=False, stop=True).then_inc(gate_ps, 1)

            def thought_in(f):
                pe.wait_ge(xnn_done, NB * (f + 1))
                pe.wait_ge(cols_ready, 1)
                for b in range(NB):
                    for t in range(KT):
                        last = pe.matmul(bank[5][:, t * NB + b:t * NB + b + 1], xnn[:, b, t * P:(t + 1) * P], ident[:, P - 1:P],
                                         start=True, stop=True)
                last.then_inc(last_ps, 1)

            def thought_agg(f):
                pe.wait_ge(ld_agg, 16)
                pe.wait_ge(last_done, f + 1)
                for m in range(KT):
                    for t in range(KT):
                        last = pe.matmul(bank[5][:, 4 + m * NB:4 + (m + 1) * NB], w_agg[:, t, m * P:(m + 1) * P], lastg[:, t, :],
                                         start=(t == 0), stop=(t == KT - 1))
                last.then_inc(agg_ps, 1)

            def variance(f):
                pe.wait_ge(sq_done, STEPS * f + 1)
                for t in range(KT):
                    last = pe.matmul(bank[5][:, 8:8 + NB], avg[:, :], sq[:, t, :], start=(t == 0), stop=(t == KT - 1))
                last.then_inc(var_ps, 1)

            def up(f, s):
                n, at = STEPS * f + s, (STEPS + 1) * f + s
                if s == 0:
                    pe.wait_ge(th_done, at + 1)
                    for t in range(KT):
                        last = pe.matmul(bank[5][:, 8:8 + NB], avg[:, :], th[:, at, t, :], start=(t == 0), stop=(t == KT - 1))
                else:
                    pe.wait_ge(sq_done, n + 1)
                    for t in range(KT):
                        last = pe.matmul(bank[5][:, 8:8 + 2 * NB], avg[:, :], dcsq[:, t, :, :].rearrange("p c b -> p (c b)"),
                                         start=(t == 0), stop=(t == KT - 1))
                last.then_inc(mean_ps, 1)
                pe.wait_ge(t_lo, n + 1)
                if n == 0:
                    pe.wait_ge(w_lo, 2)
                    pe.wait_ge(gb_parts, 5)
                width = 3 * TC if n == 0 else 3 * NB
                for m in range(HT):
                    if n == 0 and m == HT // 2:
                        variance(0)
                    for c in range(3):
                        for t in range(KT):
                            moving = tp[:, t, :, 0:(TC if n == 0 else NB)]
                            last = pe.matmul(bank[4][:, m * 3 * TC:m * 3 * TC + width], w_d1[:, c, t, m * P:(m + 1) * P], moving,
                                             start=(c == 0 and t == 0), stop=(c == 2 and t == KT - 1))
                last.then_inc(h_ps, 1)

            def down(f, s):
                n = STEPS * f + s
                pe.wait_ge(h_lo, n + 1)
                if n == 0:
                    pe.wait_ge(w_lo, 4)
                for m in range(KT):
                    for c in range(3):
                        for t in range(HT):
                            last = pe.matmul(bank[5][:, 16 + m * 3 * NB:16 + (m + 1) * 3 * NB], w_d2[:, c, t, m * P:(m + 1) * P],
                                             hp[:, t, :, :].rearrange("p c b -> p (c b)"),
                                             start=(c == 0 and t == 0), stop=(c == 2 and t == HT - 1))
                last.then_inc(d2_ps, 1)

            def spread_bias(f):
                pe.wait_ge(ld_bc, all_of(NB + 1))
                pe.matmul(bank[4], half_row[:, :], row_bc_b[:, :, :].rearrange("o b n -> o (b n)"), start=True, stop=False)

            def spread(f):
                pe.wait_ge(rep_done, f + 1)
                for b in range(NB):
                    for t in range(KT):
                        last = pe.matmul(bank[4][:, b * D:(b + 1) * D], th_rep[:, t, b, :], w_bc[:, t, :], start=False,
                                         stop=(b == NB - 1 and t == KT - 1))
                last.then_inc(bc_ps, 1)

            thought_in(0)
            thought_agg(0)
            for s in range(STEPS):
                up(0, s)
                if s == 2:
                    turn(0, 0)
                    turn(0, 1)
                if s == 3:
                    gate(1)
                down(0, s)
                if s == 2:
                    gate(0)
            spread_bias(0)
            spread(0)
            gate(2)
            gate(3)
            turn(0, 2)
            turn(0, 3)
            for i in range(4, NT):
                gate(i)
            turn(1, 0)
            turn(1, 1)

            def dt_products(tiles):
                base = DI + CD
                for i in tiles:
                    pe.wait_ge(xnT_lo, i // 2 + 1)
                    tok = slice(i * P, (i + 1) * P)
                    dst = bank[5][:, i * 2 * NH:(i + 1) * 2 * NH]
                    for t in range(KT):
                        pe.matmul(dst, xnT[:, 0, t, tok], w_in[:, :, t, base:base + NH], start=(t == 0), stop=False)
                        last = pe.matmul(dst[:, 0:NH], xnT[:, 1, t, tok], w_in[:, 0, t, base:base + NH], start=False, stop=(t == KT - 1))
                    last.then_inc(dt_ps, 1)

            PARTS = ((0, 0), (0, 1), (1, 0))

            def project(n):
                b, ct = divmod(n, CT)
                if n < 3:
                    pe.wait_ge(sg_done, NT)
                    pe.wait_ge(ob_done, NT)
                else:
                    pe.wait_ge(conv_done, (CW - 1) * (n - 2))
                pe.wait_ge(w_in_lo, KT)
                pe.wait_ge(xnT_lo, (b + 1) * NC // 2)
                for t in range(KT):
                    for w, x in PARTS:
                        last = pe.matmul(bank[(2, 3, 4)[n % 3]], w_in[:, w, t, DI + ct * P:DI + (ct + 1) * P], xnT[:, x, t, b * L:(b + 1) * L],
                                         start=(t == 0 and w + x == 0), stop=(t == KT - 1 and w == 1))
                last.then_inc(proj_ps, 1)

            def gate_z(n):
                if n >= 2:
                    pe.wait_ge(sz_done, n - 1)
                i = Z_ORDER[n]
                pe.wait_ge(xnT_lo, i // 2 + 1)
                for t in range(KT):
                    for x, w in PARTS:
                        last = pe.matmul(bank[z_bank(n)], xnT[:, x, t, i * P:(i + 1) * P], w_in[:, w, t, 0:DI],
                                         start=(t == 0 and w + x == 0), stop=(t == KT - 1 and x == 1))
                last.then_inc(z_ps, 1)

            def sums():
                pe.wait_ge(dA_done, 1)
                moving = dA[:, :, :].rearrange("p t h -> p (t h)")
                pe.matmul(bank[5][:, 0:N64], tri[:, :], moving, start=True, stop=True)
                pe.matmul(bank[5][:, N64:2 * N64], ones[:, :], moving, start=True, stop=True).then_inc(cs_ps, 1)

            def turn_x(i):
                pe.wait_ge(xc_done, CT * (i // NC + 1) - 1)
                if i >= 2:
                    pe.wait_ge(xt_done, i - 1)
                for t in range(XT):
                    last = pe.transpose(bank[i % 2][:, t * P:(t + 1) * P], xc[:, t, i * P:(i + 1) * P], ident[:, :])
                last.then_inc(xt_ps, 1)
                if i in STATES:
                    n = STATES.index(i)
                    if n == 0:
                        pe.wait_ge(rest_done, 2)
                    else:
                        pe.wait_ge(Bt_done, n)
                    pe.transpose(bank[5][:, 0:P], xc[:, XT, i * P:(i + 1) * P], ident[:, :]).then_inc(Bt_ps, 1)

            def new_state(n):
                pe.wait_ge(xw_done, n + 1)
                pe.wait_ge(Bt_done, n + 1)
                if n >= 2:
                    pe.wait_ge(S_done, n - 1)
                else:
                    pe.wait_ge(sz_done, NT - 1 + n)
                pe.matmul(bank[6 + n % 2], Bt[:, n % 2, :], xw[:, n % 2, :], start=True, stop=True).then_inc(st_ps, 1)

            def segments(p):
                pe.wait_ge(R_done, p + 1)
                if p >= 1:
                    pe.wait_ge(E_done, p)
                else:
                    pe.wait_ge(conv_done, (CW - 1) * (NB * CT - 1))
                if p < 2:
                    pe.wait_ge(R_lo_first, p + 1)
                else:
                    pe.wait_ge(R_lo_done, p - 1)
                pe.wait_ge(after_done, 1)
                for j in range(2):
                    for part_of_dA, moving in enumerate((R[:, p % 2, :, :], R_lo[:, p % 2, :, :])):
                        last = pe.matmul(bank[2 + j], after_r[:, :], moving.rearrange("p h l -> p (h l)")[:, j * 512:(j + 1) * 512],
                                         start=(part_of_dA == 0), stop=(part_of_dA == 1))
                last.then_inc(seg_ready, 1)

            for n in range(NB * CT):
                project(n)
                if n < 2:
                    turn(1, 2 + n)
                if n in DT_WITH:
                    dt_products(DT_WITH[n])
                if n == CT + 1:
                    sums()
                if n in Z_WITH:
                    gate_z(Z_WITH[n])
                if n == NB * CT - 1:
                    new_state(0)
                if n in TURN_WITH:
                    turn_x(TURN_WITH[n])
            new_state(1)
            turn_x(NC)
            new_state(2)
            for i in range(NC + 1, NT):
                turn_x(i)
                if i == NT - 1:
                    segments(0)
                new_state(STATES.index(i - 1))

            def b_by_c(p):
                tok = slice(ORDER[p] * P, (ORDER[p] + 1) * P)
                if p == 0:
                    pe.wait_ge(xt_done, NT)
                elif p >= 4:
                    pe.wait_ge(sg2_done, p - 3)
                else:
                    pe.wait_ge(GT_done, p)
                pe.matmul(bank[1][:, 0:P], xc[:, XT, tok], xc[:, XT + 1, tok], start=True, stop=True).then_inc(G_ps, 1)

            def from_state(p):
                i = ORDER[p]
                if i % NC > 0:
                    pe.wait_ge(S_done, STATES.index(i - 1) + 1)
                    if offs(p) >= 1:
                        pe.wait_ge(yo_done, offs(p))
                    else:
                        pe.wait_ge(S_done, len(STATES))
                    if p >= 2:
                        pe.wait_ge(x2_done, p - 1)
                    pe.matmul(bank[7], xc[:, XT + 1, i * P:(i + 1) * P], state(i - 1), start=True, stop=True).then_inc(yoff_ps, 1)

            def within_chunk(p):
                pe.wait_ge(M_done, p + 1)
                pe.wait_ge(xdt_done, p + 1)
                if p >= 1:
                    pe.wait_ge(yd_done, p)
                else:
                    pe.wait_ge(S_done, len(STATES))
                for h in range(NH):
                    last = pe.matmul(bank[6][:, h * HD:(h + 1) * HD], M[:, p % 2, h, :], xdt[:, p % 2, h * HD:(h + 1) * HD],
                                     start=True, stop=True)
                last.then_inc(y_ps, 1)

            def turn_u(p):
                pe.wait_ge(u_done, p + 1)
                if p >= 2:
                    pe.wait_ge(xnT2_done, p - 1)
                elif p == 1:
                    pe.wait_ge(uT_done, 1)
                for t in range(XT):
                    last = pe.transpose(bank[0][:, t * P:(t + 1) * P], yd[:, p % 2, t * P:(t + 1) * P], ident[:, :])
                last.then_inc(uT_ps, 1)

            def project_out(p):
                pe.wait_ge(uT_done, p + 1)
                pe.wait_ge(out_scaled, XT)
                pe.wait_ge(yo_done, offs(min(p + 2, NT)))
                if p >= 1:
                    pe.wait_ge(x2_done, p)
                for t in range(XT):
                    last = pe.matmul(bank[7][:, 0:D], uT[:, p % 2, t, :], w_out[:, t, :],
                                     start=(t == 0), stop=(t == XT - 1))
                last.then_inc(out_ps, 1)

            def turn_xn2(p):
                i = ORDER[p]
                pe.wait_ge(xn2_done, p + 1)
                pe.wait_ge(uT_done, min(p + 2, NT))
                for t in range(KT):
                    last = pe.transpose(bank[0][:, t * P:(t + 1) * P], xn[:, i, t * P:(t + 1) * P], ident[:, :])
                last.then_inc(xnT2_ps, 1)

            def gate2(p):
                pe.wait_ge(xnT2_done, p + 1)
                if p + 3 < NT:
                    pe.wait_ge(GT_done, p + 4)
                else:
                    pe.wait_ge(sg2_done, p)
                for t in range(KT):
                    pe.matmul(bank[1][:, 0:D], xnT2[:, p % 2, t, :], w_gate[:, t, :], start=(t == 0), stop=False)
                pe.matmul(bank[1][:, 0:D], ones_r[:, :], gate_b_parts[:, :], start=False, stop=True).then_inc(gate2_ps, 1)

            b_by_c(0)
            for p in range(NT):
                if p + 1 < NT:
                    segments(p + 1)
                    b_by_c(p + 1)
                if p in STEP_AT:
                    up(1, STEP_AT[p])
                from_state(p)
                if p >= 1:
                    turn_u(p - 1)
                if STEP_AT.get(p) == 0:
                    variance(1)
                within_chunk(p)
                if p == THOUGHT_AT:
                    thought_in(1)
                if p >= 2:
                    turn_xn2(p - 2)
                if p >= 1:
                    project_out(p - 1)
                if p in STEP_AT:
                    down(1, STEP_AT[p])
                if p >= 2:
                    gate2(p - 2)
                if p == THOUGHT_AT:
                    thought_agg(1)
            spread_bias(1)
            turn_u(NT - 1)
            spread(1)
            project_out(NT - 1)
            turn_xn2(NT - 2)
            gate2(NT - 2)
            turn_xn2(NT - 1)
            gate2(NT - 1)

        @block.vector
        def _(dve):
            def ln_stats(k, src, wait):
                tiles = LN_TILES[k]
                at = bn_before[k]
                for n, i in enumerate(tiles):
                    wait(i)
                    dve.bn_stats(bn[:, at + n, :], src(n, i)).then_inc(bn_done, 1)
                for n, i in enumerate(tiles):
                    dve.wait_ge(bn_done, at + n + 1)
                    dve.bn_aggr(mv[:, at + n, :], bn[:, at + n, :]).then_inc(ag_done, 1)
                dve.wait_ge(ag_done, bn_before[k + 1])
                dve.tensor_scalar(ve[:, at:bn_before[k + 1]], mv[:, at:bn_before[k + 1], 1], LN_EPS[k], None, ALU.add).then_inc(ve_done, 1)

            def normalise(k, n, src, dst):
                at = bn_before[k] + n
                return dve.tensor_scalar(dst, src, mv[:, at, 0:1], rstd[:, at:at + 1], ALU.subtract, ALU.mult)

            def normalise_group(k, x, done):
                dve.wait_ge(rstd_done, k + 1)
                for n, i in enumerate(LN_TILES[k]):
                    normalise(k, n, x[:, i, :], xn[:, i, :]).then_inc(done, 1)

            wide = lambda v: v.unsqueeze(2).to_broadcast([P, v.shape[1], NB])

            def without_high(q):
                dve.wait_ge(w_hi, q + 1)
                dve.tensor_tensor(raw[q], raw[q], part(q, 0), ALU.subtract).then_inc(w_left, 1)

            def low(q):
                dve.wait_ge(w_mid, q + 1)
                dve.tensor_tensor(part(q, 2), raw[q], part(q, 1), ALU.subtract).then_inc(w_lo, 1)

            def columns():
                dve.wait_ge(rows_T, 1)
                dve.tensor_copy(cols[:, :], bank[5][:, 0:n_rows]).then_inc(cols_ready, 1)
                dve.wait_ge(cols_ready, 1)
                at, _ = row_at["pn_gamma"]
                both = cols[:, at:at + 2 * KT].rearrange("p (c t) -> p t c", c=2)
                dve.tensor_copy(tp[:, :, 0, NB:TC], both).then_inc(gb_parts, 1)
                dve.wait_ge(gb_parts, 1)
                dve.tensor_tensor(gb_rest[:, :, :], both, tp[:, :, 0, NB:TC], ALU.subtract).then_inc(gb_parts, 1)
                dve.wait_ge(gb_parts, 2)
                dve.tensor_copy(tp[:, :, 1, NB:TC], gb_rest[:, :, :]).then_inc(gb_parts, 1)
                dve.wait_ge(gb_parts, 3)
                dve.tensor_tensor(tp[:, :, 2, NB:TC], gb_rest[:, :, :], tp[:, :, 1, NB:TC], ALU.subtract).then_inc(gb_parts, 2)

            def thought_start(f):
                dve.wait_ge(last_ps, f + 1)
                dve.tensor_tensor(lastT[:, :, :], bank[5][:, 0:KT * NB].rearrange("p (t b) -> p t b", t=KT), wide(col("in_gamma")),
                                  ALU.mult).then_inc(last_mid, 1)
                dve.wait_ge(last_mid, f + 1)
                dve.tensor_tensor(lastg[:, :, :], lastT[:, :, :], wide(col("in_beta")), ALU.add).then_inc(last_done, 1)

            def thought_first(f):
                dve.wait_ge(agg_ps, f + 1)
                at = (STEPS + 1) * f
                dve.tensor_tensor(th[:, at, :, :], bank[5][:, 4:4 + KT * NB].rearrange("p (t b) -> p t b", t=KT), wide(col("agg_b")),
                                  ALU.add).then_inc(th_done, 1)


            def step_parts(f, s):
                n, at = STEPS * f + s, (STEPS + 1) * f + s
                now = th[:, at, :, :]
                dve.wait_ge(th_done, at + 1)
                if s > 0:
                    dve.wait_ge(mu_done, n)
                    dve.tensor_tensor(dc, now, mu[:, (n - 1) % 2, :].unsqueeze(1).to_broadcast([P, KT, NB]), ALU.subtract).then_inc(dc_done, 1)
                if n >= 1:
                    dve.wait_ge(h_ps, n)
                dve.tensor_tensor(tg[:, :, :], now, wide(col("pn_gamma")), ALU.mult).then_inc(tg_done, 1)
                dve.tensor_tensor(tp[:, :, 0, 0:NB], now, wide(col("pn_gamma")), ALU.mult).then_inc(t_hi, 1)
                if s > 0:
                    dve.wait_ge(dc_done, n + 1)
                    dve.tensor_tensor(sq, dc, dc, ALU.mult).then_inc(sq_done, 1)
                dve.wait_ge(tg_done, n + 1)
                dve.wait_ge(t_hi, n + 1)
                dve.tensor_tensor(tr[:, :, :], tg[:, :, :], tp[:, :, 0, 0:NB], ALU.subtract).then_inc(t_left, 1)
                dve.wait_ge(t_left, n + 1)
                dve.tensor_copy(tp[:, :, 1, 0:NB], tr[:, :, :]).then_inc(t_mid, 1)
                dve.wait_ge(t_mid, n + 1)
                dve.tensor_tensor(tp[:, :, 2, 0:NB], tr[:, :, :], tp[:, :, 1, 0:NB], ALU.subtract).then_inc(t_lo, 1)

            def step_mean(f, s):
                n, at = STEPS * f + s, (STEPS + 1) * f + s
                now = th[:, at, :, :]
                dve.wait_ge(mean_ps, n + 1)
                if s == 0:
                    dve.tensor_copy(mu[:, n % 2, :], bank[5][:, 8:8 + NB]).then_inc(mu_done, 1)
                    dve.wait_ge(mu_done, n + 1)
                    dve.tensor_tensor(dc, now, mu[:, n % 2, :].unsqueeze(1).to_broadcast([P, KT, NB]), ALU.subtract).then_inc(dc_done, 1)
                    dve.wait_ge(dc_done, n + 1)
                    dve.tensor_tensor(sq, dc, dc, ALU.mult).then_inc(sq_done, 1)
                else:
                    shifted, squares = bank[5][:, 8:8 + NB], bank[5][:, 8 + NB:8 + 2 * NB]
                    dve.tensor_copy(dmean[:, :], shifted).then_inc(dmean_done, 1)
                    dve.wait_ge(dmean_done, f * (STEPS - 1) + s)
                    dve.tensor_tensor(m2[:, :], dmean[:, :], dmean[:, :], ALU.mult).then_inc(m2_done, 1)
                    dve.tensor_tensor(mu[:, n % 2, :], dmean[:, :], mu[:, (n - 1) % 2, :], ALU.add).then_inc(mu_done, 1)
                    dve.wait_ge(m2_done, f * (STEPS - 1) + s)
                    dve.scalar_tensor_tensor(out=vs[:, :], in0=squares, scalar=EPS_FFN, in1=m2[:, :], op0=ALU.add,
                                             op1=ALU.subtract).then_inc(vs_done, 1)
                    dve.wait_ge(mu_done, n + 1)
                dve.tensor_tensor(thb[:, n, :, :], now, wide(col("d2_b")), ALU.add).then_inc(thb_done, 1)
                by_mean = mu[:, n % 2, :].unsqueeze(1).to_broadcast([P, HT, NB])
                if n > 0:
                    dve.tensor_tensor(mgW[:, :, :], wide(gW[:, :]), by_mean, ALU.mult).then_inc(mgW_done, 1)

            def step_variance(f, s):
                if s == 0:
                    dve.wait_ge(var_ps, f + 1)
                    dve.tensor_scalar(vs[:, :], bank[5][:, 8:8 + NB], EPS_FFN, None, ALU.add).then_inc(vs_done, 1)

            def step_hidden(n):
                by_mean = mu[:, n % 2, :].unsqueeze(1).to_broadcast([P, HT, NB])
                dve.wait_ge(h_ps, n + 1)
                hidden = bank[4][:, 0:HT * 3 * TC].rearrange("p (m r) -> p m r", m=HT)
                if n == 0:
                    both = hidden[:, :, :].rearrange("p m (c j) -> p m j c", c=3)
                    dve.tensor_reduce(gW[:, :], both[:, :, NB, :], AX.X, ALU.add).then_inc(gW_done, 1)
                    dve.tensor_reduce(c1[:, :], both[:, :, NB + 1, :], AX.X, ALU.add).then_inc(c1_done, 1)
                    dve.wait_ge(gW_done, 1)
                    dve.tensor_tensor(mgW[:, :, :], wide(gW[:, :]), by_mean, ALU.mult).then_inc(mgW_done, 1)
                    dve.wait_ge(c1_done, 1)
                    dve.tensor_tensor(c1[:, :], c1[:, :], col("d1_b"), ALU.add).then_inc(c1_done, 1)
                    here = both[:, :, 0:NB, :]
                else:
                    here = hidden[:, :, 0:3 * NB].rearrange("p m (c j) -> p m j c", c=3)
                dve.tensor_reduce(hs[:, :, :], here, AX.X, ALU.add).then_inc(hs_done, 1)
                dve.wait_ge(hs_done, n + 1)
                dve.wait_ge(mgW_done, n + 1)
                dve.tensor_tensor(hc[:, :, :], hs[:, :, :], mgW[:, :, :], ALU.subtract).then_inc(hc_done, 1)
                dve.wait_ge(hc_done, n + 1)
                dve.wait_ge(rs_done, n + 1)
                dve.wait_ge(c1_done, 2)
                for b in range(NB):
                    dve.scalar_tensor_tensor(out=hb[:, :, b], in0=hc[:, :, b], scalar=rs[:, b:b + 1], in1=c1[:, :], op0=ALU.mult,
                                             op1=ALU.add).then_inc(hb_done, 1)

            def step_gelu(n):
                dve.wait_ge(gelu_done, n + 1)
                dve.wait_ge(h_hi, n + 1)
                dve.tensor_tensor(hrest[:, :, :], hg[:, :, :], hp[:, :, 0, :], ALU.subtract).then_inc(h_left, 1)
                dve.wait_ge(h_left, n + 1)
                dve.tensor_copy(hp[:, :, 1, :], hrest[:, :, :]).then_inc(h_mid, 1)
                dve.wait_ge(h_mid, n + 1)
                dve.tensor_tensor(hp[:, :, 2, :], hrest[:, :, :], hp[:, :, 1, :], ALU.subtract).then_inc(h_lo, 1)

            def step_end(f, s):
                n, at = STEPS * f + s, (STEPS + 1) * f + s
                dve.wait_ge(d2_ps, n + 1)
                dve.tensor_reduce(dsum[:, :, :], bank[5][:, 16:16 + KT * 3 * NB].rearrange("p (t c b) -> p t b c", t=KT, c=3),
                                  AX.X, ALU.add).then_inc(dsum_done, 1)
                dve.wait_ge(dsum_done, n + 1)
                dve.wait_ge(thb_done, n + 1)
                dve.tensor_tensor(th[:, at + 1, :, :], dsum[:, :, :], thb[:, n, :, :], ALU.add).then_inc(th_done, 1)


            def repeat_thought(f):
                at = (STEPS + 1) * f + STEPS
                dve.wait_ge(th_done, at + 1)
                dve.tensor_scalar(th_rep[:, :, :, :], th[:, at, :, :].unsqueeze(3).to_broadcast([P, KT, NB, P]), 0.5, None,
                                  ALU.mult).then_inc(rep_done, 1)

            def gated(i):
                b = i // NC
                dve.scalar_tensor_tensor(out=o[:, i, :], in0=sg[:, i, :], scalar=1.0, in1=bank[4][:, b * D:(b + 1) * D],
                                         op0=ALU.add, op1=ALU.mult).then_inc(ob_done, 1)

            def out_centred(k):
                for n, i in enumerate(LN_TILES[k]):
                    dve.scalar_tensor_tensor(out=o[:, i, :], in0=o[:, i, :], scalar=mv[:, bn_before[k] + n, 0:1], in1=gam[:, :],
                                             op0=ALU.subtract, op1=ALU.mult).then_inc(og_done, 1)

            def out_added(f, before, k):
                dve.wait_ge(rstd_done, k + 1)
                for n, i in enumerate(LN_TILES[k]):
                    dve.wait_ge(og_done, NT * f + before + n + 1)
                    dve.wait_ge(xb_done, before // 2 + 1 if f == 0 else PAIRS + before + n + 1)
                    at = bn_before[k] + n
                    dve.scalar_tensor_tensor(out=x_sb[2 * f + 1][:, i, :], in0=o[:, i, :], scalar=rstd[:, at:at + 1],
                                             in1=x_sb[2 * f][:, i, :], op0=ALU.mult, op1=ALU.add).then_inc(x_done, 1)

            tiles_of = lambda t: lambda n, i: t[:, i, :]
            x = x_sb[0]
            ln_stats(0, tiles_of(x), lambda i: dve.wait_ge(ld_x, all_of(NB)))
            normalise_group(0, x, xn_last)
            ln_stats(1, tiles_of(xn), lambda i: dve.wait_ge(xn_last, LAST.index(i) + 1))
            dve.wait_ge(rstd_done, 2)
            for b in range(NB):
                normalise(1, b, xn[:, LAST[b], :], xnn[:, b, :]).then_inc(xnn_done, 1)
            without_high(0)
            without_high(1)
            columns()
            thought_start(0)
            low(0)
            low(1)
            thought_first(0)
            for s in range(STEPS):
                step_parts(0, s)
                step_mean(0, s)
                if s == 0:
                    without_high(2)
                step_variance(0, s)
                if s == 0:
                    without_high(3)
                if s == 1:
                    dve.wait_ge(ld_gate, all_of(2))
                    dve.wait_ge(consts_done, 3)
                    dve.tensor_scalar(gate_b_parts[:, :], rows_gate_b, -1.0, None, ALU.mult).then_inc(gate_b_done, 1)
                    dve.wait_ge(gate_b_done, 1)
                    dve.scalar_tensor_tensor(out=gate_b_parts[:, :], in0=gate_b_parts[:, :].bitcast(F32), scalar=after[0:2, 0:1],
                                             in1=rows_gate_b, op0=ALU.mult, op1=ALU.add).then_inc(gate_b_done, 1)
                    dve.wait_ge(ld_aff, all_of(2))
                    dve.tensor_scalar(bet[:, :], bet[:, :], 0.5, None, ALU.mult).then_inc(beta_ready, 1)
                    dve.tensor_scalar(gam[:, :], gam[:, :], 0.5, None, ALU.mult).then_inc(gamma_ready, 1)
                step_hidden(s)
                if s == 0:
                    low(2)
                step_gelu(s)
                if s == 0:
                    low(3)
                    ln_stats(2, tiles_of(x), lambda i: dve.wait_ge(ld_x2, all_of(NB)))
                if s == 1:
                    normalise_group(2, x, xn_others)
                step_end(0, s)
            repeat_thought(0)
            dve.wait_ge(bc_ps, 1)

            def gated_pair(g):
                for i in PAIR[g]:
                    dve.wait_ge(sg_done, i + 1)
                    gated(i)

            def out_stats(g):
                ln_stats(OUT1[g], tiles_of(o), lambda i: dve.wait_ge(o_done, g + 1))

            def out_pair(g):
                out_added(0, 2 * g, OUT1[g])
                ln_stats(MAMBA[g], tiles_of(x_sb[1]), lambda i: dve.wait_ge(x_done, i + 1))

            def mamba_bias(g):
                at = bn_before[MAMBA[g]]
                dve.wait_ge(rstd_done, MAMBA[g] + 1)
                dve.scalar_tensor_tensor(out=nb[:, 2 * g:2 * g + 2], in0=mv[:, at:at + 2, 0], scalar=-1.0, in1=rstd[:, at:at + 2],
                                         op0=ALU.mult, op1=ALU.mult).then_inc(nb_done, 1)

            dve.wait_ge(gamma_ready, 1)
            gated_pair(0)
            gated_pair(1)
            out_stats(0)
            gated_pair(2)
            out_centred(OUT1[0])
            out_stats(1)
            out_pair(0)
            gated_pair(3)
            out_centred(OUT1[1])
            out_stats(2)
            out_pair(1)
            mamba_bias(0)
            out_centred(OUT1[2])
            out_stats(3)
            out_pair(2)
            mamba_bias(1)
            out_centred(OUT1[3])
            out_pair(3)
            mamba_bias(2)
            mamba_bias(3)

            def second_part(g):
                cols_g = slice(2 * P * g, 2 * P * (g + 1))
                dve.wait_ge(xnT_hi, g + 1)
                dve.tensor_tensor(xnT[:, 1, :, cols_g], bank[g % 2].rearrange("p (t n) -> p t n", t=KT),
                                  xnT[:, 0, :, cols_g].bitcast(F32), ALU.subtract).then_inc(xnT_lo, 1)

            second_part(0)
            second_part(1)

            by_tile = lambda v: v.unsqueeze(1).to_broadcast([P, NT, NH])
            flat = lambda v: v[:, :, :].rearrange("p t h -> p (t h)")

            def dt_start():
                dve.wait_ge(ld_head, all_of(3))
                dve.wait_ge(dt_ps, NT)
                sums = bank[5][:, 0:2 * N64].rearrange("p (t c h) -> p t c h", t=NT, c=2)
                dve.tensor_tensor(dtv[:, :, :], sums[:, :, 0, :], by_tile(head_par[:, 0, :]), ALU.add).then_inc(dt_v, 1)
                dve.wait_ge(dt_v, 1)
                dve.tensor_tensor(dtv[:, :, :], dtv[:, :, :], sums[:, :, 1, :], ALU.add).then_inc(dt_v, 1)
                dve.wait_ge(dt_v, 2)
                dve.scalar_tensor_tensor(out=flat(dtn), in0=flat(dtv), scalar=-1.0, in1=flat(dtv), op0=ALU.mult, op1=ALU.min).then_inc(dt_n, 1)

            def dt_end():
                dve.wait_ge(dt_l, 1)
                dve.scalar_tensor_tensor(out=flat(dt), in0=flat(dtv), scalar=0.0, in1=flat(dtl), op0=ALU.max, op1=ALU.add).then_inc(dt_done, 1)
                dve.wait_ge(dt_done, 1)
                dve.wait_ge(ea_done, 1)
                dve.scalar_tensor_tensor(out=dA[:, :, :], in0=dt[:, :, :], scalar=-1.0, in1=by_tile(ea[:, :]), op0=ALU.mult,
                                         op1=ALU.mult).then_inc(dA_done, 1)
                dve.wait_ge(dA_done, 1)
                dve.tensor_copy(dA_parts[:, 0, :, :].rearrange("p t h -> p (t h)"), flat(dA)).then_inc(dA_hi, 1)
                dve.wait_ge(dA_hi, 1)
                dve.tensor_tensor(dA_parts[:, 1, :, :], dA[:, :, :], dA_parts[:, 0, :, :].bitcast(F32), ALU.subtract).then_inc(dA_lo, 1)

            heads = lambda v: v.rearrange("p (h q) -> p h q", h=NH)

            def convolve(n):
                b, ct = divmod(n, CT)
                dve.wait_ge(tap0_done, n + 1)
                for k in range(1, CW):
                    dst = cv[:, n % 3, k:L]
                    if k > 1:
                        dve.wait_ge(conv_done, (CW - 1) * n + k - 1)
                    dve.scalar_tensor_tensor(out=dst, in0=bank[(2, 3, 4)[n % 3]][:, 0:L - k], scalar=conv_w[:, ct, CW - 1 - k:CW - k],
                                             in1=dst, op0=ALU.mult, op1=ALU.add).then_inc(conv_done, 1)

            def sums():
                dve.wait_ge(cs_ps, 1)
                dve.tensor_copy(flat(cs), bank[5][:, 0:N64]).then_inc(cs_done, 1)
                dve.tensor_copy(flat(tot), bank[5][:, N64:2 * N64]).then_inc(rest_done, 1)
                dve.wait_ge(cs_done, 1)
                dve.wait_ge(rest_done, 1)
                dve.tensor_tensor(flat(rest), flat(tot), flat(cs), ALU.subtract).then_inc(rest_done, 1)

            def evac_B(n):
                dve.wait_ge(Bt_ps, n + 1)
                if n >= 2:
                    dve.wait_ge(st_ps, n - 1)
                dve.tensor_copy(Bt[:, n % 2, :], bank[5][:, 0:P]).then_inc(Bt_done, 1)

            def advance(n):
                i = STATES[n]
                if i % NC > 0:
                    dve.wait_ge(S_done, n)
                    dve.tensor_tensor(heads(Sd[:, n % 2, :]), heads(state(i - 1)), dec[:, i, :].unsqueeze(2).to_broadcast([P, NH, HD]),
                                      ALU.mult).then_inc(Sd_done, 1)
                dve.wait_ge(st_ps, n + 1)
                if i % NC == 0:
                    dve.tensor_copy(state(i), bank[6 + n % 2]).then_inc(S_done, 1)
                else:
                    dve.wait_ge(Sd_done, n - i // NC)
                    dve.tensor_tensor(state(i), Sd[:, n % 2, :], bank[6 + n % 2], ALU.add).then_inc(S_done, 1)

            for n in range(NB * CT):
                convolve(n)
                if n < 2:
                    second_part(2 + n)
                if n == 4:
                    dt_start()
                if n == 6:
                    dt_end()
                if n == CT + 1:
                    sums()
                if n == CT + 2:
                    dve.wait_ge(exps_done, 2)
                    dve.tensor_tensor(flat(wd), flat(erest), flat(dt), ALU.mult).then_inc(wd_done, 1)
                    evac_B(0)
                if n == CT + 3:
                    evac_B(1)
                if n == CT + 4:
                    advance(0)
                    evac_B(2)
                    advance(1)
            evac_B(3)
            for n in range(2, len(STATES)):
                advance(n)
                if n + 2 < len(STATES):
                    evac_B(n + 2)

            def masked(p):
                dve.wait_ge(G_ps, p + 1)
                if p >= 2:
                    dve.wait_ge(M_done, p - 1)
                if p == 0:
                    dve.wait_ge(after_done, 1)
                dve.tensor_tensor(GT[:, p % 2, :], bank[1][:, 0:P], tri[:, :], ALU.mult).then_inc(GT_done, 1)

            def weights(p):
                dve.wait_ge(E_done, p + 1)
                dve.wait_ge(GT_done, p + 1)
                dve.tensor_tensor(M[:, p % 2, :, :], E[:, p % 2, :, :], GT[:, p % 2, :].unsqueeze(1).to_broadcast([P, NH, P]), ALU.mult)\
                   .then_inc(M_done, 1)

            def residual(p):
                i = ORDER[p]
                dve.wait_ge(out_ps, p + 1)
                dve.wait_ge(sr_done, p + 1)
                dve.scalar_tensor_tensor(out=x_sb[2][:, i, :], in0=bank[7][:, 0:D], scalar=sr[:, i:i + 1],
                                         in1=x_sb[1][:, i, :], op0=ALU.mult, op1=ALU.add).then_inc(x2_done, 1)
                ln_stats(IN2[p], tiles_of(x_sb[2]), lambda i: dve.wait_ge(x2_done, p + 1))

            def next_xn(p):
                i = ORDER[p]
                normalise_group(IN2[p], x_sb[2], xn2_done)
                if p in LAST2:
                    ln_stats(LAST2[p], tiles_of(xn), lambda i: dve.wait_ge(xn2_done, p + 1))
                    dve.wait_ge(rstd_done, LAST2[p] + 1)
                    normalise(LAST2[p], 0, xn[:, i, :], xnn[:, p, :]).then_inc(xnn_done, 1)

            def gated_2(g):
                for p in (2 * g, 2 * g + 1):
                    dve.wait_ge(sg2_done, p + 1)
                    gated(ORDER[p])

            def out_stats_2(g):
                ln_stats(OUT2 + g, tiles_of(o), lambda i: dve.wait_ge(o_done, PAIRS + ORDER.index(i) + 1))

            masked(0)
            weights(0)
            for p in range(NT):
                i, j = ORDER[p], p % 2
                step = STEP_AT.get(p)
                if step is not None:
                    step_parts(1, step)
                if p + 1 < NT:
                    masked(p + 1)
                if step is not None:
                    step_mean(1, step)
                if p >= 2 and p - 1 != NB:
                    next_xn(p - 2)
                if i % NC > 0:
                    dve.wait_ge(yoff_ps, offs(p) + 1)
                    if offs(p) == 0:
                        dve.wait_ge(S_done, len(STATES))
                    elif offs(p) >= 2:
                        dve.wait_ge(xo_done, offs(p) - 1)
                    dve.tensor_tensor(heads(yo[:, j, :]), heads(bank[7]), ecs[:, i, :].unsqueeze(2).to_broadcast([P, NH, HD]), ALU.mult)\
                       .then_inc(yo_done, 1)
                if step is not None:
                    step_variance(1, step)
                if p + 1 < NT:
                    weights(p + 1)
                if step is not None:
                    step_hidden(STEPS + step)
                dve.wait_ge(y_ps, p + 1)
                if i % NC > 0:
                    dve.wait_ge(xo_done, offs(p) + 1)
                else:
                    dve.wait_ge(xD_done, p + 1)
                if p >= 2:
                    dve.wait_ge(uT_ps, p - 1)
                    dve.wait_ge(ss_done, p - 1)
                dve.tensor_tensor(yd[:, j, :], bank[6], xD[:, j, :], ALU.add).then_inc(yd_done, 1)
                if step is not None:
                    step_gelu(STEPS + step)
                dve.wait_ge(yd_done, p + 1)
                dve.wait_ge(sz_done, Z_ORDER.index(i) + 1)
                dve.tensor_tensor(yd[:, j, :], yd[:, j, :], sz[:, i, :], ALU.mult).then_inc(u_done, 1)
                if p == THOUGHT_AT:
                    thought_start(1)
                if p >= 1:
                    residual(p - 1)
                if p == NB:
                    next_xn(p - 1)
                dve.wait_ge(ss_done, p + 1)
                dve.tensor_scalar(se[:, i:i + 1], ss[:, i:i + 1], 1.0 / DI, EPS_LN, ALU.mult, ALU.add).then_inc(se_done, 1)
                if p == THOUGHT_AT:
                    thought_first(1)
                if step is not None:
                    step_end(1, step)
            repeat_thought(1)
            next_xn(NT - 2)
            dve.wait_ge(bc_ps, 2)
            gated_2(0)
            gated_2(1)
            residual(NT - 1)
            next_xn(NT - 1)
            out_stats_2(0)
            gated_2(2)
            out_centred(OUT2)
            out_stats_2(1)
            out_added(1, 0, OUT2)
            gated_2(3)
            out_centred(OUT2 + 1)
            out_stats_2(2)
            out_added(1, 2, OUT2 + 1)
            out_centred(OUT2 + 2)
            out_stats_2(3)
            out_added(1, 4, OUT2 + 2)
            out_centred(OUT2 + 3)
            out_added(1, 6, OUT2 + 3)


_SHORT = {
    "u": "L0_attn_u", "in_proj": "L0_attn_in_proj_kernel", "conv_w": "L0_attn_conv1d_weight", "conv_b": "L0_attn_conv1d_bias",
    "dt_bias": "L0_attn_dt_bias", "A_log": "L0_attn_A_log", "D": "L0_attn_D", "norm_w": "L0_attn_norm_weight",
    "out_proj": "L0_attn_out_proj_kernel", "in_gamma": "L0_ffn_in_gamma", "in_beta": "L0_ffn_in_beta", "agg_w": "L0_ffn_agg_w",
    "agg_b": "L0_ffn_agg_b", "pn_gamma": "L0_ffn_pn_gamma", "pn_beta": "L0_ffn_pn_beta", "d1_w": "L0_ffn_d1_w",
    "d1_b": "L0_ffn_d1_b", "d2_w": "L0_ffn_d2_w", "d2_b": "L0_ffn_d2_b", "bc_w": "L0_ffn_bc_w", "bc_b": "L0_ffn_bc_b",
    "gate_w": "L0_ffn_gate_w", "gate_b": "L0_ffn_gate_b", "out_gamma": "L0_ffn_out_gamma", "out_beta": "L0_ffn_out_beta",
}


def kernel(**inputs):
    import numpy as _np
    import concourse.bacc as _bacc
    from concourse import mybir as _mybir
    from concourse.bass_utils import run_bass_kernel_spmd as _run

    nc = _bacc.Bacc("TRN2", target_bir_lowering=False, num_devices=1)
    arrays, args = {}, {}
    for short, name in _SHORT.items():
        v = _np.ascontiguousarray(inputs[name])
        arrays[f"in_{name}"] = v
        args[short] = nc.dram_tensor(f"in_{name}", v.shape, _mybir.dt.from_np(v.dtype), kind="ExternalInput").ap()
    shape = arrays["in_L0_attn_u"].shape
    result = nc.dram_tensor("result", shape, _mybir.dt.float32, kind="ExternalOutput").ap()
    macaron_program(nc, args, result)
    r = _run(nc, [arrays], core_ids=[0])
    return r.results[0]["result"]
```
